# Optimizing a Trainium2 kernel written in Bass

```python
import numpy as np
import jax
import jax.numpy as jnp

def _softmax(x, axis=-1):
    return jax.nn.softmax(x, axis=axis)

def _gelu(x):
    return jax.nn.gelu(x, approximate=True)

def _silu(x):
    return jax.nn.silu(x)

def _sigmoid(x):
    return jax.nn.sigmoid(x)

def _layernorm(x, axis=-1, eps=1e-05):
    m = jnp.mean(x, axis=axis, keepdims=True)
    v = jnp.var(x, axis=axis, keepdims=True)
    return (x - m) / jnp.sqrt(v + eps)

def _scatter_add(tgt, idx, src, axis=0):
    return tgt.at[idx].add(src)

def _segment_sum(src, seg, n):
    return jax.ops.segment_sum(src, seg, n)
kernel_name = 'mk_audio_tower_d1_tok_audfeat512_r4_826270'

def setup_inputs(seed: int=0):
    np.random.seed(seed)
    _w = jnp.asarray

    def _rec_inputs():
        import jax
        import jax.numpy as jnp
        _rk = jax.random.key(seed)
        x = -0.000124254 + 0.999853 * jax.random.normal(jax.random.fold_in(_rk, 1), (16, 750, 128), jnp.float32)
        return x
    x = _rec_inputs()

    def _L0_tok_setup():
        import jax, jax.numpy as jnp
        import numpy as np
        B, T, C = (16, 1000, 128)
        MS = 5
        RED = 2
        EXP = 1
        D = C * MS

        def _layernorm(h, g, b, eps=1e-05):
            m = jnp.mean(h, axis=-1, keepdims=True)
            v = jnp.var(h, axis=-1, keepdims=True)
            return (h - m) * jax.lax.rsqrt(v + eps) * g + b
        key = jax.random.key(seed)
        ks = jax.random.split(key, 5)

        def xav(k, shape):
            fan_in, fan_out = shape
            lim = np.sqrt(6.0 / (fan_in + fan_out)).astype(np.float32)
            return jax.random.uniform(k, shape, jnp.float32, -lim, lim)
        return {'x': jax.random.normal(ks[0], (B, T, C), jnp.float32), 'w1': xav(ks[1], (D, D * RED)), 'w2': xav(ks[2], (D * RED, D)), 'fc_w': xav(ks[3], (C, C * EXP)), 'fc_b': jnp.zeros((C * EXP,), jnp.float32), 'ln_g': jnp.ones((C * EXP,), jnp.float32), 'ln_b': jnp.zeros((C * EXP,), jnp.float32)}
    _L0_tok_all = _L0_tok_setup()
    _L0_tok_in = {k: v for k, v in _L0_tok_all.items() if k in ('w1', 'w2', 'fc_w', 'fc_b', 'ln_g', 'ln_b')}
    del _L0_tok_all

    def _L0_attn_setup():
        import jax, jax.numpy as jnp
        import numpy as np
        B, T, D = (8, 1024, 128)
        S = 128
        E = 2 * D
        CHUNK = 64
        MAXPOS = 128
        EPS = 1e-05

        def rope_gn(x):
            b, g, n, s = x.shape
            half = s // 2
            pos = jnp.arange(g * n, dtype=x.dtype).reshape(g, n)
            inv_freq = 10000.0 ** (-jnp.arange(half, dtype=x.dtype) / half)
            sinusoid = pos[..., None] * inv_freq
            sin, cos = (jnp.sin(sinusoid), jnp.cos(sinusoid))
            x1, x2 = jnp.split(x, 2, axis=-1)
            return jnp.concatenate([x1 * cos - x2 * sin, x2 * cos + x1 * sin], axis=-1)

        def rel_pos_bias(w, L):
            t = jnp.pad(w[:2 * L - 1], (0, L))
            t = jnp.tile(t, L)[:-L].reshape(L, 3 * L - 2)
            r = (2 * L - 1) // 2
            return t[:, r:3 * L - 2 - r]
        key = jax.random.key(seed)
        ks = jax.random.split(key, 20)

        def nrm(k, shape, std=0.02):
            return (jax.random.normal(k, shape, jnp.float32) * std).astype(jnp.float32)
        return {'query': jax.random.normal(ks[0], (B, T, D), jnp.float32), 'scala': jnp.ones((1,), jnp.float32), 'u_w': nrm(ks[1], (E, D)), 'u_b': jnp.zeros((E,), jnp.float32), 'v_w': nrm(ks[2], (E, D)), 'v_b': jnp.zeros((E,), jnp.float32), 'base_w': nrm(ks[3], (S, D)), 'base_b': jnp.zeros((S,), jnp.float32), 'qq_w': nrm(ks[4], (1, S)), 'qq_b': jnp.zeros((1, S), jnp.float32), 'qk_w': nrm(ks[5], (1, S)), 'qk_b': jnp.zeros((1, S), jnp.float32), 'lq_w': nrm(ks[6], (1, S)), 'lq_b': jnp.zeros((1, S), jnp.float32), 'lk_w': nrm(ks[7], (1, S)), 'lk_b': jnp.zeros((1, S), jnp.float32), 'o_w': nrm(ks[8], (D, E)), 'o_b': jnp.zeros((D,), jnp.float32), 'w': nrm(ks[9], (2 * MAXPOS - 1,))}
    _L0_attn_all = _L0_attn_setup()
    _L0_attn_in = {k: v for k, v in _L0_attn_all.items() if k in ('scala', 'u_w', 'u_b', 'v_w', 'v_b', 'base_w', 'base_b', 'qq_w', 'qq_b', 'qk_w', 'qk_b', 'lq_w', 'lq_b', 'lk_w', 'lk_b', 'o_w', 'o_b', 'w')}
    del _L0_attn_all

    def _L0_ffn_setup():
        import jax, jax.numpy as jnp
        import numpy as np
        D, H, E, B, S = (128, 512, 16, 8, 2048)
        MAX_GROUP_SIZE = 1024
        MIN_CAPACITY = 8
        CAPACITY_FACTOR = 1.0

        def _group_dims(num_tokens, num_experts):
            num_groups = -(-num_tokens // MAX_GROUP_SIZE)
            while num_tokens % num_groups != 0 or num_groups % num_experts != 0:
                num_groups += 1
            return (num_tokens // num_groups, num_groups)
        key = jax.random.key(seed)
        ks = jax.random.split(key, 6)
        s = 0.02
        return {'x': jax.random.normal(ks[0], (B, S, D), jnp.float32), 'gate_w': jax.random.normal(ks[1], (D, E), jnp.float32) * s, 'w1': jax.random.normal(ks[2], (E, D, H), jnp.float32) * s, 'b1': jnp.zeros((E, H), jnp.float32), 'w2': jax.random.normal(ks[3], (E, H, D), jnp.float32) * s, 'b2': jnp.zeros((E, D), jnp.float32), 'sw1': jax.random.normal(ks[4], (D, H), jnp.float32) * s, 'sb1': jnp.zeros((H,), jnp.float32), 'sw2': jax.random.normal(ks[5], (H, D), jnp.float32) * s, 'sb2': jnp.zeros((D,), jnp.float32)}
    _L0_ffn_all = _L0_ffn_setup()
    _L0_ffn_in = {k: v for k, v in _L0_ffn_all.items() if k in ('gate_w', 'w1', 'b1', 'w2', 'b2', 'sw1', 'sb1', 'sw2', 'sb2')}
    del _L0_ffn_all
    return {'x': x, 'L0_tok_w1': _L0_tok_in['w1'], 'L0_tok_w2': _L0_tok_in['w2'], 'L0_tok_fc_w': _L0_tok_in['fc_w'], 'L0_tok_fc_b': _L0_tok_in['fc_b'], 'L0_tok_ln_g': _L0_tok_in['ln_g'], 'L0_tok_ln_b': _L0_tok_in['ln_b'], 'L0_attn_scala': _L0_attn_in['scala'], 'L0_attn_u_w': _L0_attn_in['u_w'], 'L0_attn_u_b': _L0_attn_in['u_b'], 'L0_attn_v_w': _L0_attn_in['v_w'], 'L0_attn_v_b': _L0_attn_in['v_b'], 'L0_attn_base_w': _L0_attn_in['base_w'], 'L0_attn_base_b': _L0_attn_in['base_b'], 'L0_attn_qq_w': _L0_attn_in['qq_w'], 'L0_attn_qq_b': _L0_attn_in['qq_b'], 'L0_attn_qk_w': _L0_attn_in['qk_w'], 'L0_attn_qk_b': _L0_attn_in['qk_b'], 'L0_attn_lq_w': _L0_attn_in['lq_w'], 'L0_attn_lq_b': _L0_attn_in['lq_b'], 'L0_attn_lk_w': _L0_attn_in['lk_w'], 'L0_attn_lk_b': _L0_attn_in['lk_b'], 'L0_attn_o_w': _L0_attn_in['o_w'], 'L0_attn_o_b': _L0_attn_in['o_b'], 'L0_attn_w': _L0_attn_in['w'], 'L0_ffn_gate_w': _L0_ffn_in['gate_w'], 'L0_ffn_w1': _L0_ffn_in['w1'], 'L0_ffn_b1': _L0_ffn_in['b1'], 'L0_ffn_w2': _L0_ffn_in['w2'], 'L0_ffn_b2': _L0_ffn_in['b2'], 'L0_ffn_sw1': _L0_ffn_in['sw1'], 'L0_ffn_sb1': _L0_ffn_in['sb1'], 'L0_ffn_sw2': _L0_ffn_in['sw2'], 'L0_ffn_sb2': _L0_ffn_in['sb2']}

def reference(x, L0_tok_w1, L0_tok_w2, L0_tok_fc_w, L0_tok_fc_b, L0_tok_ln_g, L0_tok_ln_b, L0_attn_scala, L0_attn_u_w, L0_attn_u_b, L0_attn_v_w, L0_attn_v_b, L0_attn_base_w, L0_attn_base_b, L0_attn_qq_w, L0_attn_qq_b, L0_attn_qk_w, L0_attn_qk_b, L0_attn_lq_w, L0_attn_lq_b, L0_attn_lk_w, L0_attn_lk_b, L0_attn_o_w, L0_attn_o_b, L0_attn_w, L0_ffn_gate_w, L0_ffn_w1, L0_ffn_b1, L0_ffn_w2, L0_ffn_b2, L0_ffn_sw1, L0_ffn_sb1, L0_ffn_sw2, L0_ffn_sb2):
    import jax
    import jax.numpy as jnp

    def _L0_tok_ref(x, w1, w2, fc_w, fc_b, ln_g, ln_b):
        import jax, jax.numpy as jnp
        import numpy as np
        B, T, C = (16, 1000, 128)
        MS = 5
        RED = 2
        EXP = 1
        D = C * MS

        def _layernorm(h, g, b, eps=1e-05):
            m = jnp.mean(h, axis=-1, keepdims=True)
            v = jnp.var(h, axis=-1, keepdims=True)
            return (h - m) * jax.lax.rsqrt(v + eps) * g + b
        Bb, Tt, Cc = x.shape
        ms = MS
        pad = -Tt % ms
        if pad:
            x = jnp.pad(x, ((0, 0), (0, pad), (0, 0)))
        Tp = Tt + pad
        Tw = Tp // ms
        xt = jnp.swapaxes(x.reshape(Bb, Tw, ms, Cc), -1, -2)
        flat = xt.reshape(Bb, Tw, Cc * ms)
        y = jax.nn.sigmoid(jax.nn.relu(flat @ w1) @ w2)
        y = jax.nn.softmax(y.reshape(Bb, Tw, Cc, ms), axis=-1)
        pooled = jnp.sum(xt * y, axis=-1)
        return _layernorm(pooled @ fc_w + fc_b, ln_g, ln_b)

    def _L0_attn_ref(query, scala, u_w, u_b, v_w, v_b, base_w, base_b, qq_w, qq_b, qk_w, qk_b, lq_w, lq_b, lk_w, lk_b, o_w, o_b, w):
        import jax, jax.numpy as jnp
        import numpy as np
        B, T, D = (8, 1024, 128)
        S = 128
        E = 2 * D
        CHUNK = 64
        MAXPOS = 128
        EPS = 1e-05

        def rope_gn(x):
            b, g, n, s = x.shape
            half = s // 2
            pos = jnp.arange(g * n, dtype=x.dtype).reshape(g, n)
            inv_freq = 10000.0 ** (-jnp.arange(half, dtype=x.dtype) / half)
            sinusoid = pos[..., None] * inv_freq
            sin, cos = (jnp.sin(sinusoid), jnp.cos(sinusoid))
            x1, x2 = jnp.split(x, 2, axis=-1)
            return jnp.concatenate([x1 * cos - x2 * sin, x2 * cos + x1 * sin], axis=-1)

        def rel_pos_bias(w, L):
            t = jnp.pad(w[:2 * L - 1], (0, L))
            t = jnp.tile(t, L)[:-L].reshape(L, 3 * L - 2)
            r = (2 * L - 1) // 2
            return t[:, r:3 * L - 2 - r]
        b, t, d = query.shape
        pad = -t % CHUNK
        q = jnp.pad(query, ((0, 0), (0, pad), (0, 0)))
        g = q.shape[1] // CHUNK
        ms = jnp.mean(q * q, axis=-1, keepdims=True)
        x = q * jax.lax.rsqrt(ms + EPS) * scala
        u = jax.nn.silu(x @ u_w.T + u_b)
        v = jax.nn.silu(x @ v_w.T + v_b)
        base = jax.nn.silu(x @ base_w.T + base_b)

        def heads(wt, bs):
            return rope_gn((base * wt + bs).reshape(b, g, CHUNK, S))
        quad_q = heads(qq_w, qq_b)
        quad_k = heads(qk_w, qk_b)
        lin_q = heads(lq_w, lq_b)
        lin_k = heads(lk_w, lk_b)
        v_c = v.reshape(b, g, CHUNK, E)
        u_c = u.reshape(b, g, CHUNK, E)
        qk = jnp.einsum('bgns,bgms->bgnm', quad_q, quad_k)
        bias = rel_pos_bias(w, MAXPOS)[:CHUNK, :CHUNK]
        kern = jnp.square(jax.nn.relu(qk / CHUNK + bias))
        quadratic = jnp.einsum('bgnm,bgme->bgne', kern, v_c)
        lin_kv = jnp.einsum('bgns,bgne->bse', lin_k, v_c) / CHUNK
        linear = jnp.einsum('bgns,bse->bgne', lin_q, lin_kv)
        out = (u_c * (linear + quadratic)).reshape(b, g * CHUNK, E)
        out = out @ o_w.T + o_b
        return out[:, :t, :]

    def _L0_ffn_ref(x, gate_w, w1, b1, w2, b2, sw1, sb1, sw2, sb2):
        import jax, jax.numpy as jnp
        import numpy as np
        D, H, E, B, S = (128, 512, 16, 8, 2048)
        MAX_GROUP_SIZE = 1024
        MIN_CAPACITY = 8
        CAPACITY_FACTOR = 1.0

        def _group_dims(num_tokens, num_experts):
            num_groups = -(-num_tokens // MAX_GROUP_SIZE)
            while num_tokens % num_groups != 0 or num_groups % num_experts != 0:
                num_groups += 1
            return (num_tokens // num_groups, num_groups)
        Bn, Sn, Dn = x.shape
        En = gate_w.shape[1]
        T = Bn * Sn
        group_size, num_groups = _group_dims(T, En)
        cap = max(int(round(CAPACITY_FACTOR * group_size * num_groups / En)), MIN_CAPACITY)
        xg = x.reshape(num_groups, group_size, Dn)
        logits = jnp.einsum('gsd,de->gse', xg, gate_w)
        probs = jax.nn.softmax(logits, axis=-1)
        flat_probs = probs.transpose(2, 0, 1).reshape(En, T)
        scores, tok_idx = jax.lax.top_k(flat_probs, cap)
        xf = x.reshape(T, Dn)
        toks = xf[tok_idx]
        h = jax.nn.gelu(jnp.einsum('ecd,edh->ech', toks, w1) + b1[:, None, :])
        y = jnp.einsum('ech,ehd->ecd', h, w2) + b2[:, None, :]
        y = y * scores[..., None]
        routed = jnp.zeros_like(xf).at[tok_idx.reshape(-1)].add(y.reshape(-1, Dn))
        shared = jax.nn.gelu(xf @ sw1 + sb1) @ sw2 + sb2
        out = (routed + shared).reshape(Bn, Sn, Dn)
        return out
    h = _L0_tok_ref(x, L0_tok_w1, L0_tok_w2, L0_tok_fc_w, L0_tok_fc_b, L0_tok_ln_g, L0_tok_ln_b)
    h = h + _L0_attn_ref(_layernorm(h, axis=-1), L0_attn_scala, L0_attn_u_w, L0_attn_u_b, L0_attn_v_w, L0_attn_v_b, L0_attn_base_w, L0_attn_base_b, L0_attn_qq_w, L0_attn_qq_b, L0_attn_qk_w, L0_attn_qk_b, L0_attn_lq_w, L0_attn_lq_b, L0_attn_lk_w, L0_attn_lk_b, L0_attn_o_w, L0_attn_o_b, L0_attn_w)
    h = h + _L0_ffn_ref(_layernorm(h, axis=-1), L0_ffn_gate_w, L0_ffn_w1, L0_ffn_b1, L0_ffn_w2, L0_ffn_b2, L0_ffn_sw1, L0_ffn_sb1, L0_ffn_sw2, L0_ffn_sb2)
    return h

_drawn_inputs = setup_inputs


def setup_inputs(seed=0):
    import zlib

    import numpy as np

    out = dict(_drawn_inputs(seed))
    spreads = {'L0_tok_fc_b': (0.0, 0.1),
     'L0_tok_ln_g': (1.0, 0.2),
     'L0_tok_ln_b': (0.0, 0.1),
     'L0_attn_u_b': (0.0, 0.8),
     'L0_attn_v_b': (0.0, 0.8),
     'L0_attn_base_b': (0.0, 0.8),
     'L0_attn_qq_b': (0.0, 0.8),
     'L0_attn_qk_b': (0.0, 0.8),
     'L0_attn_lq_b': (0.0, 0.8),
     'L0_attn_lk_b': (0.0, 0.8),
     'L0_attn_o_b': (0.0, 2.0),
     'L0_ffn_b1': (0.0, 2.0),
     'L0_ffn_b2': (0.0, 2.0),
     'L0_ffn_sb1': (0.0, 2.0),
     'L0_ffn_sb2': (0.0, 2.0)}
    factors = {'L0_attn_u_w': 8.0,
     'L0_attn_v_w': 8.0,
     'L0_attn_base_w': 8.0,
     'L0_attn_qq_w': 8.0,
     'L0_attn_qk_w': 8.0,
     'L0_attn_lq_w': 8.0,
     'L0_attn_lk_w': 8.0,
     'L0_attn_o_w': 8.0,
     'L0_attn_w': 8.0,
     'L0_ffn_gate_w': 5.704,
     'L0_ffn_w1': 8.0,
     'L0_ffn_w2': 8.0,
     'L0_ffn_sw1': 8.0,
     'L0_ffn_sw2': 8.0}
    for name, (base, spread) in spreads.items():
        noise = np.random.default_rng([zlib.crc32(name.encode()), seed]).standard_normal(out[name].shape)
        drawn = base * np.exp(spread * noise) if base else spread * noise
        out[name] = jnp.asarray(drawn.astype(out[name].dtype))
    for name, factor in factors.items():
        out[name] = (out[name] * factor).astype(out[name].dtype)
    return out
```

```python
from contextlib import ExitStack

import numpy as np

import concourse.bass as bass
from concourse import mybir

F32 = mybir.dt.float32
F16 = mybir.dt.float16
U32 = mybir.dt.uint32
I32 = mybir.dt.int32
ALU = mybir.AluOpType
ACT = mybir.ActivationFunctionType
AX_X = mybir.AxisListType.X

BATCH, STEPS, C = 16, 750, 128
MS = 5
TW = STEPS // MS
TOKENS = BATCH * TW
HID = 2 * C * MS
KH = HID // 128
E = 2 * C
CHUNK = 64
PADDED = 3 * CHUNK
A_TOK = 2 * CHUNK
B_TOK = TW - A_TOK
PAD_TOK = PADDED - TW
MAXPOS = 128
GB = 2
GT = GB * TW
GROUPS = BATCH // GB
TT = 100
TPG = GT // TT
TILES = TOKENS // TT
EXPERTS, FF = 16, 512
KF = FF // 128
CAP = TOKENS // EXPERTS
ROW = C + EXPERTS
EPS = 1e-5
OFF_BLOCK = -1e30

SCALE = 16.0

TABLE = GT + PAD_TOK
COLUMNS = {}
_at = 0
for _name, _width in (("ident", 128), ("swap", 128), ("anti", CHUNK), ("mask", A_TOK), ("cos", TABLE), ("sin", TABLE)):
    COLUMNS[_name] = slice(_at, _at + _width)
    _at += _width
N_COLUMNS = _at
STEPS_R = 32
RCOLUMNS = {}
_at = 0
for _name, _width in (("same_expert", 128), ("before", TT), ("tile_first", EXPERTS * TILES), ("not_first", EXPERTS * TILES),
                      ("partition", 1), ("diagonal", 128), ("bit_value", STEPS_R), ("bit", STEPS_R + 1), ("pick_b2", EXPERTS)):
    RCOLUMNS[_name] = slice(_at, _at + _width)
    _at += _width
N_RCOLUMNS = _at
DIG_A, DIG_B = 10, 16
LIST = DIG_A * DIG_B
HALF_E = EXPERTS // 2
HC = CAP // 2
LO_ROW = 32


RING = 4
REGION = 13044


def routing_table():
    t = np.zeros((128, N_RCOLUMNS), np.float32)
    p = np.arange(128)
    t[:, RCOLUMNS["same_expert"]] = p[:, None] % EXPERTS == p[None, :] % EXPERTS
    t[:, RCOLUMNS["before"]] = p[:, None] < np.arange(TT)[None, :]
    tile = np.tile(np.arange(TILES), EXPERTS)
    t[:, RCOLUMNS["tile_first"]] = tile * TT
    t[:, RCOLUMNS["not_first"]] = tile > 0
    t[:, RCOLUMNS["partition"]] = p[:, None]
    t[:, RCOLUMNS["diagonal"]] = p[:, None] % HALF_E == p[None, :] % HALF_E
    bits = np.concatenate([1 << (29 - np.arange(30)), np.zeros(3, np.int64)]).astype(np.uint32)
    t[:, RCOLUMNS["bit_value"]] = bits[:STEPS_R].astype(np.float32)
    t[:, RCOLUMNS["bit"]] = bits.view(np.float32)
    e = np.arange(EXPERTS)
    t[:, RCOLUMNS["pick_b2"]] = (p[:, None] == e[None, :]) | (p[:, None] == LO_ROW + e[None, :])
    return t


def constant_table():
    t = np.zeros((128, N_COLUMNS), np.float32)
    p = np.arange(128)
    t[p, COLUMNS["ident"].start + p] = 1
    t[p, COLUMNS["swap"].start + (p + 64) % 128] = 1
    q = np.arange(CHUNK)
    t[q, COLUMNS["anti"].start + CHUNK - 1 - q] = 1
    t[:, COLUMNS["mask"]] = np.where(p[:, None] // CHUNK == p[None, :] // CHUNK, 0, OFF_BLOCK)
    half = C // 2
    inv_freq = (10000.0 ** (-np.arange(half, dtype=np.float32) / half)).astype(np.float32)
    pos = np.concatenate([np.arange(TW)] * GB + [np.arange(TW, PADDED)]).astype(np.float32)
    angle = (pos[None, :] * inv_freq[:, None]).astype(np.float32)
    t[:half, COLUMNS["cos"]] = t[half:, COLUMNS["cos"]] = np.cos(angle)
    t[:half, COLUMNS["sin"]] = -np.sin(angle)
    t[half:, COLUMNS["sin"]] = np.sin(angle)
    return t


V_QQW, V_QQB, V_QKW, V_QKB, V_LQW, V_LQB, V_LKW, V_LKB, V_BASE = range(9)
V_U = 9
V_SB1 = V_U + 2
V_B1 = V_SB1 + KF
N_VEC = V_B1 + EXPERTS * KF
HEADS = (("lk", V_LKW, V_LKB), ("qk", V_QKW, V_QKB), ("qq", V_QQW, V_QQB), ("lq", V_LQW, V_LQB))


def build(nc, a, out):
    x = a["x"]
    with ExitStack() as ctx:
        def sb(name, shape, dt=F32):
            return ctx.enter_context(nc.sbuf_tensor(name, shape, dt))

        def bank(name):
            return ctx.enter_context(nc.psum_tensor(name, [128, 512], F32))

        def sem(name):
            return ctx.enter_context(nc.semaphore(name))

        const = sb("const", [128, N_COLUMNS])
        ident, swap_m, mask = (const[:, COLUMNS[n]] for n in ("ident", "swap", "mask"))
        anti = const[0:CHUNK, COLUMNS["anti"]]
        cos, sin = const[:, COLUMNS["cos"]], const[:, COLUMNS["sin"]]

        arena = sb("arena", [128, 4 * MS * HID + 2 * MS * HID], F16)
        part = MS * HID
        w1h = arena[:, 0:part].rearrange("p (m n) -> p m n", m=MS)
        w1l = arena[:, part:2 * part].rearrange("p (m n) -> p m n", m=MS)
        w2h = arena[:, 2 * part:3 * part].rearrange("p (k m c) -> p k m c", k=KH, m=MS)
        w2l = arena[:, 3 * part:4 * part].rearrange("p (k m c) -> p k m c", k=KH, m=MS)
        stage = arena[:, 4 * part:6 * part].bitcast(F32)
        stage1 = stage.rearrange("p (m n) -> p m n", m=MS)
        stage2 = stage.rearrange("p (k n) -> p k n", k=KH)
        stage2m = stage.rearrange("p (k c m) -> p k m c", k=KH, m=MS)

        wT = sb("wT", [128, 8, 128])
        uT_w, vT_w, baseT_w, swapT_w, oT_w = wT[:, 0:2, :], wT[:, 2:4, :], wT[:, 4, :], wT[:, 5, :], wT[:, 6:8, :]
        fc_w = sb("fc_w", [128, 128])
        gate_w = sb("gate_w", [128, EXPERTS])
        vec = sb("vec", [128, N_VEC])
        vswap = sb("vswap", [128, V_U])
        whalf = sb("whalf", [128, 2, V_U])
        fcb_bc, lng_bc, lnb_bc, ob_bc = (sb(n, [TT, 128]) for n in ("fcb_bc", "lng_bc", "lnb_bc", "ob_bc"))
        scala = sb("scala", [TT, 1])
        vb_row = sb("vb_row", [1, E])
        sb2_bc = sb("sb2_bc", [TT, 128])
        ones = sb("ones", [128, 128])
        mhalf = sb("mhalf", [TT, TPG])
        zw = sb("zw", [CHUNK, A_TOK])
        biasA = sb("biasA", [128, A_TOK])
        halfb = sb("halfb", [128, 4])
        padc = sb("padc", [128, 4, PAD_TOK])
        padv = sb("padv", [128, 4])

        xbuf = sb("xbuf", [128, TPG * MS * C])
        x_tok = xbuf[0:TT, :].rearrange("p (k n) -> p k n", k=TPG)
        xp_xu = sb("xp_xu", [128, max(2 * MS * GT, DIG_B * EXPERTS * TILES // 2)])
        xp32, xu32 = (xp_xu[:, k * MS * GT:(k + 1) * MS * GT].rearrange("p (m n) -> p m n", m=MS) for k in (0, 1))
        xh = sb("xh", [128, MS, GT], F16)
        xl = sb("xl", [128, MS, GT], F16)
        hid = sb("hid", [128, 2, KH * GT], F16)
        hidh, hidl = (hid[:, k, :].rearrange("p (k n) -> p k n", k=KH) for k in (0, 1))
        mte = sb("mte", [128, 4, GT])
        mtanh, mexp = mte[:, 0:2, :], mte[:, 2:4, :]
        den, num, prod = (sb(n, [128, GT]) for n in ("den", "num", "prod"))
        pooled = sb("pooled", [128, GT])

        region = sb("region", [128, REGION])

        def carver():
            at = [0]

            def carve(shape, dt=F32):
                n = int(np.prod(shape[1:]))
                words = n if dt != F16 else (n + 1) // 2
                v = region[:, at[0]:at[0] + words]
                at[0] += words
                assert at[0] <= REGION, at[0]
                if dt != F32:
                    v = v.bitcast(dt)
                v = v[0:shape[0], 0:n]
                if len(shape) == 3:
                    v = v.rearrange("p (a n) -> p a n", a=shape[1])
                if len(shape) == 4:
                    v = v.rearrange("p (a b n) -> p a b n", a=shape[1], b=shape[2])
                return v
            return carve

        carve = carver()
        z = carve([TT, TPG, 128])
        h1 = carve([TT, TPG, 128])
        xn = carve([TT, TPG, 128])
        h1ob = carve([TT, TPG, 128])
        st6 = sb("st6", [TT, TPG, 6])
        mv = sb("mv", [TT, 3, TPG, 2])
        pst = sb("pst", [TT, 8, TPG])
        xnT = carve([128, GT])
        ptanh = carve([128, 2, GT])
        pz = carve([128, 4, GT])
        wst = pz.rearrange("p a n -> p (a n)")[:, 0:1024].rearrange("p (k n) -> p k n", k=8)
        vrows = pz.rearrange("p a n -> p (a n)")[0:N_VEC, 1024:1152]
        base2 = carve([128, 2, GT])
        u2 = carve([128, 2, GT])
        rot = carve([128, 2, GT])
        htmp = carve([128, 2, GT])
        qT = {n: carve([128, GB, PADDED]) for n in ("lk", "qk")}
        for n in ("qq", "lq"):
            qT[n] = carve([128, GB, TW])
        vtA = carve([128, GB, E])
        vtB = carve([CHUNK, GB, E])
        vA = carve([128, GB, E])
        vB = carve([CHUNK, GB, E])
        lkA = carve([128, GB, 128])
        lkB = carve([CHUNK, GB, 128])
        linkv = carve([128, GB, E])
        sA = carve([128, GB, A_TOK])
        sB = carve([CHUNK, GB, B_TOK])
        kA = carve([128, GB, A_TOK])
        kB = carve([CHUNK, GB, B_TOK])
        gT = carve([128, 2, GT])
        ctab = carve([128, 4, TABLE])
        h2 = sb("h2", [TT, TPG, 128])
        h2s = sb("h2s", [TT, TPG, 128])
        rows = sb("rows", [TT, TPG, ROW])
        n2T = sb("n2T", [128, GT])
        n2hl = sb("n2hl", [128, 2, TOKENS], F16)
        n2h, n2l = n2hl[:, 0, :], n2hl[:, 1, :]
        lmax = sb("lmax", [TT, TPG])
        lg = sb("lg", [TT, TPG, EXPERTS])
        pexp = sb("pexp", [TT, TPG, EXPERTS])
        psum_ = sb("psum_", [TT, TPG])
        prcp = sb("prcp", [TT, TPG])
        probs = sb("probs", [TT, TILES, EXPERTS])

        ew = EXPERTS * FF
        EC = 4

        def chunk(lo, c):
            at_ = (2 * (c // (EXPERTS // EC)) + lo) * ew + c % (EXPERTS // EC) * EC * FF
            return arena[:, at_:at_ + EC * FF]

        e1h, e1l = (arena[:, k * ew:(k + 1) * ew].rearrange("p (e n) -> p e n", e=EXPERTS) for k in (0, 1))
        e2h, e2l = (arena[:, k * ew:(k + 1) * ew].rearrange("p (e j n) -> p e j n", e=EXPERTS, j=KF) for k in (2, 3))
        estage = [arena[:, 4 * ew:4 * ew + 2 * EC * FF].bitcast(F32), xp_xu[:, 0:EC * FF]]
        sw_stage = hid[:, 0, :].bitcast(F32)[:, 0:2 * FF].rearrange("p (a n) -> p a n", a=2)
        sw = mte[:].rearrange("p a n -> p (a n)").bitcast(F16)[:, 0:4 * FF].rearrange("p (a n) -> p a n", a=4)
        sw1h, sw1l = sw[:, 0, :], sw[:, 1, :]
        sw2h, sw2l = (sw[:, k, :].rearrange("p (j n) -> p j n", j=KF) for k in (2, 3))
        shh, shl = (hid[:, 1, k * KF * GT:(k + 1) * KF * GT].rearrange("p (j n) -> p j n", j=KF) for k in (0, 1))
        rc = xbuf[:, 0:N_RCOLUMNS]
        b2st = sb("b2st", [2 * LO_ROW, 128])
        b2hl = sb("b2hl", [128, 128], F16)
        b2t = sb("b2t", [2 * LO_ROW, 128], F16)
        pickb = sb("pickb", [128, EXPERTS], F16)
        same16 = sb("same16", [128, 128], F16)
        before16 = sb("before16", [TT, TT], F16)
        ones16 = sb("ones16", [TT, TT], F16)

        carve = carver()
        sh32 = carve([128, KF, GT])
        h2b = carve([TT, TPG, 128])
        fin = carve([TT, TPG, 128])
        pe_major = carve([128, GT])
        hits = carve([128, GT])
        cur, cand, bitv = (sb(n, [128, 1], U32) for n in ("cur", "cand", "bitv"))
        cnt = sb("cnt", [128, 1], F16)
        thr_wide = carve([128, TT])
        thr = carve([TT, EXPERTS])
        over16, tie16, over_c, tie_c = (carve([TT, EXPERTS, TILES], F16) for _ in range(4))
        pos1, pos2 = (carve([TT, EXPERTS, TILES]) for _ in range(2))
        pos_i, dig_ai, dig_bi = (carve([TT, EXPERTS, TILES], I32) for _ in range(3))
        dig_a, dig_b = (carve([TT, EXPERTS, TILES], F16) for _ in range(2))
        ET = EXPERTS * TILES
        hotA = carve([TT, 2, DIG_A, HALF_E * TILES], F16)
        hotB = carve([TT, DIG_B, EXPERTS, TILES], F16)
        hotAt = n2hl[:].rearrange("p a n -> p (a n)")[0:TT, 0:DIG_A * ET].rearrange("p (h a n) -> p h a n", h=2, a=DIG_A)
        hotBp = xp_xu[:].bitcast(F16)[0:TT, 0:DIG_B * ET].rearrange("p (b e t) -> p b e t", b=DIG_B, e=EXPERTS)
        picked = carve([DIG_A * HALF_E, 2, DIG_B * HALF_E])
        lists_f = carve([DIG_A * HALF_E, 2, DIG_B])
        lists = carve([EXPERTS, LIST])
        idx = sb("idx", [HC, 2 * EXPERTS], U32)

        carve = carver()
        gath = [carve([HC, 2, ROW]) for _ in range(RING)]
        gidx = [sb(f"gidx{i}", [HC, 2], U32) for i in range(RING)]
        sidx = [sb(f"sidx{i}", [HC, 2], U32) for i in range(RING)]
        score = carve([HC, RING, 2])
        eXh, eXl = (carve([128, RING, CAP], F16) for _ in range(2))
        eh32 = carve([128, 2, KF * CAP])
        ehh, ehl = (carve([128, 2, KF * CAP], F16) for _ in range(2))
        ey = [carve([HC, 2, 128]) for _ in range(RING)]

        lists_dram = nc.dram_tensor("lists_dram", (DIG_A, HALF_E, 2, DIG_B), F32, kind="Internal").ap()
        h2_dram = nc.dram_tensor("h2_dram", (TILES, TT, C), F32, kind="Internal").ap()
        rows_dram = nc.dram_tensor("rows_dram", (TILES, TT, ROW), F32, kind="Internal").ap()

        T = [bank(f"T{i}") for i in range(3)]
        X = bank("X")
        Q = [bank(f"Q{i}") for i in range(4)]

        x_loaded = sem("x_loaded")
        w1_split = sem("w1_split")
        w2_split = sem("w2_split")
        w1_hi = sem("w1_hi")
        w2_hi = sem("w2_hi")
        small_loaded = sem("small_loaded")
        const_loaded = sem("const_loaded")
        setup_mm = sem("setup_mm")
        setup_copy = sem("setup_copy")
        setup_vec = sem("setup_vec")
        ones_done = sem("ones_done")
        xT_mm = sem("xT_mm")
        xT_copied = sem("xT_copied")
        xh_done = sem("xh_done")
        xl_done = sem("xl_done")
        xu_done = sem("xu_done")
        hid_mm = sem("hid_mm")
        hid_hi = sem("hid_hi")
        hid_lo = sem("hid_lo")
        mix_mm = sem("mix_mm")
        mix_tanh = sem("mix_tanh")
        mix_exp = sem("mix_exp")
        mix_step = sem("mix_step")
        pooled_done = sem("pooled_done")
        fc_mm = sem("fc_mm")
        ln_step = sem("ln_step")
        ln1_stats = sem("ln1_stats")
        ln1_rstd = sem("ln1_rstd")
        h1_done = sem("h1_done")
        ln2_stats = sem("ln2_stats")
        ln2_r = sem("ln2_r")
        h1ob_done = sem("h1ob_done")
        pool_step = sem("pool_step")
        xn_done = sem("xn_done")
        xnT_mm = sem("xnT_mm")
        xnT_copied = sem("xnT_copied")
        proj_mm = sem("proj_mm")
        proj_tanh = sem("proj_tanh")
        proj_z = sem("proj_z")
        base_done = sem("base_done")
        u_done = sem("u_done")
        rot_step = sem("rot_step")
        head_done = sem("head_done")
        v_mm = sem("v_mm")
        v_tanh = sem("v_tanh")
        v_done = sem("v_done")
        lkT_mm = sem("lkT_mm")
        lk_copied = sem("lk_copied")
        qk_mm = sem("qk_mm")
        score_done = sem("score_done")
        kern_done = sem("kern_done")
        linkv_mm = sem("linkv_mm")
        linkv_done = sem("linkv_done")
        ot_mm = sem("ot_mm")
        g_done = sem("g_done")
        out_mm = sem("out_mm")
        h2_done = sem("h2_done")
        ln3_stats = sem("ln3_stats")
        ln3_rstd = sem("ln3_rstd")
        n2_done = sem("n2_done")
        n2T_mm = sem("n2T_mm")
        n2T_copied = sem("n2T_copied")
        n2h_done = sem("n2h_done")
        n2_split = sem("n2_split")
        gate_mm = sem("gate_mm")
        lmax_done = sem("lmax_done")
        lg_done = sem("lg_done")
        lexp_done = sem("lexp_done")
        gsum_done = sem("gsum_done")
        grcp_done = sem("grcp_done")
        probs_done = sem("probs_done")
        rows_stored = sem("rows_stored")
        h2_stored = sem("h2_stored")
        h2s_done = sem("h2s_done")
        dve_passed = sem("dve_passed")
        pool_passed = sem("pool_passed")
        rc_loaded = sem("rc_loaded")
        sw_loaded = sem("sw_loaded")
        rc_ready = sem("rc_ready")
        sw_hi = sem("sw_hi")
        sw_split = sem("sw_split")
        ew_hi = sem("ew_hi")
        ew_split = sem("ew_split")
        b2_step = sem("b2_step")
        pm_mm = sem("pm_mm")
        cur_ready = sem("cur_ready")
        cand_ready = sem("cand_ready")
        hits_done = sem("hits_done")
        count_mm = sem("count_mm")
        bitv_done = sem("bitv_done")
        sh1_mm = sem("sh1_mm")
        sh_gelu = sem("sh_gelu")
        sh_hi = sem("sh_hi")
        sh_lo = sem("sh_lo")
        sh2_mm = sem("sh2_mm")
        h2b_loaded = sem("h2b_loaded")
        fin_done = sem("fin_done")
        out_stored = sem("out_stored")
        thr_wide_done = sem("thr_wide_done")
        thr_mm = sem("thr_mm")
        thr_done = sem("thr_done")
        masks_done = sem("masks_done")
        scans_done = sem("scans_done")
        prefix_mm = sem("prefix_mm")
        pos_done = sem("pos_done")
        digits_done = sem("digits_done")
        hot_done = sem("hot_done")
        lists_mm = sem("lists_mm")
        picked_done = sem("picked_done")
        lists_done = sem("lists_done")
        lists_stored = sem("lists_stored")
        lists_loaded = sem("lists_loaded")
        idx_mm = sem("idx_mm")
        idx_done = sem("idx_done")
        gidx_copied = sem("gidx_copied")
        sidx_copied = sem("sidx_copied")
        added = sem("added")
        eX_mm = sem("eX_mm")
        eX_hi = sem("eX_hi")
        eX_split = sem("eX_split")
        eh_mm = sem("eh_mm")
        eh_gelu = sem("eh_gelu")
        eh_hi = sem("eh_hi")
        eh_split = sem("eh_split")
        ey_mm = sem("ey_mm")
        ey_scaled = sem("ey_scaled")
        w1_loaded, w2_loaded = ([sem(f"{n}_loaded{i}") for i in range(MS)] for n in ("w1", "w2"))
        estage_loaded = [sem(f"estage_loaded{i}") for i in range(2)]
        gathered = [[sem(f"gathered{i}{h}") for h in range(2)] for i in range(RING)]
        scattered = [sem(f"scattered{h}") for h in range(2)]

        def past(group, n=1):
            return not isinstance(group, int) or group >= n

        def col(c0, n=1):
            return vec[:, c0:c0 + n]

        block = ctx.enter_context(nc.Block())

        SLOTS = KH + MS

        def schedule(eng, tok, attn):
            for s in range(SLOTS):
                tok(0, s)
            with eng.Fori(1, GROUPS - 1) as g:
                for s in range(SLOTS):
                    attn(g - 1, s)
                    tok(g, s)
            for s in range(SLOTS):
                attn(GROUPS - 2, s)
                tok(GROUPS - 1, s)
            for s in range(SLOTS):
                attn(GROUPS - 1, s)

        MIX_STEPS = 1 + 3 * (MS - 1) + 1

        def mix_after(m):
            return 1 + 3 * m if m >= -1 else -1

        expert_turn = [0]

        def expert_steps(eng, step):
            for k in range(3):
                step(k, k % RING)
            with eng.Fori(0, (EXPERTS - 4) // RING) as i:
                expert_turn[0] = i
                for q in range(RING):
                    step(i * RING + q + 3, (q + 3) % RING)
            for k in range(EXPERTS - 1, EXPERTS + 2):
                step(k, k % RING)

        def ring_use(k, q):
            if isinstance(k, int):
                return k // RING + 1
            return expert_turn[0] + (2 if q < 3 else 1)

        NSMALL = [0]

        @block.sync
        def _(sp):
            def load_x(g):
                src = x[bass.ds(g * GB, GB)].rearrange("b (t m) c -> (b t) (m c)", m=MS)
                sp.dma_start(x_tok[:], src.rearrange("(k p) n -> p k n", p=TT)).then_inc(x_loaded, 16)

            load_x(0)
            w1 = a["L0_tok_w1"].rearrange("(c m) n -> c m n", m=MS)
            for n in range(MS):
                sp.dma_start(stage1[:, :, n * 256:(n + 1) * 256], w1[:, :, n * 256:(n + 1) * 256]).then_inc(w1_loaded[n], 16)
            w2 = a["L0_tok_w2"].rearrange("(k p) n -> p k n", p=128)
            sp.wait_ge(w1_split, MS)
            for n in range(MS):
                sp.dma_start(stage2[:, 2 * n:2 * n + 2, :], w2[:, 2 * n:2 * n + 2, :]).then_inc(w2_loaded[n], 16)

            def tok(g, s):
                if s == 0 and not (isinstance(g, int) and g == GROUPS - 1):
                    sp.wait_ge(xT_mm, (g + 1) * MS)
                    load_x(g + 1)

            def attn(a_, s):
                if s == SLOTS - 1:
                    sp.wait_ge(h2s_done, a_ + 1)
                    sp.dma_start(h2_dram[bass.ds(a_ * TPG, TPG)].rearrange("k p n -> p k n"), h2s[:]).then_inc(h2_stored, 16)
                    sp.wait_ge(probs_done, a_ + 1)
                    sp.dma_start(rows_dram[bass.ds(a_ * TPG, TPG)].rearrange("k p n -> p k n"), rows[:]).then_inc(rows_stored, 16)

            tok(0, 0)
            with sp.Fori(1, GROUPS - 1) as g:
                for s in range(SLOTS):
                    attn(g - 1, s)
                    tok(g, s)
            attn(GROUPS - 2, SLOTS - 1)
            sp.wait_ge(xT_mm, GROUPS * MS)
            sp.dma_start(rc, a["routing"]).then_inc(rc_loaded, 16)
            sp.wait_ge(mix_mm, GROUPS * MS)
            sp.dma_start(sw_stage[:, 0, :], a["L0_ffn_sw1"]).then_inc(sw_loaded, 16)
            sp.dma_start(sw_stage[:, 1, :].rearrange("p (j n) -> p j n", j=KF), a["L0_ffn_sw2"].rearrange("(j p) n -> p j n", p=128))\
                .then_inc(sw_loaded, 16)
            sp.wait_ge(pooled_done, GROUPS)
            for c in range(2 * EXPERTS // EC):
                if c >= 2:
                    sp.wait_ge(ew_split, c - 1)
                e = slice(c % (EXPERTS // EC) * EC, (c % (EXPERTS // EC) + 1) * EC)
                if c < EXPERTS // EC:
                    src = a["L0_ffn_w1"][e].rearrange("e p n -> p e n")
                    dst = estage[c % 2].rearrange("p (e n) -> p e n", e=EC)
                else:
                    src = a["L0_ffn_w2"][e].rearrange("e (j p) n -> p (e j) n", p=128)
                    dst = estage[c % 2].rearrange("p (k n) -> p k n", k=EC * KF)
                sp.dma_start(dst, src).then_inc(estage_loaded[c % 2], 16)
            attn(GROUPS - 1, SLOTS - 1)
            sp.wait_ge(rows_stored, 16 * (GROUPS + 1))
            sp.wait_ge(h2_stored, 16 * (GROUPS + 1))
            with sp.Fori(0, GROUPS) as i:
                sp.wait_ge(fin_done, i + 1)
                sp.dma_start(h2b, h2_dram[bass.ds(i * TPG, TPG)].rearrange("k p n -> p k n")).then_inc(h2b_loaded, 16)
                sp.wait_ge(fin_done, i + 2)
                sp.dma_start(out[bass.ds(i * TPG * TT, TPG * TT)].rearrange("(k p) n -> p k n", p=TT), fin).then_inc(out_stored, 16)
            sp.wait_ge(lists_done, 1)
            sp.dma_start(lists_dram.rearrange("a e h b -> (a e) h b"), lists_f).then_inc(lists_stored, 16)
            sp.wait_ge(lists_stored, 16)
            for h in range(2):
                sp.dma_start(lists[h * HALF_E:(h + 1) * HALF_E, :].rearrange("e (a b) -> e a b", a=DIG_A),
                             lists_dram[:, :, h, :].rearrange("a e b -> e a b")).then_inc(lists_loaded, 16)

        @block.gpsimd
        def _(pool):
            def small(dst, src):
                NSMALL[0] += 1
                pool.dma_start(dst, src).then_inc(small_loaded, 16)

            pool.dma_start(const[:], a["constants"]).then_inc(const_loaded, 16)
            small(fc_w[:], a["L0_tok_fc_w"])
            small(fcb_bc[:], a["L0_tok_fc_b"].partition_broadcast(TT))
            small(lng_bc[:], a["L0_tok_ln_g"].partition_broadcast(TT))
            small(lnb_bc[:], a["L0_tok_ln_b"].partition_broadcast(TT))
            small(ob_bc[:], a["L0_attn_o_b"].partition_broadcast(TT))
            small(scala[:], a["L0_attn_scala"].partition_broadcast(TT))
            small(vb_row[:], a["L0_attn_v_b"].rearrange("(a n) -> a n", a=1))
            small(vtB[:, 0, :], a["L0_attn_v_b"].partition_broadcast(CHUNK))
            small(wst[:, 0:2, :], a["L0_attn_u_w"].rearrange("(e p) d -> p e d", p=128))
            small(wst[:, 2:4, :], a["L0_attn_v_w"].rearrange("(e p) d -> p e d", p=128))
            small(wst[:, 4, :], a["L0_attn_base_w"])
            small(wst[0:64, 5, :], a["L0_attn_base_w"][64:128, :])
            small(wst[64:128, 5, :], a["L0_attn_base_w"][0:64, :])
            small(wst[:, 6:8, :], a["L0_attn_o_w"].rearrange("d (e p) -> d e p", e=2))
            small(gate_w[:], a["L0_ffn_gate_w"])
            small(sb2_bc[:], a["L0_ffn_sb2"].partition_broadcast(TT))
            small(b2st[0:EXPERTS, :], a["L0_ffn_b2"])
            small(b2st[LO_ROW:LO_ROW + EXPERTS, :], a["L0_ffn_b2"])
            for i, n in enumerate(("qq_w", "qq_b", "qk_w", "qk_b", "lq_w", "lq_b", "lk_w", "lk_b")):
                small(vrows[i:i + 1, :], a["L0_attn_" + n])
            small(vrows[V_BASE:V_BASE + 1, :], a["L0_attn_base_b"].rearrange("(a n) -> a n", a=1))
            small(vrows[V_U:V_U + 2, :], a["L0_attn_u_b"].rearrange("(a n) -> a n", n=128))
            small(vrows[V_SB1:V_SB1 + KF, :], a["L0_ffn_sb1"].rearrange("(a n) -> a n", n=128))
            small(vrows[V_B1:N_VEC, :], a["L0_ffn_b1"].rearrange("e (a n) -> (e a) n", n=128))
            first = MAXPOS - CHUNK
            wv = a["L0_attn_w"]
            window = bass.AP(wv.tensor, first, [[1, CHUNK], [1, CHUNK]])
            small(zw[:, 0:CHUNK], window)
            small(zw[:, CHUNK:A_TOK], window)
            pool.memset(ones[:], 1.0).then_inc(ones_done, 1)
            pool.memset(mhalf[:], -0.5).then_inc(ones_done, 1)
            pool.memset(ones16[:], 1.0).then_inc(ones_done, 1)
            pool.memset(b2hl[:], 0.0).then_inc(ones_done, 1)
            pool.wait_ge(ones_done, 4)
            pool.wait_ge(small_loaded, 16 * NSMALL[0])

            def tok(g, s):
                if s == 0:
                    pool.wait_ge(xT_copied, (g + 1) * MS)
                    if past(g):
                        pool.wait_ge(pooled_done, g)
                    pool.sem_inc(pool_passed, 1)
                    pool.tensor_copy(xu32[:], xp32[:]).then_inc(xu_done, 1)

            POOL_STEPS = 8

            def attn(a_, s):
                n = [0]

                def step(ins):
                    ins.then_inc(pool_step, 1)
                    n[0] += 1
                    pool.wait_ge(pool_step, a_ * POOL_STEPS + base + n[0])

                if s == 0:
                    base = 0
                    pool.wait_ge(ln1_stats, a_ + 1)
                    pool.sem_inc(pool_passed, 1)
                    step(pool.tensor_scalar(pst[:, 0, :], mv[:, 0, :, 1], EPS, None, ALU.add))
                    pool.tensor_tensor(pst[:, 1, :], pst[:, 0, :], mhalf[:], ALU.pow).then_inc(ln1_rstd, 1)
                if s == 1:
                    base = 1
                    pool.wait_ge(ln2_stats, a_ + 1)
                    pool.sem_inc(pool_passed, 1)
                    step(pool.tensor_scalar(pst[:, 2, :], mv[:, 1, :, 1], EPS, None, ALU.add))
                    step(pool.tensor_tensor(pst[:, 3, :], pst[:, 2, :], mhalf[:], ALU.pow))
                    step(pool.tensor_tensor(pst[:, 4, :], pst[:, 3, :], pst[:, 3, :], ALU.mult))
                    step(pool.tensor_tensor(pst[:, 4, :], pst[:, 4, :], mv[:, 1, :, 1], ALU.mult))
                    pool.sem_inc(pool_passed, 1)
                    step(pool.tensor_scalar(pst[:, 4, :], pst[:, 4, :], EPS, None, ALU.add))
                    step(pool.tensor_tensor(pst[:, 5, :], pst[:, 4, :], mhalf[:], ALU.pow))
                    pool.tensor_tensor(pst[:, 6, :], pst[:, 5, :], pst[:, 3, :], ALU.mult).then_inc(ln2_r, 1)
                    pool.wait_ge(h1_done, a_ + 1)
                    pool.tensor_tensor(h1ob[:], h1[:], ob_bc[:].unsqueeze(1).broadcast_to([TT, TPG, 128]), ALU.add)\
                        .then_inc(h1ob_done, 1)
                if s == 10:
                    base = 7
                    pool.wait_ge(ln3_stats, a_ + 1)
                    pool.sem_inc(pool_passed, 1)
                    step(pool.tensor_scalar(pst[:, 7, :], mv[:, 2, :, 1], EPS, None, ALU.add))
                    pool.tensor_tensor(pst[:, 7, :], pst[:, 7, :], mhalf[:], ALU.pow).then_inc(ln3_rstd, 1)
                    pool.wait_ge(h2_done, a_ + 1)
                    pool.wait_ge(h2_stored, 16 * (a_ + 1))
                    pool.tensor_tensor(h2s[:], h2[:], sb2_bc[:].unsqueeze(1).broadcast_to([TT, TPG, 128]), ALU.add)\
                        .then_inc(h2s_done, 1)

            schedule(pool, tok, attn)

            pool.sem_inc(sh_lo, 1)
            with pool.Fori(0, GROUPS) as i:
                pool.wait_ge(sh_gelu, (i + 1) * KF + KF)
                pool.wait_ge(sh2_mm, i + 1)
                pool.sem_inc(pool_passed, 1)
                pool.tensor_copy(shh, sh32).then_inc(sh_hi, 1)
                pool.wait_ge(sh_hi, i + 1)
                pool.tensor_tensor(shl, sh32, shh, ALU.subtract).then_inc(sh_lo, 1)

            table = rows_dram.rearrange("k p n -> (k p) n")

            def gather(e, q):
                pool.wait_ge(gidx_copied, e + 1)
                pool.sem_inc(pool_passed, 1)
                for h in range(2):
                    pool.indirect_dma_start(gath[q][:, h, :], None, table,
                                            bass.IndirectOffsetOnAxis(ap=gidx[q][:, h:h + 1], axis=0))\
                        .then_inc(gathered[q][h], 16)

            def scatter(e, q):
                pool.wait_ge(ey_scaled, e + 1)
                if past(e):
                    pool.wait_ge(scattered[0], 16 * e)
                    pool.wait_ge(scattered[1], 16 * e)
                pool.sem_inc(added, 1)
                for h in range(2):
                    pool.indirect_dma_start(out, bass.IndirectOffsetOnAxis(ap=sidx[q][:, h:h + 1], axis=0), ey[q][:, h, :], None,
                                            compute_op=ALU.add).then_inc(scattered[h], 16)

            gather(0, 0)

            def step(k, q):
                if not isinstance(k, int) or k + 1 < EXPERTS:
                    gather(k + 1, (q + 1) % RING)
                if isinstance(k, int) and k == 1:
                    pool.wait_ge(out_stored, 16 * GROUPS)
                if past(k, 2):
                    scatter(k - 2, (q + 2) % RING)

            expert_steps(pool, step)
            pool.wait_ge(scattered[0], 16 * EXPERTS)
            pool.wait_ge(scattered[1], 16 * EXPERTS)

        @block.scalar
        def _(act):
            def prep(g, m):
                act.wait_ge(xT_mm, g * MS + m + 1)
                if past(g):
                    act.wait_ge(xu_done, g)
                act.activation(xp32[:, m, :], X[:, 0:GT], ACT.Copy).then_inc(xT_copied, 1)

            for m in range(MS):
                prep(0, m)
            for n in range(MS):
                act.wait_ge(w1_loaded[n], 16)
                act.activation(w1h[:, :, n * 256:(n + 1) * 256], stage1[:, :, n * 256:(n + 1) * 256], ACT.Copy, scale=SCALE)\
                    .then_inc(w1_hi, 1)
            def setup():
                act.wait_ge(setup_mm, 1)
                act.activation(wT[:, 0:4, :], Q[0][:].rearrange("p (k n) -> p k n", k=4), ACT.Copy).then_inc(setup_copy, 1)
                act.wait_ge(setup_mm, 2)
                act.activation(wT[:, 4:8, :], Q[1][:].rearrange("p (k n) -> p k n", k=4), ACT.Copy).then_inc(setup_copy, 1)
                act.wait_ge(setup_mm, 3)
                act.activation(vec[:], Q[2][:, 0:N_VEC], ACT.Copy).then_inc(setup_copy, 1)
                act.wait_ge(setup_mm, 4)
                act.activation(vswap[:], Q[3][:, 0:V_U], ACT.Copy).then_inc(setup_copy, 1)
                act.wait_ge(setup_copy, 4)
                act.activation(padv[:, 0:1], col(V_BASE), ACT.Tanh, scale=0.5).then_inc(setup_copy, 1)
                act.activation(padv[:, 1:2], vswap[:, V_BASE:V_BASE + 1], ACT.Tanh, scale=0.5).then_inc(setup_copy, 1)
                act.wait_ge(small_loaded, 16 * NSMALL[0])
                act.activation(vtB[:, 1, :], vtB[:, 0, :], ACT.Tanh, scale=0.5).then_inc(setup_copy, 1)
                act.activation(halfb[:, 0:1], col(V_BASE), ACT.Copy, scale=0.5)
                act.activation(halfb[:, 1:2], vswap[:, V_BASE:V_BASE + 1], ACT.Copy, scale=0.5)
                act.activation(halfb[:, 2:4], col(V_U, 2), ACT.Copy, scale=0.5).then_inc(setup_copy, 1)

            def last(s):
                if s == 5:
                    act.wait_ge(sw_loaded, 32)
                    act.wait_ge(pooled_done, GROUPS)
                    act.activation(sw1h, sw_stage[:, 0, :], ACT.Copy)
                    act.activation(sw[:, 2, :], sw_stage[:, 1, :], ACT.Copy).then_inc(sw_hi, 1)
                c = s - 5
                if 0 <= c < 2 * EXPERTS // EC:
                    act.wait_ge(mix_mm, GROUPS * MS)
                    act.wait_ge(estage_loaded[c % 2], 16 * (c // 2 + 1))
                    act.activation(chunk(0, c), estage[c % 2], ACT.Copy).then_inc(ew_hi, 1)

            w2_now = [0]

            def tok(g, s):
                if isinstance(g, int) and s >= 2 and w2_now[0] < MS:
                    n = w2_now[0]
                    w2_now[0] += 1
                    act.wait_ge(w2_loaded[n], 16)
                    for k in (2 * n, 2 * n + 1):
                        ins = act.activation(w2h[:, k], stage2m[:, k], ACT.Copy, scale=SCALE)
                    ins.then_inc(w2_hi, 1)
                if isinstance(g, int) and g == 0 and s == KH:
                    setup()
                if s < KH:
                    act.wait_ge(hid_mm, g * KH + s + 1)
                    act.activation(hidh[:, s, :], T[s % 3][:, 0:GT], ACT.Relu).then_inc(hid_hi, 1)
                else:
                    m = s - KH
                    act.wait_ge(mix_mm, g * MS + m + 1)
                    act.activation(mtanh[:, m % 2, :], T[s % 3][:, 0:GT], ACT.Tanh, scale=0.5 / SCALE ** 2)\
                        .then_inc(mix_tanh, 1)
                    act.wait_ge(mix_tanh, g * MS + m + 1)
                    if past(g) or m >= 2:
                        act.wait_ge(mix_step, g * MIX_STEPS + mix_after(m - 2))
                    act.activation(mexp[:, m % 2, :], mtanh[:, m % 2, :], ACT.Exp, scale=0.5).then_inc(mix_exp, 1)
                    if not (isinstance(g, int) and g == GROUPS - 1):
                        prep(g + 1, m)

            def attn(a_, s):
                if isinstance(a_, int) and a_ == GROUPS - 1:
                    last(s)
                if s == 3:
                    act.wait_ge(xnT_mm, a_ + 1)
                    act.activation(xnT[:], Q[0][:, 0:GT], ACT.Copy).then_inc(xnT_copied, 1)
                if s in (4, 5):
                    for i in ((0, 1) if s == 4 else (2, 3)):
                        bank_ = Q[(1, 2, 3, 0)[i]]
                        bias = (col(V_BASE), vswap[:, V_BASE:V_BASE + 1], col(V_U), col(V_U + 1))[i]
                        act.wait_ge(proj_mm, a_ * 4 + i + 1)
                        if i >= 2:
                            act.wait_ge(base_done, a_ * 2 + i - 1)
                        act.activation(ptanh[:, i % 2, :], bank_[:, 0:GT], ACT.Tanh, bias=halfb[:, i:i + 1], scale=0.5)\
                            .then_inc(proj_tanh, 1)
                        act.activation(pz[:, i, :], bank_[:, 0:GT], ACT.Identity, bias=bias).then_inc(proj_z, 1)
                if s == 6:
                    act.wait_ge(v_mm, a_ * 2 + 1)
                    act.activation(vtA[:], Q[1][:].rearrange("p (b n) -> p b n", b=GB), ACT.Tanh, scale=0.5)\
                        .then_inc(v_tanh, 1)
                    act.wait_ge(v_mm, a_ * 2 + 2)
                    act.activation(vtB[0:B_TOK], Q[2][0:B_TOK, :].rearrange("p (b n) -> p b n", b=GB), ACT.Tanh, scale=0.5)\
                        .then_inc(v_tanh, 1)
                    act.wait_ge(lkT_mm, a_ + 1)
                    q3 = Q[3][:].rearrange("p (k b n) -> p k b n", k=2, b=GB)
                    act.activation(lkA[:], q3[:, 0], ACT.Copy)
                    act.activation(lkB[:], q3[0:CHUNK, 1], ACT.Copy).then_inc(lk_copied, 1)
                if s == 8:
                    act.wait_ge(linkv_mm, a_ + 1)
                    act.activation(linkv[:], Q[1][:].rearrange("p (b n) -> p b n", b=GB), ACT.Copy, scale=1.0 / CHUNK)\
                        .then_inc(linkv_done, 1)
                if s == 12:
                    act.wait_ge(n2T_mm, a_ + 1)
                    act.activation(n2T[:], Q[1][:, 0:GT], ACT.Copy).then_inc(n2T_copied, 1)
                if s == 13:
                    act.wait_ge(lg_done, a_ + 1)
                    act.activation(pexp[:], lg[:], ACT.Exp).then_inc(lexp_done, 1)

            schedule(act, tok, attn)

            act.sem_inc(sh_gelu, KF)
            with act.Fori(0, GROUPS) as i:
                act.wait_ge(sh_lo, i + 1)
                for j in range(KF):
                    act.wait_ge(sh1_mm, i * KF + j + 1)
                    act.activation(sh32[:, j, :], Q[j][:, 0:GT], ACT.Gelu_apprx_tanh, bias=col(V_SB1 + j)).then_inc(sh_gelu, 1)

            def step(k, q):
                if not isinstance(k, int) or 1 <= k <= EXPERTS:
                    e, r2 = k - 1, (q + 1) % 2
                    if past(e):
                        act.wait_ge(eh_split, e)
                    for j in range(KF):
                        act.wait_ge(eh_mm, 2 * e + j // 2 + 1)
                        bias = vec[:, bass.ds(V_B1 + e * KF + j, 1)]
                        ins = act.activation(eh32[:, r2, j * CAP:(j + 1) * CAP], Q[2 * r2 + j // 2][:, j % 2 * CAP:(j % 2 + 1) * CAP],
                                             ACT.Gelu_apprx_tanh, bias=bias)
                    ins.then_inc(eh_gelu, 1)

            expert_steps(act, step)

        @block.tensor
        def _(pe):
            def transposes(dst, src, n=TPG):
                for k in range(n):
                    ins = pe.transpose(dst[:, k * TT:(k + 1) * TT], src(k), ident[0:TT, 0:TT])
                return ins

            def prep(g, m):
                pe.wait_ge(x_loaded, 16 * (g + 1))
                if past(g) or m > 0:
                    pe.wait_ge(xT_copied, g * MS + m)
                transposes(X, lambda k: x_tok[:, k, m * C:(m + 1) * C]).then_inc(xT_mm, 1)

            def setup():
                pe.wait_ge(small_loaded, 16 * NSMALL[0])
                for k in range(8):
                    ins = pe.transpose(Q[k // 4][:, (k % 4) * 128:(k % 4 + 1) * 128], wst[:, k, :], ident)
                    if k % 4 == 3:
                        ins.then_inc(setup_mm, 1)
                pe.transpose(Q[2][:, 0:N_VEC], vrows, ident[0:N_VEC, 0:N_VEC]).then_inc(setup_mm, 1)
                pe.wait_ge(setup_copy, 3)
                pe.matmul(Q[3][:, 0:V_U], swap_m, vec[:, 0:V_U], start=True, stop=True).then_inc(setup_mm, 1)
                pe.matmul(Q[0][:, 0:CHUNK], zw[:], anti, start=True, stop=True).then_inc(setup_mm, 1)

            pe.wait_ge(const_loaded, 16)
            for m in range(MS):
                prep(0, m)

            def tok(g, s):
                if isinstance(g, int) and g == 0 and s == KH:
                    setup()
                dst = T[s % 3][:, 0:GT]
                if s < KH:
                    pe.wait_ge(xl_done, (g + 1) * MS)
                    if s < 3 and past(g):
                        pe.wait_ge(mix_tanh, g * MS + s - 2)
                    if s >= 3:
                        pe.wait_ge(hid_lo, g * KH + s - 2)
                    if isinstance(g, int) and g == 0:
                        pe.wait_ge(w1_split, s // 2 + 1)
                    n = slice(s * 128, (s + 1) * 128)
                    for m in range(MS):
                        pe.matmul(dst, w1h[:, m, n], xh[:, m, :], start=(m == 0), stop=False)
                        pe.matmul(dst, w1h[:, m, n], xl[:, m, :], start=False, stop=False)
                        ins = pe.matmul(dst, w1l[:, m, n], xh[:, m, :], start=False, stop=(m == MS - 1))
                    ins.then_inc(hid_mm, 1)
                else:
                    m = s - KH
                    if isinstance(g, int) and g == 0:
                        pe.wait_ge(w2_split, MS)
                    pe.wait_ge(hid_lo, (g + 1) * KH)
                    if m >= 3:
                        pe.wait_ge(mix_tanh, g * MS + m - 2)
                    for k in range(KH):
                        pe.matmul(dst, w2h[:, k, m, :], hidh[:, k, :], start=(k == 0), stop=False)
                        pe.matmul(dst, w2h[:, k, m, :], hidl[:, k, :], start=False, stop=False)
                        ins = pe.matmul(dst, w2l[:, k, m, :], hidh[:, k, :], start=False, stop=(k == KH - 1))
                    ins.then_inc(mix_mm, 1)
                    if not (isinstance(g, int) and g == GROUPS - 1):
                        prep(g + 1, m)

            def attn(a_, s):
                if s == 0:
                    pe.wait_ge(pooled_done, a_ + 1)
                    pe.wait_ge(xT_copied, (a_ + 2) * MS if not (isinstance(a_, int) and a_ == GROUPS - 1) else GROUPS * MS)
                    for k in range(TPG):
                        ins = pe.matmul(X[0:TT, k * 128:(k + 1) * 128], pooled[:, k * TT:(k + 1) * TT], fc_w[:], start=True, stop=True)
                    ins.then_inc(fc_mm, 1)
                if s == 3:
                    pe.wait_ge(xn_done, a_ + 1)
                    transposes(Q[0], lambda k: xn[:, k, :]).then_inc(xnT_mm, 1)
                if s in (4, 5):
                    pe.wait_ge(xnT_copied, a_ + 1)
                    for i in ((0, 1) if s == 4 else (2, 3)):
                        wt = (baseT_w, swapT_w, uT_w[:, 0, :], uT_w[:, 1, :])[i]
                        pe.matmul(Q[(1, 2, 3, 0)[i]][:, 0:GT], wt, xnT[:], start=True, stop=True).then_inc(proj_mm, 1)
                if s == 6:
                    pe.wait_ge(proj_z, a_ * 4 + 4)
                    for b in range(GB):
                        t0 = b * TW
                        o = Q[1][:, b * E:(b + 1) * E]
                        pe.matmul(o, xnT[:, t0:t0 + A_TOK], vT_w, start=True, stop=False)
                        ins = pe.matmul(o, ones[0:1, 0:A_TOK], vb_row[:], start=False, stop=True)
                    ins.then_inc(v_mm, 1)
                    for b in range(GB):
                        t0 = b * TW + A_TOK
                        o = Q[2][0:B_TOK, b * E:(b + 1) * E]
                        pe.matmul(o, xnT[:, t0:t0 + B_TOK], vT_w, start=True, stop=False)
                        ins = pe.matmul(o, ones[0:1, 0:B_TOK], vb_row[:], start=False, stop=True)
                    ins.then_inc(v_mm, 1)
                    pe.wait_ge(head_done, a_ * 4 + 1)
                    for b in range(GB):
                        pe.transpose(Q[3][:, b * 128:(b + 1) * 128], qT["lk"][:, b, 0:A_TOK], ident)
                        ins = pe.transpose(Q[3][0:CHUNK, (GB + b) * 128:(GB + b + 1) * 128], qT["lk"][:, b, A_TOK:PADDED], ident)
                    ins.then_inc(lkT_mm, 1)
                if s == 7:
                    pe.wait_ge(head_done, a_ * 4 + 4)
                    for b in range(GB):
                        pe.matmul(Q[0][:, b * A_TOK:(b + 1) * A_TOK], qT["qk"][:, b, 0:A_TOK], qT["qq"][:, b, 0:A_TOK],
                                  start=True, stop=True)
                        c0 = GB * A_TOK + b * B_TOK
                        ins = pe.matmul(Q[0][0:CHUNK, c0:c0 + B_TOK], qT["qk"][:, b, A_TOK:PADDED], qT["qq"][:, b, A_TOK:TW],
                                        start=True, stop=True)
                    ins.then_inc(qk_mm, 1)
                if s == 8:
                    pe.wait_ge(lk_copied, a_ + 1)
                    pe.wait_ge(v_done, a_ * 2 + 2)
                    for b in range(GB):
                        o = Q[1][:, b * E:(b + 1) * E]
                        pe.matmul(o, lkA[:, b, :], vA[:, b, :], start=True, stop=False)
                        ins = pe.matmul(o, lkB[:, b, :], vB[:, b, :], start=False, stop=True)
                    ins.then_inc(linkv_mm, 1)
                if s == 9:
                    pe.wait_ge(linkv_done, a_ + 1)
                    pe.wait_ge(kern_done, a_ + 1)
                    for i in range(2):
                        e = slice(i * 128, (i + 1) * 128)
                        for b in range(GB):
                            t0 = b * TW
                            o = Q[2 + i]
                            pe.matmul(o[:, t0:t0 + TW], linkv[:, b, e], qT["lq"][:, b, :], start=True, stop=False)
                            pe.matmul(o[:, t0:t0 + A_TOK], vA[:, b, e], kA[:, b, :], start=False, stop=False)
                            ins = pe.matmul(o[:, t0 + A_TOK:t0 + TW], vB[:, b, e], kB[:, b, :], start=False, stop=True)
                    ins.then_inc(ot_mm, 1)
                if s == 10:
                    pe.wait_ge(g_done, a_ + 1)
                    for k in range(TPG):
                        o = Q[0][0:TT, k * 128:(k + 1) * 128]
                        for i in range(2):
                            ins = pe.matmul(o, gT[:, i, k * TT:(k + 1) * TT], oT_w[:, i, :], start=(i == 0), stop=(i == 1))
                    ins.then_inc(out_mm, 1)
                if s == 12:
                    pe.wait_ge(n2_done, a_ + 1)
                    transposes(Q[1], lambda k: rows[:, k, 0:C]).then_inc(n2T_mm, 1)
                if s == 13:
                    pe.wait_ge(n2T_copied, a_ + 1)
                    for k in range(TPG):
                        ins = pe.matmul(Q[2][0:TT, k * EXPERTS:(k + 1) * EXPERTS], n2T[:, k * TT:(k + 1) * TT], gate_w[:],
                                        start=True, stop=True)
                    ins.then_inc(gate_mm, 1)

            schedule(pe, tok, attn)

            pe.wait_ge(probs_done, GROUPS)
            for n in range(TPG):
                ins = pe.transpose(T[0][:, n * TT:(n + 1) * TT], probs[:, n * 8:(n + 1) * 8, :].rearrange("p k e -> p (k e)"),
                                   ident[0:TT, 0:TT])
            ins.then_inc(pm_mm, 1)

            pe.wait_ge(rc_ready, 1)
            pe.wait_ge(sw_split, 1)
            pe.wait_ge(n2_split, GROUPS)
            pe.sem_inc(sh2_mm, 1)
            with pe.Fori(0, GROUPS) as i:
                def count(q):
                    pe.wait_ge(hits_done, i * 4 + q + 1)
                    pe.matmul(T[1][:, 0:1], same16[:], cnt[:], start=True, stop=True).then_inc(count_mm, 1)

                pe.wait_ge(sh_gelu, i * KF + KF)
                toks = bass.ds(i * GT, GT)
                for j in range(KF):
                    n = slice(j * 128, (j + 1) * 128)
                    pe.matmul(Q[j][:, 0:GT], sw1h[:, n], n2h[:, toks], start=True, stop=False)
                    pe.matmul(Q[j][:, 0:GT], sw1h[:, n], n2l[:, toks], start=False, stop=False)
                    pe.matmul(Q[j][:, 0:GT], sw1l[:, n], n2h[:, toks], start=False, stop=True).then_inc(sh1_mm, 1)
                count(0)
                count(1)
                pe.wait_ge(sh_lo, i + 2)
                pe.wait_ge(fin_done, i + 1)
                for k in range(TPG):
                    o = X[0:TT, k * 128:(k + 1) * 128]
                    t = slice(k * TT, (k + 1) * TT)
                    for j in range(KF):
                        pe.matmul(o, shh[:, j, t], sw2h[:, j, :], start=(j == 0), stop=False)
                        pe.matmul(o, shl[:, j, t], sw2h[:, j, :], start=False, stop=False)
                        ins = pe.matmul(o, shh[:, j, t], sw2l[:, j, :], start=False, stop=(j == KF - 1))
                ins.then_inc(sh2_mm, 1)
                count(2)
                count(3)

            pe.wait_ge(thr_wide_done, 1)
            pe.transpose(T[2][0:TT, 0:128], thr_wide, ident).then_inc(thr_mm, 1)
            pe.wait_ge(scans_done, 2)
            later = [T[n][0:TT, 0:ET].rearrange("p (e t) -> p e t", e=EXPERTS)[:, :, 1:TILES] for n in (0, 1)]
            flat = lambda v: v.rearrange("p e t -> p (e t)")
            pe.matmul(T[0][0:TT, 0:ET], before16[:], flat(over16), start=True, stop=False)
            pe.matmul(later[0], ones16[:], over_c[:, :, 0:TILES - 1], start=False, stop=True)
            pe.matmul(T[1][0:TT, 0:ET], before16[:], flat(tie16), start=True, stop=False)
            pe.matmul(later[1], ones16[:], tie_c[:, :, 0:TILES - 1], start=False, stop=False)
            pe.matmul(T[1][0:TT, 0:ET].rearrange("p (e t) -> p e t", e=EXPERTS), ones16[:],
                      over_c[:, :, TILES - 1:TILES].broadcast_to([TT, EXPERTS, TILES]), start=False, stop=True).then_inc(prefix_mm, 1)
            pe.wait_ge(hot_done, 1)
            for h in range(2):
                e = slice(h * HALF_E, (h + 1) * HALF_E)
                o = Q[h][0:DIG_A * HALF_E, 0:DIG_B * HALF_E]

                def tile(t, first, last_):
                    of_t = [v[:, h].rearrange("p a (e t) -> p (a e) t", t=TILES)[:, :, t] for v in (hotA, hotAt)]
                    pe.matmul(o, of_t[0], hotBp[:, :, e, t], start=first, stop=False)
                    return pe.matmul(o, of_t[1], hotB[:, :, e, t], start=False, stop=last_)

                for t in range(TILES):
                    ins = tile(t, t == 0, t == TILES - 1)
            ins.then_inc(lists_mm, 1)
            pe.wait_ge(lists_loaded, 32)
            for h in range(2):
                ins = pe.transpose(T[2][0:HC, h * EXPERTS:(h + 1) * EXPERTS], lists[:, h * HC:(h + 1) * HC], ident[0:EXPERTS, 0:EXPERTS])
            ins.then_inc(idx_mm, 1)

            def step(k, q):
                if not isinstance(k, int) or k < EXPERTS:
                    for h in range(2):
                        pe.wait_ge(gathered[q][h], 16 * ring_use(k, q))
                        ins = pe.transpose(T[q % 2][:, h * HC:(h + 1) * HC], gath[q][:, h, 0:C], ident[0:HC, 0:HC])
                    ins.then_inc(eX_mm, 1)
                if not isinstance(k, int) or 1 <= k <= EXPERTS:
                    e, r2, slot = k - 1, (q + 1) % 2, (q + 3) % RING
                    pe.wait_ge(eX_split, e + 1)
                    for j in range(KF):
                        o = Q[2 * r2 + j // 2][:, j % 2 * CAP:(j % 2 + 1) * CAP]
                        wh, wl = (v[:, bass.ds(e, 1), j * 128:(j + 1) * 128].rearrange("p a n -> p (a n)") for v in (e1h, e1l))
                        pe.matmul(o, wh, eXh[:, slot, :], start=True, stop=False)
                        pe.matmul(o, wh, eXl[:, slot, :], start=False, stop=False)
                        ins = pe.matmul(o, wl, eXh[:, slot, :], start=False, stop=True)
                        if j % 2:
                            ins.then_inc(eh_mm, 1)
                if past(k, 2):
                    e, r2 = k - 2, q % 2
                    pe.wait_ge(eh_split, e + 2)
                    for h in range(2):
                        o = (T[2], X)[r2][0:HC, h * 128:(h + 1) * 128]
                        for j in range(KF):
                            sl = slice(j * CAP + h * HC, j * CAP + (h + 1) * HC)
                            wh, wl = (v[:, bass.ds(e, 1), j, :].rearrange("p a n -> p (a n)") for v in (e2h, e2l))
                            pe.matmul(o, ehh[:, r2, sl], wh, start=(j == 0), stop=False)
                            pe.matmul(o, ehl[:, r2, sl], wh, start=False, stop=False)
                            pe.matmul(o, ehh[:, r2, sl], wl, start=False, stop=False)
                        ins = pe.matmul(o, pickb[:, bass.ds(e, 1)].broadcast_to([128, HC]), b2hl[:], start=False, stop=True)
                    ins.then_inc(ey_mm, 1)

            expert_steps(pe, step)

        @block.vector
        def _(dve):
            def split_x(g, m):
                dve.wait_ge(xT_copied, g * MS + m + 1)
                if past(g):
                    dve.wait_ge(hid_mm, g * KH)
                dve.tensor_copy(xh[:, m, :], xp32[:, m, :]).then_inc(xh_done, 1)
                dve.wait_ge(xh_done, g * MS + m + 1)
                dve.tensor_tensor(xl[:, m, :], xp32[:, m, :], xh[:, m, :], ALU.subtract).then_inc(xl_done, 1)

            for m in range(MS):
                split_x(0, m)
            for n in range(MS):
                cols = slice(n * 256, (n + 1) * 256)
                dve.wait_ge(w1_hi, n + 1)
                dve.scalar_tensor_tensor(w1l[:, :, cols], stage1[:, :, cols], SCALE, w1h[:, :, cols], ALU.mult, ALU.subtract)\
                    .then_inc(w1_split, 1)

            def setup():
                n = [0]

                def step(ins):
                    n[0] += 1
                    ins.then_inc(setup_vec, 1)
                    dve.wait_ge(setup_vec, n[0])

                dve.wait_ge(setup_copy, 8)
                dve.wait_ge(setup_mm, 5)
                dve.wait_ge(small_loaded, 16 * NSMALL[0])
                for h in range(GB):
                    c = slice(h * CHUNK, (h + 1) * CHUNK)
                    step(dve.tensor_tensor(biasA[:, c], Q[0][:, 0:CHUNK], mask[:, c], ALU.add))
                step(dve.tensor_scalar(whalf[:, 0, :], vec[:, 0:V_U], 0.5, None, ALU.mult))
                step(dve.tensor_scalar(whalf[:, 1, :], vswap[:], 0.5, None, ALU.mult))
                step(dve.scalar_tensor_tensor(padv[:, 2:3], padv[:, 0:1], 1.0, col(V_BASE), ALU.add, ALU.mult))
                step(dve.scalar_tensor_tensor(padv[:, 3:4], padv[:, 1:2], 1.0, vswap[:, V_BASE:V_BASE + 1], ALU.add, ALU.mult))
                step(dve.scalar_tensor_tensor(vB[:, 0, :], vtB[:, 1, :], 1.0, vtB[:, 0, :], ALU.add, ALU.mult))
                step(dve.tensor_copy(vB[:, 1, :], vB[:, 0, :]))
                pad = slice(GT, TABLE)
                step(dve.tensor_scalar(padc[:, 0, :], cos[:, pad], padv[:, 2:3], None, ALU.mult))
                step(dve.tensor_scalar(padc[:, 1, :], sin[:, pad], padv[:, 3:4], None, ALU.mult))
                for i, (name, wc, bc) in enumerate(HEADS):
                    step(dve.tensor_scalar(ctab[:, i, :], cos, col(bc), None, ALU.mult))
                    step(dve.scalar_tensor_tensor(ctab[:, i, :], sin, vswap[:, bc:bc + 1], ctab[:, i, :], ALU.mult, ALU.add))
                    if name in ("lk", "qk"):
                        step(dve.scalar_tensor_tensor(padc[:, 2, :], padc[:, 0, :], whalf[:, 0, wc:wc + 1], ctab[:, i, pad],
                                                      ALU.mult, ALU.add))
                        step(dve.scalar_tensor_tensor(padc[:, 3, :], padc[:, 1, :], whalf[:, 1, wc:wc + 1], padc[:, 2, :],
                                                      ALU.mult, ALU.add))
                        for b in range(GB):
                            step(dve.tensor_copy(qT[name][:, b, TW:PADDED], padc[:, 3, :]))

            w2_now = [0]

            def tok(g, s):
                first = isinstance(g, int) and g == 0
                if first and s >= 2 and w2_now[0] < MS:
                    n = w2_now[0]
                    w2_now[0] += 1
                    dve.wait_ge(w2_hi, n + 1)
                    for k in (2 * n, 2 * n + 1):
                        ins = dve.scalar_tensor_tensor(w2l[:, k], stage2m[:, k], SCALE, w2h[:, k], ALU.mult, ALU.subtract)
                    ins.then_inc(w2_split, 1)
                if first and s == KH + 1:
                    setup()
                if s < KH:
                    dve.wait_ge(hid_hi, g * KH + s + 1)
                    dve.scalar_tensor_tensor(hidl[:, s, :], T[s % 3][:, 0:GT], 0.0, hidh[:, s, :], ALU.max, ALU.subtract)\
                        .then_inc(hid_lo, 1)
                    return
                m = s - KH
                base = g * MIX_STEPS + mix_after(m - 1)

                def done(ins):
                    return ins.then_inc(mix_step, 1)

                dve.wait_ge(mix_exp, g * MS + m + 1)
                if m == 0:
                    dve.wait_ge(xu_done, g + 1)
                    dve.tensor_copy(den[:], mexp[:, 0, :])
                    done(dve.tensor_tensor(num[:], mexp[:, 0, :], xu32[:, 0, :], ALU.mult))
                else:
                    dve.wait_ge(mix_step, base)
                    done(dve.tensor_tensor(prod[:], mexp[:, m % 2, :], xu32[:, m, :], ALU.mult))
                    done(dve.tensor_tensor(den[:], den[:], mexp[:, m % 2, :], ALU.add))
                    dve.wait_ge(mix_step, base + 1)
                    done(dve.tensor_tensor(num[:], num[:], prod[:], ALU.add))
                if m == MS - 1:
                    dve.wait_ge(mix_step, base + 3)
                    done(dve.reciprocal(den[:], den[:]))
                    dve.wait_ge(mix_step, base + 4)
                    dve.tensor_tensor(pooled[:], num[:], den[:], ALU.mult).then_inc(pooled_done, 1)
                if not (isinstance(g, int) and g == GROUPS - 1):
                    split_x(g + 1, m)

            LN_STEPS = 5

            def stats(a_, src, n, signal):
                for k in range(TPG):
                    ins = dve.bn_stats(st6[:, k, :], src(k))
                ins.then_inc(ln_step, 1)
                dve.wait_ge(ln_step, a_ * LN_STEPS + (2, 4, 5)[n])
                dve.sem_inc(dve_passed, 1)
                for k in range(TPG):
                    ins = dve.bn_aggr(mv[:, n, k, :], st6[:, k, :])
                ins.then_inc(signal, 1)

            def bc(t):
                return t[:].unsqueeze(1).broadcast_to([TT, TPG, 128])

            def last(s):
                if s == 5:
                    dve.wait_ge(sw_hi, 1)
                    dve.tensor_tensor(sw1l, sw_stage[:, 0, :], sw1h, ALU.subtract)
                    dve.tensor_tensor(sw[:, 3, :], sw_stage[:, 1, :], sw[:, 2, :], ALU.subtract).then_inc(sw_split, 1)
                    dve.wait_ge(rc_loaded, 16)
                    dve.wait_ge(ones_done, 4)
                    rl = slice(LO_ROW, LO_ROW + EXPERTS)
                    dve.tensor_copy(b2t[rl, :], b2st[rl, :])
                    dve.tensor_copy(b2t[0:EXPERTS, :], b2st[0:EXPERTS, :]).then_inc(b2_step, 1)
                    dve.tensor_copy(same16[:], rc[:, RCOLUMNS["same_expert"]])
                    dve.tensor_copy(before16[:], rc[0:TT, RCOLUMNS["before"]])
                    dve.tensor_copy(pickb[:], rc[:, RCOLUMNS["pick_b2"]])
                    dve.wait_ge(b2_step, 1)
                    dve.tensor_copy(b2hl[0:EXPERTS, :], b2t[0:EXPERTS, :])
                    dve.tensor_tensor(b2hl[rl, :], b2st[rl, :], b2t[rl, :], ALU.subtract).then_inc(rc_ready, 1)
                c = s - 5
                if 0 <= c < 2 * EXPERTS // EC:
                    dve.wait_ge(ew_hi, c + 1)
                    dve.tensor_tensor(chunk(1, c), estage[c % 2], chunk(0, c), ALU.subtract).then_inc(ew_split, 1)

            def attn(a_, s):
                if isinstance(a_, int) and a_ == GROUPS - 1:
                    last(s)
                if s == 0:
                    dve.wait_ge(fc_mm, a_ + 1)
                    dve.tensor_tensor(z[:], X[0:TT, 0:GT + 84].rearrange("p (k n) -> p k n", k=TPG), bc(fcb_bc), ALU.add)\
                        .then_inc(ln_step, 1)
                    dve.wait_ge(ln_step, a_ * LN_STEPS + 1)
                    stats(a_, lambda k: z[:, k, :], 0, ln1_stats)
                if s == 1:
                    dve.wait_ge(ln1_stats, a_ + 1)
                    dve.wait_ge(ln1_rstd, a_ + 1)
                    for k in range(TPG):
                        ins = dve.tensor_scalar(xn[:, k, :], z[:, k, :], mv[:, 0, k, 0:1], pst[:, 1, k:k + 1], ALU.subtract, ALU.mult)
                    ins.then_inc(ln_step, 1)
                    dve.wait_ge(ln_step, a_ * LN_STEPS + 3)
                    dve.tensor_tensor(z[:], xn[:], bc(lng_bc), ALU.mult).then_inc(rot_step, 1)
                    dve.wait_ge(rot_step, a_ * ROT_STEPS + 1)
                    dve.tensor_tensor(h1[:], z[:], bc(lnb_bc), ALU.add).then_inc(h1_done, 1)
                    dve.wait_ge(h1_done, a_ + 1)
                    stats(a_, lambda k: h1[:, k, :], 1, ln2_stats)
                if s == 2:
                    dve.wait_ge(ln2_stats, a_ + 1)
                    dve.wait_ge(ln2_r, a_ + 1)
                    for k in range(TPG):
                        ins = dve.tensor_scalar(z[:, k, :], h1[:, k, :], mv[:, 1, k, 0:1], pst[:, 6, k:k + 1], ALU.subtract, ALU.mult)
                    ins.then_inc(rot_step, 1)
                    dve.wait_ge(rot_step, a_ * ROT_STEPS + 2)
                    dve.tensor_scalar(xn[:], z[:], scala[:, 0:1], None, ALU.mult).then_inc(xn_done, 1)
                if s == 4:
                    for i in range(2):
                        dve.wait_ge(proj_z, a_ * 4 + i + 1)
                        ins = dve.scalar_tensor_tensor(base2[:, i, :], ptanh[:, i, :], 1.0, pz[:, i, :], ALU.add, ALU.mult)
                        ins.then_inc(base_done, 1)
                    dve.wait_ge(base_done, a_ * 2 + 2)
                    dve.tensor_tensor(rot[:, 0, :], base2[:, 0, :], cos[:, 0:GT], ALU.mult)
                    dve.tensor_tensor(rot[:, 1, :], base2[:, 1, :], sin[:, 0:GT], ALU.mult).then_inc(rot_step, 1)
                    dve.wait_ge(rot_step, a_ * ROT_STEPS + 3)
                    for i, (name, wc, _) in enumerate(HEADS):
                        dve.scalar_tensor_tensor(htmp[:, i % 2, :], rot[:, 0, :], whalf[:, 0, wc:wc + 1], ctab[:, i, 0:GT],
                                                 ALU.mult, ALU.add).then_inc(rot_step, 1)
                        dve.wait_ge(rot_step, a_ * ROT_STEPS + 4 + i)
                        dve.scalar_tensor_tensor(qT[name][:, :, 0:TW], rot[:, 1, :].rearrange("p (b n) -> p b n", b=GB),
                                                 whalf[:, 1, wc:wc + 1], htmp[:, i % 2, :].rearrange("p (b n) -> p b n", b=GB),
                                                 ALU.mult, ALU.add).then_inc(head_done, 1)
                if s == 5:
                    for i in range(2):
                        dve.wait_ge(proj_z, a_ * 4 + i + 3)
                        dve.scalar_tensor_tensor(u2[:, i, :], ptanh[:, i, :], 1.0, pz[:, 2 + i, :], ALU.add, ALU.mult)\
                            .then_inc(u_done, 1)
                if s == 6:
                    dve.wait_ge(v_tanh, a_ * 2 + 1)
                    dve.scalar_tensor_tensor(vA[:], vtA[:], 1.0, Q[1][:].rearrange("p (b n) -> p b n", b=GB), ALU.add, ALU.mult)\
                        .then_inc(v_done, 1)
                    dve.wait_ge(v_tanh, a_ * 2 + 2)
                    dve.scalar_tensor_tensor(vB[0:B_TOK], vtB[0:B_TOK], 1.0, Q[2][0:B_TOK, :].rearrange("p (b n) -> p b n", b=GB),
                                             ALU.add, ALU.mult).then_inc(v_done, 1)
                if s == 7:
                    dve.wait_ge(qk_mm, a_ + 1)
                    n = GB * A_TOK
                    dve.scalar_tensor_tensor(sA[:], Q[0][:, 0:n].rearrange("p (b n) -> p b n", b=GB), 1.0 / CHUNK,
                                             biasA[:].unsqueeze(1).broadcast_to([128, GB, A_TOK]), ALU.mult, ALU.add)
                    dve.scalar_tensor_tensor(sB[:], Q[0][0:CHUNK, n:n + GB * B_TOK].rearrange("p (b n) -> p b n", b=GB), 1.0 / CHUNK,
                                             biasA[0:CHUNK, 0:B_TOK].unsqueeze(1).broadcast_to([CHUNK, GB, B_TOK]),
                                             ALU.mult, ALU.add).then_inc(score_done, 1)
                    dve.wait_ge(score_done, a_ + 1)
                    dve.scalar_tensor_tensor(kA[:], sA[:], 0.0, sA[:], ALU.max, ALU.mult)
                    dve.scalar_tensor_tensor(kB[:], sB[:], 0.0, sB[:], ALU.max, ALU.mult).then_inc(kern_done, 1)
                if s == 9:
                    dve.wait_ge(ot_mm, a_ + 1)
                    dve.wait_ge(u_done, a_ * 2 + 2)
                    for i in range(2):
                        ins = dve.scalar_tensor_tensor(gT[:, i, :], Q[2 + i][:, 0:GT], 0.25, u2[:, i, :], ALU.mult, ALU.mult)
                    ins.then_inc(g_done, 1)
                if s == 10:
                    dve.wait_ge(out_mm, a_ + 1)
                    dve.wait_ge(h1ob_done, a_ + 1)
                    dve.tensor_tensor(h2[:], Q[0][0:TT, 0:TPG * 128].rearrange("p (k n) -> p k n", k=TPG), h1ob[:], ALU.add)\
                        .then_inc(h2_done, 1)
                    dve.wait_ge(h2_done, a_ + 1)
                    stats(a_, lambda k: h2[:, k, :], 2, ln3_stats)
                if s == 11:
                    dve.wait_ge(ln3_stats, a_ + 1)
                    dve.wait_ge(ln3_rstd, a_ + 1)
                    dve.wait_ge(rows_stored, 16 * (a_ + 1))
                    for k in range(TPG):
                        ins = dve.tensor_scalar(rows[:, k, 0:C], h2[:, k, :],
                                                mv[:, 2, k, 0:1], pst[:, 7, k:k + 1], ALU.subtract, ALU.mult)
                    ins.then_inc(n2_done, 1)
                if s == 12:
                    dve.wait_ge(n2T_copied, a_ + 1)
                    dve.tensor_copy(n2h[:, bass.ds(a_ * GT, GT)], n2T[:]).then_inc(n2h_done, 1)
                    dve.wait_ge(n2h_done, a_ + 1)
                    dve.tensor_tensor(n2l[:, bass.ds(a_ * GT, GT)], n2T[:], n2h[:, bass.ds(a_ * GT, GT)], ALU.subtract)\
                        .then_inc(n2_split, 1)
                if s == 13:
                    dve.wait_ge(gate_mm, a_ + 1)
                    q2 = Q[2][0:TT, 0:TPG * EXPERTS].rearrange("p (k n) -> p k n", k=TPG)

                    def over(t):
                        return t[:].unsqueeze(2).broadcast_to([TT, TPG, EXPERTS])

                    dve.tensor_reduce(lmax[:], q2, AX_X, ALU.max).then_inc(lmax_done, 1)
                    dve.wait_ge(lmax_done, a_ + 1)
                    dve.tensor_tensor(lg[:], q2, over(lmax), ALU.subtract).then_inc(lg_done, 1)
                    dve.wait_ge(lexp_done, a_ + 1)
                    dve.tensor_reduce(psum_[:], pexp[:], AX_X, ALU.add).then_inc(gsum_done, 1)
                    dve.wait_ge(gsum_done, a_ + 1)
                    dve.reciprocal(prcp[:], psum_[:]).then_inc(grcp_done, 1)
                    dve.wait_ge(grcp_done, a_ + 1)
                    dve.tensor_tensor(rows[:, :, C:ROW], pexp[:], over(prcp), ALU.mult)
                    dve.tensor_tensor(probs[:, bass.ds(a_ * TPG, TPG), :], pexp[:], over(prcp), ALU.mult)\
                        .then_inc(probs_done, 1)

            ROT_STEPS = 7
            dve.sem_inc(rows_stored, 16)
            dve.sem_inc(h2_stored, 16)
            schedule(dve, tok, attn)

            dve.wait_ge(pm_mm, 1)
            dve.memset(cur[:], 0)
            dve.tensor_copy(pe_major, T[0][:, 0:GT]).then_inc(cur_ready, 1)
            dve.wait_ge(cur_ready, 1)
            bits, values = rc[:, RCOLUMNS["bit"]].bitcast(U32), rc[:, RCOLUMNS["bit_value"]]
            dve.tensor_scalar(cand[:], cur[:], bits[:, 0:1], None, ALU.bitwise_or).then_inc(cand_ready, 1)
            dve.sem_inc(fin_done, 1)
            with dve.Fori(0, GROUPS) as i:
                for q in range(4):
                    n = i * 4 + q
                    dve.wait_ge(cand_ready, n + 1)
                    dve.tensor_scalar(hits, pe_major, cand[:].bitcast(F32), None, ALU.is_ge, ALU.add, accum_out=cnt[:])\
                        .then_inc(hits_done, 1)
                    dve.wait_ge(count_mm, n + 1)
                    dve.tensor_scalar(bitv[:], T[1][:, 0:1], CAP - 0.5, values[:, bass.ds(n, 1)], ALU.is_ge, ALU.mult)\
                        .then_inc(bitv_done, 1)
                    dve.wait_ge(bitv_done, n + 1)
                    dve.scalar_tensor_tensor(cand[:], bitv[:], bits[:, bass.ds(n + 1, 1)], cur[:], ALU.bitwise_or, ALU.bitwise_or)\
                        .then_inc(cand_ready, 1)
                    dve.tensor_tensor(cur[:], cur[:], bitv[:], ALU.bitwise_or).then_inc(cur_ready, 1)
                dve.wait_ge(sh2_mm, i + 2)
                dve.wait_ge(h2b_loaded, 16 * (i + 1))
                dve.tensor_tensor(fin, X[0:TT, 0:TPG * 128].rearrange("p (k n) -> p k n", k=TPG), h2b, ALU.add)\
                    .then_inc(fin_done, 1)
                dve.wait_ge(fin_done, i + 2)
                dve.wait_ge(out_stored, 16 * (i + 1))
            dve.wait_ge(cur_ready, 1 + STEPS_R)
            dve.tensor_copy(thr_wide, cur[:].bitcast(F32).broadcast_to([128, TT])).then_inc(thr_wide_done, 1)
            dve.wait_ge(thr_mm, 1)
            dve.tensor_copy(thr, T[2][0:TT, 0:EXPERTS]).then_inc(thr_done, 1)
            dve.wait_ge(thr_done, 1)
            wide = thr.unsqueeze(2).broadcast_to([TT, EXPERTS, TILES])
            by_e = probs[:].rearrange("p k e -> p e k")
            dve.tensor_tensor(over16, by_e, wide, ALU.is_gt)
            dve.tensor_tensor(tie16, by_e, wide, ALU.is_equal).then_inc(masks_done, 1)
            dve.wait_ge(masks_done, 1)
            flat = lambda v: v.rearrange("p e t -> p (e t)")
            fresh = rc[0:TT, RCOLUMNS["not_first"]]
            for src, dst in ((over16, over_c), (tie16, tie_c)):
                dve.tensor_tensor_scan(flat(dst), fresh, flat(src), 0.0, ALU.mult, ALU.add).then_inc(scans_done, 1)
            FAR = 1024.0
            dve.wait_ge(prefix_mm, 1)
            dve.scalar_tensor_tensor(flat(pos1), T[0][0:TT, 0:ET], FAR, flat(over16), ALU.subtract, ALU.mult)
            dve.scalar_tensor_tensor(flat(pos2), T[1][0:TT, 0:ET], FAR, flat(tie16), ALU.subtract, ALU.mult).then_inc(pos_done, 1)
            dve.wait_ge(pos_done, 1)
            dve.scalar_tensor_tensor(flat(pos_i), flat(pos1), FAR, flat(pos2), ALU.add, ALU.add).then_inc(pos_done, 1)
            dve.wait_ge(pos_done, 2)
            dve.tensor_scalar(flat(dig_ai), flat(pos_i), 4, None, ALU.arith_shift_right)
            dve.tensor_scalar(flat(dig_bi), flat(pos_i), DIG_B - 1, None, ALU.bitwise_and).then_inc(digits_done, 1)
            dve.wait_ge(digits_done, 1)
            dve.tensor_copy(flat(dig_a), flat(dig_ai))
            dve.tensor_copy(flat(dig_b), flat(dig_bi)).then_inc(digits_done, 1)
            dve.wait_ge(digits_done, 2)
            for k in range(DIG_A):
                ins = dve.tensor_scalar(hotA[:, :, k], flat(dig_a).rearrange("p (h n) -> p h n", h=2), float(k), None, ALU.is_equal)
            ins.then_inc(digits_done, 1)
            for k in range(DIG_B):
                dve.tensor_scalar(flat(hotB[:, k]), flat(dig_b), float(k), None, ALU.is_equal)
                dve.tensor_scalar(flat(hotBp[:, k]), flat(dig_b), float(k), rc[0:TT, RCOLUMNS["partition"]], ALU.is_equal, ALU.mult)
            dve.wait_ge(digits_done, 3)
            first = rc[0:TT, RCOLUMNS["tile_first"]][:, 0:HALF_E * TILES].unsqueeze(1).broadcast_to([TT, DIG_A, HALF_E * TILES])
            for h in range(2):
                ins = dve.tensor_tensor(hotAt[:, h], hotA[:, h], first, ALU.mult)
            ins.then_inc(hot_done, 1)
            dve.wait_ge(lists_mm, 1)
            na = DIG_A * HALF_E
            for h in range(2):
                ins = dve.tensor_tensor(picked[:, h, :], Q[h][0:na, 0:DIG_B * HALF_E], rc[0:na, RCOLUMNS["diagonal"]], ALU.mult)
            ins.then_inc(picked_done, 1)
            dve.wait_ge(picked_done, 1)
            dve.tensor_reduce(lists_f, picked.rearrange("p h (b e) -> p h b e", b=DIG_B), AX_X, ALU.add).then_inc(lists_done, 1)
            dve.wait_ge(idx_mm, 1)
            dve.tensor_copy(idx[:], T[2][0:HC, 0:2 * EXPERTS]).then_inc(idx_done, 1)
            dve.wait_ge(idx_done, 1)

            def indices(tile_, e):
                return dve.tensor_copy(tile_[:].rearrange("p (h a) -> p h a", h=2),
                                       idx[:].rearrange("p (h e) -> p h e", h=2)[:, :, bass.ds(e, 1)])

            def copy_gather(e, q):
                indices(gidx[q], e).then_inc(gidx_copied, 1)

            dve.sem_inc(eh_split, 1)
            copy_gather(0, 0)

            def step(k, q):
                if not isinstance(k, int) or k + 1 < EXPERTS:
                    copy_gather(k + 1, (q + 1) % RING)
                if not isinstance(k, int) or k < EXPERTS:
                    if past(k, RING):
                        dve.wait_ge(added, k - RING + 2)
                        dve.sem_inc(dve_passed, 1)
                    indices(sidx[q], k).then_inc(sidx_copied, 1)
                    dve.wait_ge(eX_mm, k + 1)
                    src = T[q % 2][:, 0:CAP]
                    dve.tensor_copy(eXh[:, q, :], src).then_inc(eX_hi, 1)
                    dve.tensor_copy(score[:, q, :].unsqueeze(2), gath[q][:, :, bass.ds(C + k, 1)])
                    dve.wait_ge(eX_hi, k + 1)
                    dve.tensor_tensor(eXl[:, q, :], src, eXh[:, q, :], ALU.subtract).then_inc(eX_split, 1)
                if not isinstance(k, int) or 1 <= k <= EXPERTS:
                    e, r2 = k - 1, (q + 1) % 2
                    dve.wait_ge(eh_gelu, e + 1)
                    dve.tensor_copy(ehh[:, r2, :], eh32[:, r2, :]).then_inc(eh_hi, 1)
                    dve.wait_ge(eh_hi, e + 1)
                    dve.tensor_tensor(ehl[:, r2, :], eh32[:, r2, :], ehh[:, r2, :], ALU.subtract).then_inc(eh_split, 1)
                if past(k, 2):
                    e, r2, slot = k - 2, q % 2, (q + 2) % RING
                    dve.wait_ge(ey_mm, e + 1)
                    for h in range(2):
                        ins = dve.tensor_scalar(ey[slot][:, h, :], (T[2], X)[r2][0:HC, h * 128:(h + 1) * 128],
                                                score[:, slot, h:h + 1], None, ALU.mult)
                    ins.then_inc(ey_scaled, 1)

            expert_steps(dve, step)


_IN = ["x", "L0_tok_w1", "L0_tok_w2", "L0_tok_fc_w", "L0_tok_fc_b", "L0_tok_ln_g", "L0_tok_ln_b", "L0_attn_scala",
       "L0_attn_u_w", "L0_attn_u_b", "L0_attn_v_w", "L0_attn_v_b", "L0_attn_base_w", "L0_attn_base_b", "L0_attn_qq_w",
       "L0_attn_qq_b", "L0_attn_qk_w", "L0_attn_qk_b", "L0_attn_lq_w", "L0_attn_lq_b", "L0_attn_lk_w", "L0_attn_lk_b",
       "L0_attn_o_w", "L0_attn_o_b", "L0_attn_w", "L0_ffn_gate_w", "L0_ffn_w1", "L0_ffn_b1", "L0_ffn_w2", "L0_ffn_b2",
       "L0_ffn_sw1", "L0_ffn_sb1", "L0_ffn_sw2", "L0_ffn_sb2"]


def kernel(**inputs):
    import concourse.bacc as bacc
    from concourse.bass_utils import run_bass_kernel_spmd

    nc = bacc.Bacc("TRN2", target_bir_lowering=False, num_devices=1)
    arrays = {n: np.ascontiguousarray(inputs[n]) for n in _IN}
    arrays["constants"] = constant_table()
    arrays["routing"] = routing_table()
    aps = {n: nc.dram_tensor(f"in_{n}", v.shape, mybir.dt.from_np(v.dtype), kind="ExternalInput").ap() for n, v in arrays.items()}
    out = nc.dram_tensor("out_h", (TOKENS, C), F32, kind="ExternalOutput").ap()
    build(nc, aps, out)
    r = run_bass_kernel_spmd(nc, [{f"in_{n}": v for n, v in arrays.items()}], core_ids=[0])
    return r.results[0]["out_h"].reshape(BATCH, TW, C)
```

```python
from contextlib import ExitStack

import numpy as np

import concourse.bass as bass
from concourse import mybir

F32 = mybir.dt.float32
F16 = mybir.dt.float16
U32 = mybir.dt.uint32
I32 = mybir.dt.int32
ALU = mybir.AluOpType
ACT = mybir.ActivationFunctionType
AX_X = mybir.AxisListType.X

BATCH, STEPS, C = 16, 750, 128
MS = 5
TW = STEPS // MS
TOKENS = BATCH * TW
HID = 2 * C * MS
KH = HID // 128
E = 2 * C
CHUNK = 64
PADDED = 3 * CHUNK
A_TOK = 2 * CHUNK
B_TOK = TW - A_TOK
PAD_TOK = PADDED - TW
MAXPOS = 128
GB = 2
GT = GB * TW
GROUPS = BATCH // GB
TT = 100
TPG = GT // TT
TILES = TOKENS // TT
EXPERTS, FF = 16, 512
KF = FF // 128
CAP = TOKENS // EXPERTS
ROW = C + EXPERTS
EPS = 1e-5
OFF_BLOCK = -1e30

SCALE = 16.0

TABLE = GT + PAD_TOK
COLUMNS = {}
_at = 0
for _name, _width in (("ident", 128), ("swap", 128), ("anti", CHUNK), ("mask", A_TOK), ("cos", TABLE), ("sin", TABLE)):
    COLUMNS[_name] = slice(_at, _at + _width)
    _at += _width
N_COLUMNS = _at
DIG_A, DIG_B = 10, 16
LIST = DIG_A * DIG_B
HALF_E = EXPERTS // 2
HC = CAP // 2
HALF_BITS = 15
SEARCH = 16
RCOLUMNS = {}
_at = 0
for _name, _width in (("same_expert", 128), ("before", TT), ("enough", 128), ("token", TILES),
                      ("not_first", EXPERTS * TILES), ("diagonal", 128), ("bounds", 4 * SEARCH), ("pick_b2", EXPERTS)):
    RCOLUMNS[_name] = slice(_at, _at + _width)
    _at += _width
N_RCOLUMNS = _at
LO_ROW = 32


RING = 4
REGION = 13044


def routing_table():
    t = np.zeros((128, N_RCOLUMNS), np.float32)
    p = np.arange(128)
    t[:, RCOLUMNS["same_expert"]] = 4 * (p[:, None] % EXPERTS == p[None, :] % EXPERTS)
    t[0, RCOLUMNS["enough"]] = -4 * (CAP - 0.5)
    t[:, RCOLUMNS["before"]] = p[:, None] < np.arange(TT)[None, :]
    t[:, RCOLUMNS["token"]] = np.arange(TILES) * TT + p[:, None] - TOKENS // 2
    t[:, RCOLUMNS["not_first"]] = np.tile(np.arange(TILES), EXPERTS) > 0
    t[:, RCOLUMNS["diagonal"]] = p[:, None] // DIG_A == p[None, :] % HALF_E
    half = 0.5 ** (np.arange(SEARCH) + 2.0)
    down, up = -half, half.copy()
    down[HALF_BITS - 1], up[HALF_BITS - 1] = -0.5 ** HALF_BITS, 0
    down[HALF_BITS], up[HALF_BITS] = 0, 0
    t[:, RCOLUMNS["bounds"]] = np.tile(np.stack([down, up], axis=1).reshape(-1), 2)
    e = np.arange(EXPERTS)
    t[:, RCOLUMNS["pick_b2"]] = (p[:, None] == e[None, :]) | (p[:, None] == LO_ROW + e[None, :])
    return t


def constant_table():
    t = np.zeros((128, N_COLUMNS), np.float32)
    p = np.arange(128)
    t[p, COLUMNS["ident"].start + p] = 1
    t[p, COLUMNS["swap"].start + (p + 64) % 128] = 1
    q = np.arange(CHUNK)
    t[q, COLUMNS["anti"].start + CHUNK - 1 - q] = 1
    t[:, COLUMNS["mask"]] = np.where(p[:, None] // CHUNK == p[None, :] // CHUNK, 0, OFF_BLOCK)
    half = C // 2
    inv_freq = (10000.0 ** (-np.arange(half, dtype=np.float32) / half)).astype(np.float32)
    pos = np.concatenate([np.arange(TW)] * GB + [np.arange(TW, PADDED)]).astype(np.float32)
    angle = (pos[None, :] * inv_freq[:, None]).astype(np.float32)
    t[:half, COLUMNS["cos"]] = t[half:, COLUMNS["cos"]] = np.cos(angle)
    t[:half, COLUMNS["sin"]] = -np.sin(angle)
    t[half:, COLUMNS["sin"]] = np.sin(angle)
    return t


V_QQW, V_QQB, V_QKW, V_QKB, V_LQW, V_LQB, V_LKW, V_LKB, V_BASE = range(9)
V_U = 9
V_SB1 = V_U + 2
V_B1 = V_SB1 + KF
N_VEC = V_B1 + EXPERTS * KF
HEADS = (("lk", V_LKW, V_LKB), ("qk", V_QKW, V_QKB), ("qq", V_QQW, V_QQB), ("lq", V_LQW, V_LQB))


def build(nc, a, out):
    x = a["x"]
    with ExitStack() as ctx:
        def sb(name, shape, dt=F32):
            return ctx.enter_context(nc.sbuf_tensor(name, shape, dt))

        def bank(name):
            return ctx.enter_context(nc.psum_tensor(name, [128, 512], F32))

        def sem(name):
            return ctx.enter_context(nc.semaphore(name))

        const = sb("const", [128, N_COLUMNS])
        ident, swap_m, mask = (const[:, COLUMNS[n]] for n in ("ident", "swap", "mask"))
        anti = const[0:CHUNK, COLUMNS["anti"]]
        cos, sin = const[:, COLUMNS["cos"]], const[:, COLUMNS["sin"]]

        arena = sb("arena", [128, 4 * MS * HID + 2 * MS * HID], F16)
        part = MS * HID
        w1h = arena[:, 0:part].rearrange("p (m n) -> p m n", m=MS)
        w1l = arena[:, part:2 * part].rearrange("p (m n) -> p m n", m=MS)
        w2h = arena[:, 2 * part:3 * part].rearrange("p (k m c) -> p k m c", k=KH, m=MS)
        w2l = arena[:, 3 * part:4 * part].rearrange("p (k m c) -> p k m c", k=KH, m=MS)
        stage = arena[:, 4 * part:6 * part].bitcast(F32)
        W1_COLS = HID // MS
        stage1 = stage.rearrange("p (i m n) -> p i m n", i=MS, m=MS)
        stage2 = stage.rearrange("p (k n) -> p k n", k=KH)
        stage2m = stage.rearrange("p (k c m) -> p k m c", k=KH, m=MS)

        wT = sb("wT", [128, 8, 128])
        uT_w, vT_w, baseT_w, swapT_w, oT_w = wT[:, 0:2, :], wT[:, 2:4, :], wT[:, 4, :], wT[:, 5, :], wT[:, 6:8, :]
        fc_w = sb("fc_w", [128, 128])
        gate_w = sb("gate_w", [128, EXPERTS])
        vec = sb("vec", [128, N_VEC])
        vswap = sb("vswap", [128, V_U])
        whalf = sb("whalf", [128, 2, V_U])
        fcb_bc, lng_bc, lnb_bc, ob_bc = (sb(n, [TT, 128]) for n in ("fcb_bc", "lng_bc", "lnb_bc", "ob_bc"))
        scala = sb("scala", [TT, 1])
        vb16 = sb("vb16", [LO_ROW + 1, E], F16)
        sb2_bc = sb("sb2_bc", [TT, 128])
        mhalf = sb("mhalf", [TT, TPG])
        zw = sb("zw", [CHUNK, A_TOK])
        biasA = sb("biasA", [128, A_TOK])
        halfb = sb("halfb", [128, 4])
        padc = sb("padc", [128, 4, PAD_TOK])
        padv = sb("padv", [128, 4])

        xbuf = sb("xbuf", [128, TPG * MS * C])
        x_tok = xbuf[0:TT, :].rearrange("p (k n) -> p k n", k=TPG)
        xp_xu = sb("xp_xu", [128, 2 * MS * GT])
        xp32, xu32 = (xp_xu[:, k * MS * GT:(k + 1) * MS * GT].rearrange("p (m n) -> p m n", m=MS) for k in (0, 1))
        xh = sb("xh", [128, MS, GT], F16)
        xl = sb("xl", [128, MS, GT], F16)
        hid = sb("hid", [128, 2, KH * GT], F16)
        hidh, hidl = (hid[:, k, :].rearrange("p (k n) -> p k n", k=KH) for k in (0, 1))
        mte = sb("mte", [128, 4, GT])
        mtanh, mexp = mte[:, 0:2, :], mte[:, 2:4, :]
        den, num, prod = (sb(n, [128, GT]) for n in ("den", "num", "prod"))
        pooled = sb("pooled", [128, GT])

        region = sb("region", [128, REGION])

        def carver():
            at = [0]

            def carve(shape, dt=F32):
                n = int(np.prod(shape[1:]))
                words = n if dt != F16 else (n + 1) // 2
                v = region[:, at[0]:at[0] + words]
                at[0] += words
                assert at[0] <= REGION, at[0]
                if dt != F32:
                    v = v.bitcast(dt)
                v = v[0:shape[0], 0:n]
                if len(shape) == 3:
                    v = v.rearrange("p (a n) -> p a n", a=shape[1])
                if len(shape) == 4:
                    v = v.rearrange("p (a b n) -> p a b n", a=shape[1], b=shape[2])
                return v
            return carve

        carve = carver()
        z = carve([TT, TPG, 128])
        h1 = carve([TT, TPG, 128])
        xn = carve([TT, TPG, 128])
        h1ob = carve([TT, TPG, 128])
        st6 = sb("st6", [TT, TPG, 6])
        mv = sb("mv", [TT, 3, TPG, 2])
        pst = sb("pst", [TT, 8, TPG])
        xnT = carve([128, GT])
        ptanh = carve([128, 2, GT])
        pz = carve([128, 4, GT])
        wst = pz.rearrange("p a n -> p (a n)")[:, 0:1024].rearrange("p (k n) -> p k n", k=8)
        vrows = pz.rearrange("p a n -> p (a n)")[0:N_VEC, 1024:1152]
        base2 = carve([128, 2, GT])
        u2 = carve([128, 2, GT])
        rot = carve([128, 2, GT])
        htmp = carve([128, 2, GT])
        qT = {n: carve([128, GB, PADDED]) for n in ("lk", "qk")}
        for n in ("qq", "lq"):
            qT[n] = carve([128, GB, TW])
        vtA = carve([128, GB, E])
        vtB = carve([CHUNK, GB, E])
        vA = carve([128, GB, E])
        vB = carve([CHUNK, GB, E])
        lkA = carve([128, GB, 128])
        lkB = carve([CHUNK, GB, 128])
        linkv = carve([128, GB, E])
        vb_row, vb_high = linkv[0:LO_ROW + 1, 0, :], linkv[0:LO_ROW + 1, 1, :].bitcast(F16)[:, 0:E]
        sA = carve([128, GB, A_TOK])
        sB = carve([CHUNK, GB, B_TOK])
        kA = carve([128, GB, A_TOK])
        kB = carve([CHUNK, GB, B_TOK])
        gT = carve([128, 2, GT])
        ctab = carve([128, 4, TABLE])
        h2 = sb("h2", [TT, TPG, 128])
        h2s = sb("h2s", [TT, TPG, 128])
        rows = sb("rows", [TT, TPG, ROW])
        n2T = sb("n2T", [128, GT])
        n2hl = sb("n2hl", [128, 2, TOKENS], F16)
        n2h, n2l = n2hl[:, 0, :], n2hl[:, 1, :]
        lmax = sb("lmax", [TT, TPG])
        lg = sb("lg", [TT, TPG, EXPERTS])
        pexp = sb("pexp", [TT, TPG, EXPERTS])
        psum_ = sb("psum_", [TT, TPG])
        prcp = sb("prcp", [TT, TPG])
        probs = sb("probs", [TT, TILES, EXPERTS])

        ew = EXPERTS * FF
        EC = 4

        def chunk(lo, c):
            at_ = (2 * (c // (EXPERTS // EC)) + lo) * ew + c % (EXPERTS // EC) * EC * FF
            return arena[:, at_:at_ + EC * FF]

        e1h, e1l = (arena[:, k * ew:(k + 1) * ew].rearrange("p (e n) -> p e n", e=EXPERTS) for k in (0, 1))
        e2h, e2l = (arena[:, k * ew:(k + 1) * ew].rearrange("p (e j n) -> p e j n", e=EXPERTS, j=KF) for k in (2, 3))
        estage = [arena[:, 4 * ew:4 * ew + 2 * EC * FF].bitcast(F32), xp_xu[:, 0:EC * FF]]
        sw_stage = hid[:, 0, :].bitcast(F32)[:, 0:2 * FF].rearrange("p (a n) -> p a n", a=2)
        sw = mte[:].rearrange("p a n -> p (a n)").bitcast(F16)[:, 0:4 * FF].rearrange("p (a n) -> p a n", a=4)
        sw1h, sw1l = sw[:, 0, :], sw[:, 1, :]
        sw2h, sw2l = (sw[:, k, :].rearrange("p (j n) -> p j n", j=KF) for k in (2, 3))
        shh, shl = (hid[:, 1, k * KF * GT:(k + 1) * KF * GT].rearrange("p (j n) -> p j n", j=KF) for k in (0, 1))
        rc = xbuf[:, 0:N_RCOLUMNS]
        b2st = sb("b2st", [2 * LO_ROW, 128])
        b2hl = sb("b2hl", [128, 128], F16)
        b2t = sb("b2t", [2 * LO_ROW, 128], F16)
        pickb = sb("pickb", [128, EXPERTS], F16)
        same16 = sb("same16", [128, 128], F16)
        enough16 = sb("enough16", [TT, 128], F16)
        token16 = sb("token16", [TT, TILES], F16)
        before16 = sb("before16", [TT, TT], F16)
        ones16 = sb("ones16", [128, 128], F16)

        carve = carver()
        sh32 = carve([128, KF, GT])
        h2b = carve([TT, TPG, 128])
        fin = carve([TT, TPG, 128])
        pe_major = carve([128, GT])
        pe_bits = carve([128, GT], U32)
        key_high, key_low, key_tie, key_over, key = (carve([128, GT]) for _ in range(5))
        hits = carve([128, GT])
        cand, cand_high, bounds = (sb(n, [128, k]) for n, k in (("cand", 1), ("cand_high", 1), ("bounds", 2)))
        thr_bits = sb("thr_bits", [128, 2], U32)
        cnt = sb("cnt", [128, 1], F16)
        thr_wide = carve([128, TT])
        thr = carve([TT, EXPERTS])
        over16, tie16, over_c, tie_c = (carve([TT, EXPERTS, TILES], F16) for _ in range(4))
        pos1, pos2 = (carve([TT, EXPERTS, TILES]) for _ in range(2))
        pos_i, dig_ai, dig_bi = (carve([TT, EXPERTS, TILES], I32) for _ in range(3))
        dig_a, dig_b = (carve([TT, EXPERTS, TILES], F16) for _ in range(2))
        ET = EXPERTS * TILES
        hotA = carve([TT, EXPERTS, DIG_A, TILES], F16)
        hotB = carve([TT, DIG_B, EXPERTS, TILES], F16)
        picked = carve([DIG_A * HALF_E, 2, DIG_B * HALF_E])
        lists_f = carve([DIG_A * HALF_E, 2, DIG_B])
        lists = carve([EXPERTS, LIST])
        idx = sb("idx", [HC, 2 * EXPERTS], U32)

        carve = carver()
        gath = [carve([HC, 2, ROW]) for _ in range(RING)]
        gidx = [sb(f"gidx{i}", [HC, 2], U32) for i in range(RING)]
        sidx = [sb(f"sidx{i}", [HC, 2], U32) for i in range(RING)]
        score = carve([HC, RING, 2])
        eXh, eXl = (carve([128, RING, CAP], F16) for _ in range(2))
        eh32 = carve([128, 2, KF * CAP])
        ehh, ehl = (carve([128, 2, KF * CAP], F16) for _ in range(2))
        ey = [carve([HC, 2, 128]) for _ in range(RING)]

        h2_dram = nc.dram_tensor("h2_dram", (TILES, TT, C), F32, kind="Internal").ap()
        rows_dram = nc.dram_tensor("rows_dram", (TILES, TT, ROW), F32, kind="Internal").ap()

        T = [bank(f"T{i}") for i in range(3)]
        X = bank("X")
        Q = [bank(f"Q{i}") for i in range(4)]

        x_loaded = sem("x_loaded")
        w1_split = sem("w1_split")
        w2_split = sem("w2_split")
        w1_hi = sem("w1_hi")
        w2_hi = sem("w2_hi")
        small_loaded = sem("small_loaded")
        ident_loaded = sem("ident_loaded")
        const_loaded = sem("const_loaded")
        setup_mm = sem("setup_mm")
        setup_copy = sem("setup_copy")
        setup_vec = sem("setup_vec")
        ones_done = sem("ones_done")
        xT_mm = sem("xT_mm")
        xT_copied = sem("xT_copied")
        xh_done = sem("xh_done")
        xl_done = sem("xl_done")
        xu_done = sem("xu_done")
        hid_mm = sem("hid_mm")
        hid_hi = sem("hid_hi")
        hid_lo = sem("hid_lo")
        mix_mm = sem("mix_mm")
        mix_tanh = sem("mix_tanh")
        mix_exp = sem("mix_exp")
        mix_step = sem("mix_step")
        pooled_done = sem("pooled_done")
        fc_mm = sem("fc_mm")
        ln_step = sem("ln_step")
        ln1_stats = sem("ln1_stats")
        ln1_rstd = sem("ln1_rstd")
        h1_done = sem("h1_done")
        ln2_stats = sem("ln2_stats")
        ln2_r = sem("ln2_r")
        h1ob_done = sem("h1ob_done")
        pool_step = sem("pool_step")
        xn_done = sem("xn_done")
        xnT_mm = sem("xnT_mm")
        xnT_copied = sem("xnT_copied")
        proj_mm = sem("proj_mm")
        proj_tanh = sem("proj_tanh")
        proj_z = sem("proj_z")
        base_done = sem("base_done")
        u_done = sem("u_done")
        rot_step = sem("rot_step")
        head_done = sem("head_done")
        v_mm = sem("v_mm")
        v_tanh = sem("v_tanh")
        v_done = sem("v_done")
        lkT_mm = sem("lkT_mm")
        lk_copied = sem("lk_copied")
        qk_mm = sem("qk_mm")
        score_done = sem("score_done")
        kern_done = sem("kern_done")
        linkv_mm = sem("linkv_mm")
        linkv_done = sem("linkv_done")
        ot_mm = sem("ot_mm")
        g_done = sem("g_done")
        out_mm = sem("out_mm")
        h2_done = sem("h2_done")
        ln3_stats = sem("ln3_stats")
        ln3_rstd = sem("ln3_rstd")
        n2_done = sem("n2_done")
        n2T_mm = sem("n2T_mm")
        n2T_copied = sem("n2T_copied")
        n2h_done = sem("n2h_done")
        n2_split = sem("n2_split")
        gate_mm = sem("gate_mm")
        lmax_done = sem("lmax_done")
        lg_done = sem("lg_done")
        lexp_done = sem("lexp_done")
        gsum_done = sem("gsum_done")
        grcp_done = sem("grcp_done")
        probs_done = sem("probs_done")
        rows_stored = sem("rows_stored")
        h2_stored = sem("h2_stored")
        h2s_done = sem("h2s_done")
        dve_passed = sem("dve_passed")
        pool_passed = sem("pool_passed")
        rc_loaded = sem("rc_loaded")
        sw_loaded = sem("sw_loaded")
        rc_ready = sem("rc_ready")
        sw_hi = sem("sw_hi")
        sw_split = sem("sw_split")
        ew_hi = sem("ew_hi")
        ew_split = sem("ew_split")
        b2_split = sem("b2_split")
        pm_mm = sem("pm_mm")
        bits_done = sem("bits_done")
        key_step = sem("key_step")
        cand_ready = sem("cand_ready")
        hits_done = sem("hits_done")
        count_mm = sem("count_mm")
        bounds_done = sem("bounds_done")
        sh1_mm = sem("sh1_mm")
        sh_gelu = sem("sh_gelu")
        sh_hi = sem("sh_hi")
        sh_lo_pool = sem("sh_lo_pool")
        sh_lo_dve = sem("sh_lo_dve")
        sh2_mm = sem("sh2_mm")
        h2b_loaded = sem("h2b_loaded")
        fin_done = sem("fin_done")
        out_stored = sem("out_stored")
        thr_wide_done = sem("thr_wide_done")
        thr_mm = sem("thr_mm")
        thr_done = sem("thr_done")
        masks_done = sem("masks_done")
        scans_done = sem("scans_done")
        prefix_mm = sem("prefix_mm")
        pos_done = sem("pos_done")
        digits_done = sem("digits_done")
        hot_done = sem("hot_done")
        lists_mm = sem("lists_mm")
        picked_done = sem("picked_done")
        lists_done = sem("lists_done")
        lists_loaded = sem("lists_loaded")
        idx_mm = sem("idx_mm")
        idx_done = sem("idx_done")
        gidx_copied = sem("gidx_copied")
        sidx_copied = sem("sidx_copied")
        added = sem("added")
        eX_mm = sem("eX_mm")
        eX_hi = sem("eX_hi")
        eX_split = sem("eX_split")
        eh_mm = sem("eh_mm")
        eh_gelu = sem("eh_gelu")
        eh_hi = sem("eh_hi")
        eh_split = sem("eh_split")
        ey_mm = sem("ey_mm")
        ey_scaled = sem("ey_scaled")
        w1_loaded, w2_loaded = ([sem(f"{n}_loaded{i}") for i in range(MS)] for n in ("w1", "w2"))
        estage_loaded = [sem(f"estage_loaded{i}") for i in range(2)]
        gathered = [[sem(f"gathered{i}{h}") for h in range(2)] for i in range(RING)]
        scattered = [sem(f"scattered{h}") for h in range(2)]

        def past(group, n=1):
            return not isinstance(group, int) or group >= n

        def col(c0, n=1):
            return vec[:, c0:c0 + n]

        block = ctx.enter_context(nc.Block())

        PLACES = KH + 2 * MS
        ATTN_STEPS = 14
        AFTER = {2: [0], 3: [1], 5: [2], 6: [3], 7: [4], 8: [5], 9: [6], 11: [7], 12: [8], 13: [9], 14: [10], 16: [11],
                 17: [12], 18: [13]}

        PREP = KH - MS

        def mix_step_of(p):
            return (p - KH) // 2, (p - KH) % 2 == 1

        def schedule(eng, tok, attn):
            for p in range(PLACES):
                tok(0, p)
            with eng.Fori(1, GROUPS - 1) as g:
                for p in range(PLACES):
                    tok(g, p)
                    for s in AFTER.get(p, []):
                        attn(g - 1, s)
            for p in range(PLACES):
                tok(GROUPS - 1, p)
                for s in AFTER.get(p, []):
                    attn(GROUPS - 2, s)
            for s in range(ATTN_STEPS):
                attn(GROUPS - 1, s)

        MIX_STEPS = 1 + 3 * (MS - 1) + 1

        def mix_after(m):
            return 1 + 3 * m if m >= -1 else -1

        expert_turn = [0]

        def expert_steps(eng, step):
            for k in range(3):
                step(k, k % RING)
            with eng.Fori(0, (EXPERTS - 5) // RING) as i:
                expert_turn[0] = i
                for q in range(RING):
                    step(i * RING + q + 3, (q + 3) % RING)
            for k in range(3 + (EXPERTS - 5) // RING * RING, EXPERTS + 2):
                step(k, k % RING)

        def ring_use(k, q):
            if isinstance(k, int):
                return k // RING + 1
            return expert_turn[0] + (2 if q < 3 else 1)

        def bank_of_x(g, m):
            return (Q + [X])[m] if not past(g) else X

        NSMALL = [0]
        ZEROED = 4

        @block.sync
        def _(sp):
            def load_x(g):
                src = x[bass.ds(g * GB, GB)].rearrange("b (t m) c -> (b t) (m c)", m=MS)
                sp.dma_start(x_tok[:], src.rearrange("(k p) n -> p k n", p=TT)).then_inc(x_loaded, 16)

            sp.dma_start(ident, a["constants"][:, COLUMNS["ident"]]).then_inc(ident_loaded, 16)
            load_x(0)
            w1 = a["L0_tok_w1"].rearrange("(c m) n -> c m n", m=MS)
            for n in range(MS):
                sp.dma_start(stage1[:, n], w1[:, :, n * W1_COLS:(n + 1) * W1_COLS]).then_inc(w1_loaded[n], 16)

            def small(dst, src):
                NSMALL[0] += 1
                sp.dma_start(dst, src).then_inc(small_loaded, 16)

            rest = slice(COLUMNS["ident"].stop, N_COLUMNS)
            sp.dma_start(const[:, rest], a["constants"][:, rest]).then_inc(const_loaded, 16)
            small(fc_w[:], a["L0_tok_fc_w"])
            small(fcb_bc[:], a["L0_tok_fc_b"].partition_broadcast(TT))
            small(lng_bc[:], a["L0_tok_ln_g"].partition_broadcast(TT))
            small(lnb_bc[:], a["L0_tok_ln_b"].partition_broadcast(TT))
            small(ob_bc[:], a["L0_attn_o_b"].partition_broadcast(TT))
            small(scala[:], a["L0_attn_scala"].partition_broadcast(TT))
            for p in (0, LO_ROW):
                small(vb_row[p:p + 1, :], a["L0_attn_v_b"].rearrange("(a n) -> a n", a=1))
            small(vtB[:, 0, :], a["L0_attn_v_b"].partition_broadcast(CHUNK))
            small(wst[:, 0:2, :], a["L0_attn_u_w"].rearrange("(e p) d -> p e d", p=128))
            small(wst[:, 2:4, :], a["L0_attn_v_w"].rearrange("(e p) d -> p e d", p=128))
            small(wst[:, 4, :], a["L0_attn_base_w"])
            small(wst[0:64, 5, :], a["L0_attn_base_w"][64:128, :])
            small(wst[64:128, 5, :], a["L0_attn_base_w"][0:64, :])
            small(wst[:, 6:8, :], a["L0_attn_o_w"].rearrange("d (e p) -> d e p", e=2))
            def load_next(g):
                sp.wait_ge(xT_mm, (g + 1) * MS)
                load_x(g + 1)

            load_next(0)
            w2 = a["L0_tok_w2"].rearrange("(k p) n -> p k n", p=128)
            for n in range(MS):
                sp.wait_ge(w1_split, n + 1)
                sp.dma_start(stage2[:, 2 * n:2 * n + 2, :], w2[:, 2 * n:2 * n + 2, :]).then_inc(w2_loaded[n], 16)
            small(gate_w[:], a["L0_ffn_gate_w"])
            small(sb2_bc[:], a["L0_ffn_sb2"].partition_broadcast(TT))
            small(b2st[0:EXPERTS, :], a["L0_ffn_b2"])
            small(b2st[LO_ROW:LO_ROW + EXPERTS, :], a["L0_ffn_b2"])
            for i, n in enumerate(("qq_w", "qq_b", "qk_w", "qk_b", "lq_w", "lq_b", "lk_w", "lk_b")):
                small(vrows[i:i + 1, :], a["L0_attn_" + n])
            small(vrows[V_BASE:V_BASE + 1, :], a["L0_attn_base_b"].rearrange("(a n) -> a n", a=1))
            small(vrows[V_U:V_U + 2, :], a["L0_attn_u_b"].rearrange("(a n) -> a n", n=128))
            small(vrows[V_SB1:V_SB1 + KF, :], a["L0_ffn_sb1"].rearrange("(a n) -> a n", n=128))
            small(vrows[V_B1:N_VEC, :], a["L0_ffn_b1"].rearrange("e (a n) -> (e a) n", n=128))
            first = MAXPOS - CHUNK
            wv = a["L0_attn_w"]
            window = bass.AP(wv.tensor, first, [[1, CHUNK], [1, CHUNK]])
            small(zw[:, 0:CHUNK], window)
            small(zw[:, CHUNK:A_TOK], window)

            def store(a_):
                sp.wait_ge(h2s_done, a_ + 1)
                sp.dma_start(h2_dram[bass.ds(a_ * TPG, TPG)].rearrange("k p n -> p k n"), h2s[:]).then_inc(h2_stored, 16)
                sp.wait_ge(probs_done, a_ + 1)
                sp.dma_start(rows_dram[bass.ds(a_ * TPG, TPG)].rearrange("k p n -> p k n"), rows[:]).then_inc(rows_stored, 16)

            with sp.Fori(1, GROUPS - 1) as g:
                load_next(g)
                store(g - 1)
            def load_chunk(c):
                if c >= 2:
                    sp.wait_ge(ew_split, c - 1)
                e = slice(c % (EXPERTS // EC) * EC, (c % (EXPERTS // EC) + 1) * EC)
                if c < EXPERTS // EC:
                    src = a["L0_ffn_w1"][e].rearrange("e p n -> p e n")
                    dst = estage[c % 2].rearrange("p (e n) -> p e n", e=EC)
                else:
                    src = a["L0_ffn_w2"][e].rearrange("e (j p) n -> p (e j) n", p=128)
                    dst = estage[c % 2].rearrange("p (k n) -> p k n", k=EC * KF)
                sp.dma_start(dst, src).then_inc(estage_loaded[c % 2], 16)

            sp.wait_ge(xT_mm, GROUPS * MS)
            sp.dma_start(rc, a["routing"]).then_inc(rc_loaded, 16)
            sp.wait_ge(w2_split, MS)
            load_chunk(0)
            store(GROUPS - 2)
            sp.wait_ge(mix_mm, GROUPS * MS)
            sp.dma_start(sw_stage[:, 0, :], a["L0_ffn_sw1"]).then_inc(sw_loaded, 16)
            sp.dma_start(sw_stage[:, 1, :].rearrange("p (j n) -> p j n", j=KF), a["L0_ffn_sw2"].rearrange("(j p) n -> p j n", p=128))\
                .then_inc(sw_loaded, 16)
            sp.wait_ge(pooled_done, GROUPS)
            for c in range(1, 6):
                load_chunk(c)
            store(GROUPS - 1)
            sp.wait_ge(rows_stored, 16 * (GROUPS + 1))
            sp.wait_ge(h2_stored, 16 * (GROUPS + 1))
            def load_h2(i):
                sp.dma_start(h2b, h2_dram[bass.ds(i * TPG, TPG)].rearrange("k p n -> p k n")).then_inc(h2b_loaded, 16)

            def store_out(i):
                sp.wait_ge(fin_done, i + 1)
                sp.dma_start(out[bass.ds(i * TPG * TT, TPG * TT)].rearrange("(k p) n -> p k n", p=TT), fin).then_inc(out_stored, 16)

            load_h2(0)
            load_chunk(6)
            with sp.Fori(0, GROUPS - 1) as i:
                store_out(i)
                load_h2(i + 1)
            store_out(GROUPS - 1)
            load_chunk(7)
            sp.wait_ge(lists_done, 1)
            for h in range(2):
                sp.dma_start(lists[h * HALF_E:(h + 1) * HALF_E, :].rearrange("e (a b) -> e a b", a=DIG_A),
                             lists_f[:, h, :]).then_inc(lists_loaded, 16)

        @block.gpsimd
        def _(pool):
            pool.memset(mhalf[:], -0.5).then_inc(ones_done, 1)
            pool.memset(ones16[:], 1.0).then_inc(ones_done, 1)
            pool.memset(b2hl[:], 0.0).then_inc(ones_done, 1)
            pool.memset(vb16[:], 0.0).then_inc(ones_done, 1)
            pool.wait_ge(ones_done, ZEROED)
            pool.wait_ge(small_loaded, 16 * NSMALL[0])

            def tok(g, p):
                pass

            POOL_STEPS = 4

            def low_part(c, halves=(0, 1)):
                for i in halves:
                    n = slice(i * EC * FF // 2, (i + 1) * EC * FF // 2)
                    pool.wait_ge(ew_hi, c + 1)
                    ins = pool.tensor_tensor(chunk(1, c)[:, n], estage[c % 2][:, n], chunk(0, c)[:, n], ALU.subtract)
                    if i == 1:
                        ins.then_inc(ew_split, 1)

            def last(s):
                if s == 0:
                    low_part(0, (0,))
                if s == 2:
                    low_part(0, (1,))
                    pool.wait_ge(sw_hi, 1)
                    pool.tensor_tensor(sw1l, sw_stage[:, 0, :], sw1h, ALU.subtract)
                    pool.tensor_tensor(sw[:, 3, :], sw_stage[:, 1, :], sw[:, 2, :], ALU.subtract).then_inc(sw_split, 1)
                if s in (3, 4, 5):
                    low_part(s - 2)
                if s == 11:
                    low_part(4)

            def attn(a_, s):
                if isinstance(a_, int) and a_ == GROUPS - 1:
                    last(s)
                n = [0]

                def step(ins):
                    ins.then_inc(pool_step, 1)
                    n[0] += 1
                    pool.wait_ge(pool_step, a_ * POOL_STEPS + base + n[0])

                if s == 0:
                    base = 0
                    pool.wait_ge(ln1_stats, a_ + 1)
                    pool.sem_inc(pool_passed, 1)
                    step(pool.tensor_scalar(pst[:, 0, :], mv[:, 0, :, 1], EPS, None, ALU.add))
                    pool.tensor_tensor(pst[:, 1, :], pst[:, 0, :], mhalf[:], ALU.pow).then_inc(ln1_rstd, 1)
                if s == 1:
                    base = 1
                    pool.wait_ge(ln2_stats, a_ + 1)
                    pool.sem_inc(pool_passed, 1)
                    step(pool.tensor_scalar(pst[:, 2, :], mv[:, 1, :, 1], 1 + EPS, EPS * EPS, ALU.mult, ALU.add))
                    step(pool.tensor_tensor(pst[:, 5, :], pst[:, 2, :], mhalf[:], ALU.pow))
                    pool.tensor_tensor(pst[:, 6, :], pst[:, 5, :], scala[:, 0:1].broadcast_to([TT, TPG]), ALU.mult).then_inc(ln2_r, 1)
                    pool.wait_ge(h1_done, a_ + 1)
                    pool.tensor_tensor(h1ob[:], h1[:], ob_bc[:].unsqueeze(1).broadcast_to([TT, TPG, 128]), ALU.add)\
                        .then_inc(h1ob_done, 1)
                if s == 10:
                    base = 3
                    pool.wait_ge(ln3_stats, a_ + 1)
                    pool.sem_inc(pool_passed, 1)
                    step(pool.tensor_scalar(pst[:, 7, :], mv[:, 2, :, 1], EPS, None, ALU.add))
                    pool.tensor_tensor(pst[:, 7, :], pst[:, 7, :], mhalf[:], ALU.pow).then_inc(ln3_rstd, 1)
                    pool.wait_ge(h2_done, a_ + 1)
                    pool.wait_ge(h2_stored, 16 * (a_ + 1))
                    pool.tensor_tensor(h2s[:], h2[:], sb2_bc[:].unsqueeze(1).broadcast_to([TT, TPG, 128]), ALU.add)\
                        .then_inc(h2s_done, 1)

            schedule(pool, tok, attn)

            with pool.Fori(0, GROUPS) as i:
                for n, j in enumerate(range(0, KF, 2)):
                    pool.wait_ge(sh_hi, i * KF + j + 1)
                    pool.tensor_tensor(shl[:, j], sh32[:, j], shh[:, j], ALU.subtract).then_inc(sh_lo_pool, 1)

            for c in (5, 6, 7):
                low_part(c)

            table = rows_dram.rearrange("k p n -> (k p) n")

            def gather(e, q):
                pool.wait_ge(gidx_copied, e + 1)
                pool.sem_inc(pool_passed, 1)
                for h in range(2):
                    pool.indirect_dma_start(gath[q][:, h, :], None, table,
                                            bass.IndirectOffsetOnAxis(ap=gidx[q][:, h:h + 1], axis=0))\
                        .then_inc(gathered[q][h], 16)

            def scatter(e, q):
                pool.wait_ge(ey_scaled, e + 1)
                if past(e):
                    pool.wait_ge(scattered[0], 16 * e)
                    pool.wait_ge(scattered[1], 16 * e)
                pool.sem_inc(added, 1)
                for h in range(2):
                    pool.indirect_dma_start(out, bass.IndirectOffsetOnAxis(ap=sidx[q][:, h:h + 1], axis=0), ey[q][:, h, :], None,
                                            compute_op=ALU.add).then_inc(scattered[h], 16)

            for e in range(2):
                gather(e, e)

            def step(k, q):
                if not isinstance(k, int) or k + 2 < EXPERTS:
                    gather(k + 2, (q + 2) % RING)
                if isinstance(k, int) and k == 1:
                    pool.wait_ge(out_stored, 16 * GROUPS)
                if past(k, 2):
                    scatter(k - 2, (q + 2) % RING)

            expert_steps(pool, step)
            pool.wait_ge(scattered[0], 16 * EXPERTS)
            pool.wait_ge(scattered[1], 16 * EXPERTS)

        @block.scalar
        def _(act):
            def prep(g, m):
                act.wait_ge(xT_mm, g * MS + m + 1)
                if past(g):
                    act.wait_ge(xu_done, g)
                act.activation(xp32[:, m, :], bank_of_x(g, m)[:, 0:GT], ACT.Copy).then_inc(xT_copied, 1)

            for m in range(MS):
                prep(0, m)
            for n in range(MS):
                act.wait_ge(w1_loaded[n], 16)
                act.activation(w1h[:, :, n * W1_COLS:(n + 1) * W1_COLS], stage1[:, n], ACT.Copy, scale=SCALE)\
                    .then_inc(w1_hi, 1)
            def setup():
                act.wait_ge(setup_mm, 1)
                act.activation(wT[:, 0:4, :], Q[0][:].rearrange("p (k n) -> p k n", k=4), ACT.Copy).then_inc(setup_copy, 1)
                act.wait_ge(setup_mm, 2)
                act.activation(wT[:, 4:8, :], Q[1][:].rearrange("p (k n) -> p k n", k=4), ACT.Copy).then_inc(setup_copy, 1)
                act.wait_ge(setup_mm, 3)
                act.activation(vec[:], Q[2][:, 0:N_VEC], ACT.Copy).then_inc(setup_copy, 1)
                act.wait_ge(setup_mm, 4)
                act.activation(vswap[:], Q[3][:, 0:V_U], ACT.Copy).then_inc(setup_copy, 1)
                act.wait_ge(setup_copy, 4)
                act.activation(padv[:, 0:1], col(V_BASE), ACT.Tanh, scale=0.5).then_inc(setup_copy, 1)
                act.activation(padv[:, 1:2], vswap[:, V_BASE:V_BASE + 1], ACT.Tanh, scale=0.5).then_inc(setup_copy, 1)
                act.wait_ge(small_loaded, 16 * NSMALL[0])
                act.activation(vtB[:, 1, :], vtB[:, 0, :], ACT.Tanh, scale=0.5).then_inc(setup_copy, 1)
                act.activation(halfb[:, 0:1], col(V_BASE), ACT.Copy, scale=0.5)
                act.activation(halfb[:, 1:2], vswap[:, V_BASE:V_BASE + 1], ACT.Copy, scale=0.5)
                act.activation(halfb[:, 2:4], col(V_U, 2), ACT.Copy, scale=0.5).then_inc(setup_copy, 1)

            def high_part(c):
                act.wait_ge(estage_loaded[c % 2], 16 * (c // 2 + 1))
                act.activation(chunk(0, c), estage[c % 2], ACT.Copy).then_inc(ew_hi, 1)

            def last(s):
                if s == 0:
                    act.wait_ge(mix_mm, GROUPS * MS)
                    high_part(0)
                    act.wait_ge(rc_loaded, 16)
                    act.wait_ge(ones_done, ZEROED)
                    act.wait_ge(small_loaded, 16 * NSMALL[0])
                    act.activation(same16[:], rc[:, RCOLUMNS["same_expert"]], ACT.Copy)
                    act.activation(enough16[:], rc[0:TT, RCOLUMNS["enough"]], ACT.Copy)
                    act.activation(token16[:], rc[0:TT, RCOLUMNS["token"]], ACT.Copy)
                    act.activation(before16[:], rc[0:TT, RCOLUMNS["before"]], ACT.Copy)
                    act.activation(pickb[:], rc[:, RCOLUMNS["pick_b2"]], ACT.Copy)
                    act.activation(b2hl[0:EXPERTS, :], b2st[0:EXPERTS, :], ACT.Copy)
                    act.activation(b2t[LO_ROW:LO_ROW + EXPERTS, :], b2st[LO_ROW:LO_ROW + EXPERTS, :], ACT.Copy).then_inc(rc_ready, 1)
                    act.wait_ge(sw_loaded, 32)
                    act.wait_ge(pooled_done, GROUPS)
                    act.activation(sw1h, sw_stage[:, 0, :], ACT.Copy)
                    act.activation(sw[:, 2, :], sw_stage[:, 1, :], ACT.Copy).then_inc(sw_hi, 1)
                if s == 3:
                    high_part(1)
                if s == 6:
                    high_part(2)
                if s in (9, 10):
                    high_part(s - 6)

            w2_now = [0]

            def tok(g, p):
                if isinstance(g, int) and p >= KH - MS and w2_now[0] < MS:
                    n = w2_now[0]
                    w2_now[0] += 1
                    act.wait_ge(w2_loaded[n], 16)
                    for k in (2 * n, 2 * n + 1):
                        ins = act.activation(w2h[:, k], stage2m[:, k], ACT.Copy, scale=SCALE)
                    ins.then_inc(w2_hi, 1)
                if isinstance(g, int) and g == 0 and p == KH:
                    setup()
                if p < KH:
                    act.wait_ge(hid_mm, g * KH + p + 1)
                    act.activation(hidh[:, p, :], T[p % 3][:, 0:GT], ACT.Relu).then_inc(hid_hi, 1)
                    if p == PREP - 1:
                        act.wait_ge(xT_copied, (g + 1) * MS)
                        if past(g):
                            act.wait_ge(pooled_done, g)
                        act.activation(xu32, xp32, ACT.Copy).then_inc(xu_done, 1)
                    if p >= PREP and not (isinstance(g, int) and g == GROUPS - 1):
                        prep(g + 1, p - PREP)
                    return
                m, second = mix_step_of(p)
                if second:
                    act.wait_ge(mix_mm, g * MS + m + 1)
                    act.activation(mtanh[:, m % 2, :], T[(KH + m) % 3][:, 0:GT], ACT.Tanh, scale=0.5 / SCALE ** 2)\
                        .then_inc(mix_tanh, 1)
                    act.wait_ge(mix_tanh, g * MS + m + 1)
                    if past(g) or m >= 2:
                        act.wait_ge(mix_step, g * MIX_STEPS + mix_after(m - 2))
                    act.activation(mexp[:, m % 2, :], mtanh[:, m % 2, :], ACT.Exp, scale=0.5).then_inc(mix_exp, 1)

            def attn(a_, s):
                if isinstance(a_, int) and a_ == GROUPS - 1:
                    last(s)
                if s == 3:
                    act.wait_ge(xnT_mm, a_ + 1)
                    act.activation(xnT[:], Q[0][:, 0:GT], ACT.Copy).then_inc(xnT_copied, 1)
                if s in (4, 5):
                    for i in ((0, 1) if s == 4 else (2, 3)):
                        bank_ = Q[(1, 2, 3, 0)[i]]
                        bias = (col(V_BASE), vswap[:, V_BASE:V_BASE + 1], col(V_U), col(V_U + 1))[i]
                        act.wait_ge(proj_mm, a_ * 4 + i + 1)
                        if i >= 2:
                            act.wait_ge(base_done, a_ * 2 + i - 1)
                        act.activation(ptanh[:, i % 2, :], bank_[:, 0:GT], ACT.Tanh, bias=halfb[:, i:i + 1], scale=0.5)\
                            .then_inc(proj_tanh, 1)
                        act.activation(pz[:, i, :], bank_[:, 0:GT], ACT.Identity, bias=bias).then_inc(proj_z, 1)
                if s == 6:
                    act.wait_ge(v_mm, a_ * 2 + 1)
                    act.activation(vtA[:], Q[1][:].rearrange("p (b n) -> p b n", b=GB), ACT.Tanh, scale=0.5)\
                        .then_inc(v_tanh, 1)
                    act.wait_ge(v_mm, a_ * 2 + 2)
                    act.activation(vtB[0:B_TOK], Q[2][0:B_TOK, :].rearrange("p (b n) -> p b n", b=GB), ACT.Tanh, scale=0.5)\
                        .then_inc(v_tanh, 1)
                    act.wait_ge(lkT_mm, a_ + 1)
                    q3 = Q[3][:].rearrange("p (k b n) -> p k b n", k=2, b=GB)
                    act.activation(lkA[:], q3[:, 0], ACT.Copy)
                    act.activation(lkB[:], q3[0:CHUNK, 1], ACT.Copy).then_inc(lk_copied, 1)
                if s == 8:
                    act.wait_ge(linkv_mm, a_ + 1)
                    act.activation(linkv[:], Q[1][:].rearrange("p (b n) -> p b n", b=GB), ACT.Copy, scale=1.0 / CHUNK)\
                        .then_inc(linkv_done, 1)
                if s == 12:
                    act.wait_ge(n2T_mm, a_ + 1)
                    act.activation(n2T[:], Q[1][:, 0:GT], ACT.Copy).then_inc(n2T_copied, 1)
                if s == 13:
                    act.wait_ge(lg_done, a_ + 1)
                    act.activation(pexp[:], lg[:], ACT.Exp).then_inc(lexp_done, 1)

            schedule(act, tok, attn)

            def shared(g):
                for j in range(KF):
                    if j == 0 and past(g):
                        act.wait_ge(sh_lo_pool, g * KF // 2)
                        act.wait_ge(sh_lo_dve, g * KF // 2)
                    act.wait_ge(sh1_mm, g * KF + j + 1)
                    act.activation(sh32[:, j, :], Q[j][:, 0:GT], ACT.Gelu_apprx_tanh, bias=col(V_SB1 + j)).then_inc(sh_gelu, 1)
                for j in range(KF):
                    if j == 0 and past(g):
                        act.wait_ge(sh2_mm, g)
                    act.wait_ge(sh_gelu, g * KF + j + 1)
                    act.activation(shh[:, j], sh32[:, j], ACT.Copy).then_inc(sh_hi, 1)

            act.wait_ge(probs_done, GROUPS)
            shared(0)
            with act.Fori(1, GROUPS) as i:
                shared(i)
            for c in (5, 6, 7):
                high_part(c)

            def step(k, q):
                if not isinstance(k, int) or 1 <= k <= EXPERTS:
                    e, r2 = k - 1, (q + 1) % 2
                    if past(e):
                        act.wait_ge(eh_split, e)
                    for j in range(KF):
                        act.wait_ge(eh_mm, 2 * e + j // 2 + 1)
                        bias = vec[:, bass.ds(V_B1 + e * KF + j, 1)]
                        ins = act.activation(eh32[:, r2, j * CAP:(j + 1) * CAP], Q[2 * r2 + j // 2][:, j % 2 * CAP:(j % 2 + 1) * CAP],
                                             ACT.Gelu_apprx_tanh, bias=bias)
                    ins.then_inc(eh_gelu, 1)

            expert_steps(act, step)

        @block.tensor
        def _(pe):
            def transposes(dst, src, n=TPG):
                for k in range(n):
                    ins = pe.transpose(dst[:, k * TT:(k + 1) * TT], src(k), ident[0:TT, 0:TT])
                return ins

            def prep(g, m):
                pe.wait_ge(x_loaded, 16 * (g + 1))
                if past(g):
                    pe.wait_ge(xT_copied, g * MS + m)
                if m == 0 and past(g, 2):
                    pe.wait_ge(ln1_stats, g - 1)
                transposes(bank_of_x(g, m), lambda k: x_tok[:, k, m * C:(m + 1) * C]).then_inc(xT_mm, 1)

            def setup():
                pe.wait_ge(const_loaded, 16)
                pe.wait_ge(small_loaded, 16 * NSMALL[0])
                for k in range(8):
                    ins = pe.transpose(Q[k // 4][:, (k % 4) * 128:(k % 4 + 1) * 128], wst[:, k, :], ident)
                    if k % 4 == 3:
                        ins.then_inc(setup_mm, 1)
                pe.transpose(Q[2][:, 0:N_VEC], vrows, ident[0:N_VEC, 0:N_VEC]).then_inc(setup_mm, 1)
                pe.wait_ge(setup_copy, 3)
                pe.matmul(Q[3][:, 0:V_U], swap_m, vec[:, 0:V_U], start=True, stop=True).then_inc(setup_mm, 1)
                pe.matmul(Q[0][:, 0:CHUNK], zw[:], anti, start=True, stop=True).then_inc(setup_mm, 1)

            pe.wait_ge(ident_loaded, 16)
            for m in range(MS):
                prep(0, m)

            def tok(g, p):
                if isinstance(g, int) and g == 0 and p == KH:
                    setup()
                if p < KH:
                    dst = T[p % 3][:, 0:GT]
                    if p < 3 and past(g):
                        pe.wait_ge(mix_tanh, g * MS + p - 2)
                    if p >= 3:
                        pe.wait_ge(hid_lo, g * KH + p - 2)
                    if isinstance(g, int) and g == 0:
                        pe.wait_ge(w1_split, p // 2 + 1)
                    n = slice(p * 128, (p + 1) * 128)
                    for m in range(MS):
                        if p == 0:
                            pe.wait_ge(xl_done, g * MS + m + 1)
                        pe.matmul(dst, w1h[:, m, n], xh[:, m, :], start=(m == 0), stop=False)
                        pe.matmul(dst, w1h[:, m, n], xl[:, m, :], start=False, stop=False)
                        ins = pe.matmul(dst, w1l[:, m, n], xh[:, m, :], start=False, stop=(m == MS - 1))
                    ins.then_inc(hid_mm, 1)
                    if p >= PREP and not (isinstance(g, int) and g == GROUPS - 1):
                        prep(g + 1, p - PREP)
                    return
                m, second = mix_step_of(p)
                dst = T[(KH + m) % 3][:, 0:GT]
                if not second and m >= 3:
                    pe.wait_ge(mix_tanh, g * MS + m - 2)
                for k in range(KH // 2, KH) if second else range(KH // 2):
                    if isinstance(g, int) and g == 0 and m == 0:
                        pe.wait_ge(w2_split, k // 2 + 1)
                    if m == 0:
                        pe.wait_ge(hid_lo, g * KH + max(k + 1, KH - 2))
                    pe.matmul(dst, w2h[:, k, m, :], hidh[:, k, :], start=(k == 0), stop=False)
                    pe.matmul(dst, w2h[:, k, m, :], hidl[:, k, :], start=False, stop=False)
                    ins = pe.matmul(dst, w2l[:, k, m, :], hidh[:, k, :], start=False, stop=(k == KH - 1))
                if second:
                    ins.then_inc(mix_mm, 1)

            def attn(a_, s):
                if s == 0:
                    pe.wait_ge(pooled_done, a_ + 1)
                    pe.wait_ge(xT_copied, (a_ + 2) * MS if not (isinstance(a_, int) and a_ == GROUPS - 1) else GROUPS * MS)
                    for k in range(TPG):
                        ins = pe.matmul(X[0:TT, k * 128:(k + 1) * 128], pooled[:, k * TT:(k + 1) * TT], fc_w[:], start=True, stop=True)
                    ins.then_inc(fc_mm, 1)
                if s == 3:
                    pe.wait_ge(xn_done, a_ + 1)
                    transposes(Q[0], lambda k: xn[:, k, :]).then_inc(xnT_mm, 1)
                if s in (4, 5):
                    pe.wait_ge(xnT_copied, a_ + 1)
                    for i in ((0, 1) if s == 4 else (2, 3)):
                        wt = (baseT_w, swapT_w, uT_w[:, 0, :], uT_w[:, 1, :])[i]
                        pe.matmul(Q[(1, 2, 3, 0)[i]][:, 0:GT], wt, xnT[:], start=True, stop=True).then_inc(proj_mm, 1)
                if s == 6:
                    pe.wait_ge(proj_z, a_ * 4 + 4)
                    for b in range(GB):
                        t0 = b * TW
                        o = Q[1][:, b * E:(b + 1) * E]
                        pe.matmul(o, xnT[:, t0:t0 + A_TOK], vT_w, start=True, stop=False)
                        ins = pe.matmul(o, ones16[0:LO_ROW + 1, 0:A_TOK], vb16[:], start=False, stop=True)
                    ins.then_inc(v_mm, 1)
                    for b in range(GB):
                        t0 = b * TW + A_TOK
                        o = Q[2][0:B_TOK, b * E:(b + 1) * E]
                        pe.matmul(o, xnT[:, t0:t0 + B_TOK], vT_w, start=True, stop=False)
                        ins = pe.matmul(o, ones16[0:LO_ROW + 1, 0:B_TOK], vb16[:], start=False, stop=True)
                    ins.then_inc(v_mm, 1)
                    pe.wait_ge(head_done, a_ * 4 + 1)
                    for b in range(GB):
                        pe.transpose(Q[3][:, b * 128:(b + 1) * 128], qT["lk"][:, b, 0:A_TOK], ident)
                        ins = pe.transpose(Q[3][0:CHUNK, (GB + b) * 128:(GB + b + 1) * 128], qT["lk"][:, b, A_TOK:PADDED], ident)
                    ins.then_inc(lkT_mm, 1)
                if s == 7:
                    pe.wait_ge(head_done, a_ * 4 + 4)
                    for b in range(GB):
                        pe.matmul(Q[0][:, b * A_TOK:(b + 1) * A_TOK], qT["qk"][:, b, 0:A_TOK], qT["qq"][:, b, 0:A_TOK],
                                  start=True, stop=True)
                        c0 = GB * A_TOK + b * B_TOK
                        ins = pe.matmul(Q[0][0:CHUNK, c0:c0 + B_TOK], qT["qk"][:, b, A_TOK:PADDED], qT["qq"][:, b, A_TOK:TW],
                                        start=True, stop=True)
                    ins.then_inc(qk_mm, 1)
                if s == 8:
                    pe.wait_ge(lk_copied, a_ + 1)
                    pe.wait_ge(v_done, a_ * 2 + 2)
                    for b in range(GB):
                        o = Q[1][:, b * E:(b + 1) * E]
                        pe.matmul(o, lkA[:, b, :], vA[:, b, :], start=True, stop=False)
                        ins = pe.matmul(o, lkB[:, b, :], vB[:, b, :], start=False, stop=True)
                    ins.then_inc(linkv_mm, 1)
                if s == 9:
                    pe.wait_ge(linkv_done, a_ + 1)
                    pe.wait_ge(kern_done, a_ + 1)
                    for i in range(2):
                        e = slice(i * 128, (i + 1) * 128)
                        for b in range(GB):
                            t0 = b * TW
                            o = Q[2 + i]
                            pe.matmul(o[:, t0:t0 + TW], linkv[:, b, e], qT["lq"][:, b, :], start=True, stop=False)
                            pe.matmul(o[:, t0:t0 + A_TOK], vA[:, b, e], kA[:, b, :], start=False, stop=False)
                            ins = pe.matmul(o[:, t0 + A_TOK:t0 + TW], vB[:, b, e], kB[:, b, :], start=False, stop=True)
                    ins.then_inc(ot_mm, 1)
                if s == 10:
                    pe.wait_ge(g_done, a_ + 1)
                    for k in range(TPG):
                        o = Q[0][0:TT, k * 128:(k + 1) * 128]
                        for i in range(2):
                            ins = pe.matmul(o, gT[:, i, k * TT:(k + 1) * TT], oT_w[:, i, :], start=(i == 0), stop=(i == 1))
                    ins.then_inc(out_mm, 1)
                if s == 12:
                    pe.wait_ge(n2_done, a_ + 1)
                    transposes(Q[1], lambda k: rows[:, k, 0:C]).then_inc(n2T_mm, 1)
                if s == 13:
                    pe.wait_ge(n2T_copied, a_ + 1)
                    for k in range(TPG):
                        ins = pe.matmul(Q[2][0:TT, k * EXPERTS:(k + 1) * EXPERTS], n2T[:, k * TT:(k + 1) * TT], gate_w[:],
                                        start=True, stop=True)
                    ins.then_inc(gate_mm, 1)

            schedule(pe, tok, attn)

            pe.wait_ge(probs_done, GROUPS)
            for n in range(TPG):
                ins = pe.transpose(T[0][:, n * TT:(n + 1) * TT], probs[:, n * 8:(n + 1) * 8, :].rearrange("p k e -> p (k e)"),
                                   ident[0:TT, 0:TT])
            ins.then_inc(pm_mm, 1)

            def first_layer(g, js):
                toks = bass.ds(g * GT, GT)
                for j in js:
                    if past(g):
                        pe.wait_ge(sh_gelu, (g - 1) * KF + j + 1)
                    n = slice(j * 128, (j + 1) * 128)
                    pe.matmul(Q[j][:, 0:GT], sw1h[:, n], n2h[:, toks], start=True, stop=False)
                    pe.matmul(Q[j][:, 0:GT], sw1h[:, n], n2l[:, toks], start=False, stop=False)
                    pe.matmul(Q[j][:, 0:GT], sw1l[:, n], n2h[:, toks], start=False, stop=True).then_inc(sh1_mm, 1)

            def second_layer(g, ks):
                if 0 in ks:
                    pe.wait_ge(sh_lo_pool, (g + 1) * KF // 2)
                    pe.wait_ge(sh_lo_dve, (g + 1) * KF // 2)
                    if past(g):
                        pe.wait_ge(fin_done, g)
                for k in ks:
                    o = X[0:TT, k * 128:(k + 1) * 128]
                    t = slice(k * TT, (k + 1) * TT)
                    for j in range(KF):
                        pe.matmul(o, shh[:, j, t], sw2h[:, j, :], start=(j == 0), stop=False)
                        pe.matmul(o, shl[:, j, t], sw2h[:, j, :], start=False, stop=False)
                        ins = pe.matmul(o, shh[:, j, t], sw2l[:, j, :], start=False, stop=(j == KF - 1))
                if TPG - 1 in ks:
                    ins.then_inc(sh2_mm, 1)

            def count(n):
                pe.wait_ge(cand_ready, n + 1)
                pe.matmul(T[1][:, 0:1], enough16[:], ones16[0:TT, 0:1], start=True, stop=False)
                pe.wait_ge(hits_done, n + 1)
                pe.matmul(T[1][:, 0:1], same16[:], cnt[:], start=False, stop=True).then_inc(count_mm, 1)

            pe.wait_ge(rc_ready, 1)
            pe.wait_ge(sw_split, 1)
            pe.wait_ge(n2_split, GROUPS)
            first_layer(0, range(KF))

            def search(i):
                count(i * 4)
                if not isinstance(i, int):
                    first_layer(i + 1, (0, 1))
                count(i * 4 + 1)
                if not isinstance(i, int):
                    first_layer(i + 1, (2, 3))
                count(i * 4 + 2)
                second_layer(i, (0,))
                count(i * 4 + 3)
                second_layer(i, (1, 2))

            with pe.Fori(0, GROUPS - 1) as i:
                search(i)
            search(GROUPS - 1)

            pe.wait_ge(thr_wide_done, 1)
            pe.transpose(T[2][0:TT, 0:128], thr_wide, ident).then_inc(thr_mm, 1)
            pe.wait_ge(masks_done, 1)
            flat = lambda v: v.rearrange("p e t -> p (e t)")
            pe.matmul(T[0][0:TT, 0:ET], before16[:], flat(over16), start=True, stop=False)
            pe.matmul(T[1][0:TT, 0:ET], before16[:], flat(tie16), start=True, stop=False)
            later = [T[n][0:TT, 0:ET].rearrange("p (e t) -> p e t", e=EXPERTS)[:, :, 1:TILES] for n in (0, 1)]
            pe.wait_ge(scans_done, 1)
            pe.matmul(later[0], ones16[0:TT, 0:TT], over_c[:, :, 0:TILES - 1], start=False, stop=True)
            pe.matmul(T[1][0:TT, 0:ET].rearrange("p (e t) -> p e t", e=EXPERTS), ones16[0:TT, 0:TT],
                      over_c[:, :, TILES - 1:TILES].broadcast_to([TT, EXPERTS, TILES]), start=False, stop=False)
            pe.wait_ge(scans_done, 2)
            pe.matmul(later[1], ones16[0:TT, 0:TT], tie_c[:, :, 0:TILES - 1], start=False, stop=True).then_inc(prefix_mm, 1)
            for h in range(2):
                pe.wait_ge(hot_done, h + 1)
                e = slice(h * HALF_E, (h + 1) * HALF_E)
                o = Q[h][0:DIG_A * HALF_E, 0:DIG_B * HALF_E]
                for t in range(TILES):
                    ins = pe.matmul(o, hotA[:, e, :, t].rearrange("p e a -> p (e a)"), hotB[:, :, e, t],
                                    start=(t == 0), stop=(t == TILES - 1))
                ins.then_inc(lists_mm, 1)
            pe.wait_ge(lists_loaded, 32)
            for h in range(2):
                ins = pe.transpose(T[2][0:HC, h * EXPERTS:(h + 1) * EXPERTS], lists[:, h * HC:(h + 1) * HC], ident[0:EXPERTS, 0:EXPERTS])
            ins.then_inc(idx_mm, 1)

            def step(k, q):
                if not isinstance(k, int) or 1 <= k <= EXPERTS:
                    e, r2, slot = k - 1, (q + 1) % 2, (q + 3) % RING
                    pe.wait_ge(eX_split, e + 1)
                    for j in range(KF):
                        o = Q[2 * r2 + j // 2][:, j % 2 * CAP:(j % 2 + 1) * CAP]
                        wh, wl = (v[:, bass.ds(e, 1), j * 128:(j + 1) * 128].rearrange("p a n -> p (a n)") for v in (e1h, e1l))
                        pe.matmul(o, wh, eXh[:, slot, :], start=True, stop=False)
                        pe.matmul(o, wh, eXl[:, slot, :], start=False, stop=False)
                        ins = pe.matmul(o, wl, eXh[:, slot, :], start=False, stop=True)
                        if j % 2:
                            ins.then_inc(eh_mm, 1)
                if not isinstance(k, int) or k < EXPERTS:
                    for h in range(2):
                        pe.wait_ge(gathered[q][h], 16 * ring_use(k, q))
                        ins = pe.transpose(T[q % 2][:, h * HC:(h + 1) * HC], gath[q][:, h, 0:C], ident[0:HC, 0:HC])
                    ins.then_inc(eX_mm, 1)
                if past(k, 2):
                    e, r2 = k - 2, q % 2
                    pe.wait_ge(eh_split, e + 2)
                    for h in range(2):
                        o = (T[2], X)[r2][0:HC, h * 128:(h + 1) * 128]
                        for j in range(KF):
                            sl = slice(j * CAP + h * HC, j * CAP + (h + 1) * HC)
                            wh, wl = (v[:, bass.ds(e, 1), j, :].rearrange("p a n -> p (a n)") for v in (e2h, e2l))
                            pe.matmul(o, ehh[:, r2, sl], wh, start=(j == 0), stop=False)
                            pe.matmul(o, ehl[:, r2, sl], wh, start=False, stop=False)
                            pe.matmul(o, ehh[:, r2, sl], wl, start=False, stop=False)
                        ins = pe.matmul(o, pickb[:, bass.ds(e, 1)].broadcast_to([128, HC]), b2hl[:], start=False, stop=True)
                    ins.then_inc(ey_mm, 1)

            pe.wait_ge(b2_split, 1)
            pe.wait_ge(ew_split, 2 * EXPERTS // EC)
            expert_steps(pe, step)

        @block.vector
        def _(dve):
            def split_x(g, m):
                dve.wait_ge(xT_copied, g * MS + m + 1)
                if past(g):
                    dve.wait_ge(hid_mm, g * KH)
                dve.tensor_copy(xh[:, m, :], xp32[:, m, :]).then_inc(xh_done, 1)
                dve.wait_ge(xh_done, g * MS + m + 1)
                dve.tensor_tensor(xl[:, m, :], xp32[:, m, :], xh[:, m, :], ALU.subtract).then_inc(xl_done, 1)

            for m in range(MS):
                split_x(0, m)
            for n in range(MS):
                cols = slice(n * W1_COLS, (n + 1) * W1_COLS)
                dve.wait_ge(w1_hi, n + 1)
                dve.scalar_tensor_tensor(w1l[:, :, cols], stage1[:, n], SCALE, w1h[:, :, cols], ALU.mult, ALU.subtract)\
                    .then_inc(w1_split, 1)

            def setup():
                n = [0]

                def step(ins):
                    n[0] += 1
                    ins.then_inc(setup_vec, 1)
                    dve.wait_ge(setup_vec, n[0])

                dve.wait_ge(setup_copy, 8)
                dve.wait_ge(setup_mm, 5)
                dve.wait_ge(small_loaded, 16 * NSMALL[0])
                dve.wait_ge(ones_done, ZEROED)
                low = slice(LO_ROW, LO_ROW + 1)
                step(dve.tensor_copy(vb16[0:1, :], vb_row[0:1, :]))
                step(dve.tensor_copy(vb_high[low, :], vb_row[low, :]))
                step(dve.tensor_tensor(vb16[low, :], vb_row[low, :], vb_high[low, :], ALU.subtract))
                for h in range(GB):
                    c = slice(h * CHUNK, (h + 1) * CHUNK)
                    step(dve.tensor_tensor(biasA[:, c], Q[0][:, 0:CHUNK], mask[:, c], ALU.add))
                step(dve.tensor_scalar(whalf[:, 0, :], vec[:, 0:V_U], 0.5, None, ALU.mult))
                step(dve.tensor_scalar(whalf[:, 1, :], vswap[:], 0.5, None, ALU.mult))
                step(dve.scalar_tensor_tensor(padv[:, 2:3], padv[:, 0:1], 1.0, col(V_BASE), ALU.add, ALU.mult))
                step(dve.scalar_tensor_tensor(padv[:, 3:4], padv[:, 1:2], 1.0, vswap[:, V_BASE:V_BASE + 1], ALU.add, ALU.mult))
                step(dve.scalar_tensor_tensor(vB[:, 0, :], vtB[:, 1, :], 1.0, vtB[:, 0, :], ALU.add, ALU.mult))
                step(dve.tensor_copy(vB[:, 1, :], vB[:, 0, :]))
                pad = slice(GT, TABLE)
                step(dve.tensor_scalar(padc[:, 0, :], cos[:, pad], padv[:, 2:3], None, ALU.mult))
                step(dve.tensor_scalar(padc[:, 1, :], sin[:, pad], padv[:, 3:4], None, ALU.mult))
                for i, (name, wc, bc) in enumerate(HEADS):
                    step(dve.tensor_scalar(ctab[:, i, :], cos, col(bc), None, ALU.mult))
                    step(dve.scalar_tensor_tensor(ctab[:, i, :], sin, vswap[:, bc:bc + 1], ctab[:, i, :], ALU.mult, ALU.add))
                    if name in ("lk", "qk"):
                        step(dve.scalar_tensor_tensor(padc[:, 2, :], padc[:, 0, :], whalf[:, 0, wc:wc + 1], ctab[:, i, pad],
                                                      ALU.mult, ALU.add))
                        step(dve.scalar_tensor_tensor(padc[:, 3, :], padc[:, 1, :], whalf[:, 1, wc:wc + 1], padc[:, 2, :],
                                                      ALU.mult, ALU.add))
                        for b in range(GB):
                            step(dve.tensor_copy(qT[name][:, b, TW:PADDED], padc[:, 3, :]))

            w2_now = [0]

            def tok(g, p):
                first = isinstance(g, int) and g == 0
                if first and p >= KH - MS and w2_now[0] < MS:
                    n = w2_now[0]
                    w2_now[0] += 1
                    dve.wait_ge(w2_hi, n + 1)
                    for k in (2 * n, 2 * n + 1):
                        ins = dve.scalar_tensor_tensor(w2l[:, k], stage2m[:, k], SCALE, w2h[:, k], ALU.mult, ALU.subtract)
                    ins.then_inc(w2_split, 1)
                if first and p == KH + 2:
                    setup()
                if p < KH:
                    dve.wait_ge(hid_hi, g * KH + p + 1)
                    dve.scalar_tensor_tensor(hidl[:, p, :], T[p % 3][:, 0:GT], 0.0, hidh[:, p, :], ALU.max, ALU.subtract)\
                        .then_inc(hid_lo, 1)
                    return
                if p - KH < MS and not (isinstance(g, int) and g == GROUPS - 1):
                    split_x(g + 1, p - KH)
                m, second = mix_step_of(p)
                if not second:
                    return
                base = g * MIX_STEPS + mix_after(m - 1)

                def done(ins):
                    return ins.then_inc(mix_step, 1)

                dve.wait_ge(mix_exp, g * MS + m + 1)
                if m == 0:
                    dve.wait_ge(xu_done, g + 1)
                    dve.tensor_copy(den[:], mexp[:, 0, :])
                    done(dve.tensor_tensor(num[:], mexp[:, 0, :], xu32[:, 0, :], ALU.mult))
                else:
                    dve.wait_ge(mix_step, base)
                    done(dve.tensor_tensor(prod[:], mexp[:, m % 2, :], xu32[:, m, :], ALU.mult))
                    done(dve.tensor_tensor(den[:], den[:], mexp[:, m % 2, :], ALU.add))
                    dve.wait_ge(mix_step, base + 1)
                    done(dve.tensor_tensor(num[:], num[:], prod[:], ALU.add))
                if m == MS - 1:
                    dve.wait_ge(mix_step, base + 3)
                    done(dve.reciprocal(den[:], den[:]))
                    dve.wait_ge(mix_step, base + 4)
                    dve.tensor_tensor(pooled[:], num[:], den[:], ALU.mult).then_inc(pooled_done, 1)

            LN_STEPS = 5

            def stats(a_, src, n, signal):
                for k in range(TPG):
                    ins = dve.bn_stats(st6[:, k, :], src(k))
                ins.then_inc(ln_step, 1)
                dve.wait_ge(ln_step, a_ * LN_STEPS + (2, 4, 5)[n])
                dve.sem_inc(dve_passed, 1)
                for k in range(TPG):
                    ins = dve.bn_aggr(mv[:, n, k, :], st6[:, k, :])
                ins.then_inc(signal, 1)

            def bc(t):
                return t[:].unsqueeze(1).broadcast_to([TT, TPG, 128])

            def attn(a_, s):
                if s == 0:
                    dve.wait_ge(fc_mm, a_ + 1)
                    dve.tensor_tensor(z[:], X[0:TT, 0:GT + 84].rearrange("p (k n) -> p k n", k=TPG), bc(fcb_bc), ALU.add)\
                        .then_inc(ln_step, 1)
                    dve.wait_ge(ln_step, a_ * LN_STEPS + 1)
                    stats(a_, lambda k: z[:, k, :], 0, ln1_stats)
                    dve.wait_ge(ln1_stats, a_ + 1)
                    for k in range(TPG):
                        ins = dve.scalar_tensor_tensor(xn[:, k, :], z[:, k, :], mv[:, 0, k, 0:1], lng_bc[:], ALU.subtract, ALU.mult)
                    ins.then_inc(ln_step, 1)
                if s == 1:
                    dve.wait_ge(ln_step, a_ * LN_STEPS + 3)
                    dve.wait_ge(ln1_rstd, a_ + 1)
                    for k in range(TPG):
                        ins = dve.scalar_tensor_tensor(h1[:, k, :], xn[:, k, :], pst[:, 1, k:k + 1], lnb_bc[:], ALU.mult, ALU.add)
                    ins.then_inc(h1_done, 1)
                    dve.wait_ge(h1_done, a_ + 1)
                    stats(a_, lambda k: h1[:, k, :], 1, ln2_stats)
                if s == 2:
                    dve.wait_ge(ln2_stats, a_ + 1)
                    dve.wait_ge(ln2_r, a_ + 1)
                    for k in range(TPG):
                        ins = dve.tensor_scalar(xn[:, k, :], h1[:, k, :], mv[:, 1, k, 0:1], pst[:, 6, k:k + 1], ALU.subtract, ALU.mult)
                    ins.then_inc(xn_done, 1)
                if s == 4:
                    for i in range(2):
                        dve.wait_ge(proj_z, a_ * 4 + i + 1)
                        ins = dve.scalar_tensor_tensor(base2[:, i, :], ptanh[:, i, :], 1.0, pz[:, i, :], ALU.add, ALU.mult)
                        ins.then_inc(base_done, 1)
                    dve.wait_ge(base_done, a_ * 2 + 2)
                    dve.tensor_tensor(rot[:, 0, :], base2[:, 0, :], cos[:, 0:GT], ALU.mult)
                    dve.tensor_tensor(rot[:, 1, :], base2[:, 1, :], sin[:, 0:GT], ALU.mult).then_inc(rot_step, 1)
                    dve.wait_ge(rot_step, a_ * ROT_STEPS + 1)
                    for i, (name, wc, _) in enumerate(HEADS):
                        dve.scalar_tensor_tensor(htmp[:, i % 2, :], rot[:, 0, :], whalf[:, 0, wc:wc + 1], ctab[:, i, 0:GT],
                                                 ALU.mult, ALU.add).then_inc(rot_step, 1)
                        dve.wait_ge(rot_step, a_ * ROT_STEPS + 2 + i)
                        dve.scalar_tensor_tensor(qT[name][:, :, 0:TW], rot[:, 1, :].rearrange("p (b n) -> p b n", b=GB),
                                                 whalf[:, 1, wc:wc + 1], htmp[:, i % 2, :].rearrange("p (b n) -> p b n", b=GB),
                                                 ALU.mult, ALU.add).then_inc(head_done, 1)
                if s == 5:
                    for i in range(2):
                        dve.wait_ge(proj_z, a_ * 4 + i + 3)
                        dve.scalar_tensor_tensor(u2[:, i, :], ptanh[:, i, :], 1.0, pz[:, 2 + i, :], ALU.add, ALU.mult)\
                            .then_inc(u_done, 1)
                if s == 6:
                    dve.wait_ge(v_tanh, a_ * 2 + 1)
                    dve.scalar_tensor_tensor(vA[:], vtA[:], 1.0, Q[1][:].rearrange("p (b n) -> p b n", b=GB), ALU.add, ALU.mult)\
                        .then_inc(v_done, 1)
                    dve.wait_ge(v_tanh, a_ * 2 + 2)
                    dve.scalar_tensor_tensor(vB[0:B_TOK], vtB[0:B_TOK], 1.0, Q[2][0:B_TOK, :].rearrange("p (b n) -> p b n", b=GB),
                                             ALU.add, ALU.mult).then_inc(v_done, 1)
                if s == 7:
                    dve.wait_ge(qk_mm, a_ + 1)
                    n = GB * A_TOK
                    dve.scalar_tensor_tensor(sA[:], Q[0][:, 0:n].rearrange("p (b n) -> p b n", b=GB), 1.0 / CHUNK,
                                             biasA[:].unsqueeze(1).broadcast_to([128, GB, A_TOK]), ALU.mult, ALU.add)
                    dve.scalar_tensor_tensor(sB[:], Q[0][0:CHUNK, n:n + GB * B_TOK].rearrange("p (b n) -> p b n", b=GB), 1.0 / CHUNK,
                                             biasA[0:CHUNK, 0:B_TOK].unsqueeze(1).broadcast_to([CHUNK, GB, B_TOK]),
                                             ALU.mult, ALU.add).then_inc(score_done, 1)
                    dve.wait_ge(score_done, a_ + 1)
                    dve.scalar_tensor_tensor(kA[:], sA[:], 0.0, sA[:], ALU.max, ALU.mult)
                    dve.scalar_tensor_tensor(kB[:], sB[:], 0.0, sB[:], ALU.max, ALU.mult).then_inc(kern_done, 1)
                if s == 9:
                    dve.wait_ge(ot_mm, a_ + 1)
                    dve.wait_ge(u_done, a_ * 2 + 2)
                    for i in range(2):
                        ins = dve.scalar_tensor_tensor(gT[:, i, :], Q[2 + i][:, 0:GT], 0.25, u2[:, i, :], ALU.mult, ALU.mult)
                    ins.then_inc(g_done, 1)
                if s == 10:
                    dve.wait_ge(out_mm, a_ + 1)
                    dve.wait_ge(h1ob_done, a_ + 1)
                    dve.tensor_tensor(h2[:], Q[0][0:TT, 0:TPG * 128].rearrange("p (k n) -> p k n", k=TPG), h1ob[:], ALU.add)\
                        .then_inc(h2_done, 1)
                    dve.wait_ge(h2_done, a_ + 1)
                    stats(a_, lambda k: h2[:, k, :], 2, ln3_stats)
                if s == 11:
                    dve.wait_ge(ln3_stats, a_ + 1)
                    dve.wait_ge(ln3_rstd, a_ + 1)
                    dve.wait_ge(rows_stored, 16 * (a_ + 1))
                    for k in range(TPG):
                        ins = dve.tensor_scalar(rows[:, k, 0:C], h2[:, k, :],
                                                mv[:, 2, k, 0:1], pst[:, 7, k:k + 1], ALU.subtract, ALU.mult)
                    ins.then_inc(n2_done, 1)
                if s == 12:
                    dve.wait_ge(n2T_copied, a_ + 1)
                    dve.tensor_copy(n2h[:, bass.ds(a_ * GT, GT)], n2T[:]).then_inc(n2h_done, 1)
                    dve.wait_ge(n2h_done, a_ + 1)
                    dve.tensor_tensor(n2l[:, bass.ds(a_ * GT, GT)], n2T[:], n2h[:, bass.ds(a_ * GT, GT)], ALU.subtract)\
                        .then_inc(n2_split, 1)
                if s == 13:
                    dve.wait_ge(gate_mm, a_ + 1)
                    q2 = Q[2][0:TT, 0:TPG * EXPERTS].rearrange("p (k n) -> p k n", k=TPG)

                    def over(t):
                        return t[:].unsqueeze(2).broadcast_to([TT, TPG, EXPERTS])

                    dve.tensor_reduce(lmax[:], q2, AX_X, ALU.max).then_inc(lmax_done, 1)
                    dve.wait_ge(lmax_done, a_ + 1)
                    dve.tensor_tensor(lg[:], q2, over(lmax), ALU.subtract).then_inc(lg_done, 1)
                    dve.wait_ge(lexp_done, a_ + 1)
                    dve.tensor_reduce(psum_[:], pexp[:], AX_X, ALU.add).then_inc(gsum_done, 1)
                    dve.wait_ge(gsum_done, a_ + 1)
                    dve.reciprocal(prcp[:], psum_[:]).then_inc(grcp_done, 1)
                    dve.wait_ge(grcp_done, a_ + 1)
                    dve.tensor_tensor(rows[:, :, C:ROW], pexp[:], over(prcp), ALU.mult)
                    dve.tensor_tensor(probs[:, bass.ds(a_ * TPG, TPG), :], pexp[:], over(prcp), ALU.mult)\
                        .then_inc(probs_done, 1)

            ROT_STEPS = 5
            dve.sem_inc(rows_stored, 16)
            dve.sem_inc(h2_stored, 16)
            schedule(dve, tok, attn)

            dve.wait_ge(pm_mm, 1)
            dve.tensor_copy(pe_major, T[0][:, 0:GT]).then_inc(bits_done, 1)
            dve.memset(cand[:], 0.5).then_inc(cand_ready, 1)
            dve.wait_ge(bits_done, 1)
            low_bits = (1 << HALF_BITS) - 1
            dve.tensor_scalar(pe_bits, pe_major.bitcast(U32), low_bits << HALF_BITS, None, ALU.bitwise_and).then_inc(bits_done, 1)
            dve.tensor_scalar(pe_major.bitcast(U32), pe_major.bitcast(U32), low_bits, None, ALU.bitwise_and).then_inc(bits_done, 1)
            dve.wait_ge(bits_done, 2)
            dve.tensor_scalar(key_high, pe_bits, 0.5 ** (2 * HALF_BITS), None, ALU.mult).then_inc(key_step, 1)
            dve.wait_ge(bits_done, 3)
            dve.tensor_scalar(key_low, pe_major.bitcast(U32), 0.5 ** HALF_BITS, None, ALU.mult).then_inc(key_step, 1)
            deltas = rc[:, RCOLUMNS["bounds"]]
            dve.wait_ge(rc_ready, 1)
            rl = slice(LO_ROW, LO_ROW + EXPERTS)
            dve.tensor_tensor(b2hl[rl, :], b2st[rl, :], b2t[rl, :], ALU.subtract).then_inc(b2_split, 1)

            def fin_rows(g):
                dve.wait_ge(sh2_mm, g + 1)
                dve.wait_ge(h2b_loaded, 16 * (g + 1))
                if past(g):
                    dve.wait_ge(out_stored, 16 * g)
                dve.tensor_tensor(fin, X[0:TT, 0:TPG * 128].rearrange("p (k n) -> p k n", k=TPG), h2b, ALU.add)\
                    .then_inc(fin_done, 1)

            def split_low(g, j):
                dve.wait_ge(sh_hi, g * KF + j + 1)
                dve.tensor_tensor(shl[:, j], sh32[:, j], shh[:, j], ALU.subtract).then_inc(sh_lo_dve, 1)

            def search(i, keys):
                for q in range(4):
                    n = i * 4 + q
                    dve.wait_ge(cand_ready, n + 1)
                    dve.tensor_scalar(hits, keys, cand[:], None, ALU.is_ge, ALU.add, accum_out=cnt[:]).then_inc(hits_done, 1)
                    dve.tensor_tensor(bounds[:], cand[:].broadcast_to([128, 2]), deltas[:, bass.ds(2 * n, 2)], ALU.add)\
                        .then_inc(bounds_done, 1)
                    if q == 0 and past(i):
                        fin_rows(i - 1)
                    if q in (1, 2):
                        split_low(i, 2 * q - 1)
                    dve.wait_ge(bounds_done, n + 1)
                    dve.wait_ge(count_mm, n + 1)
                    dve.tensor_scalar(cand[:], T[1][:, 0:1], bounds[:, 0:1], bounds[:, 1:2], ALU.max, ALU.min)\
                        .then_inc(cand_ready, 1)

            half = GROUPS // 2
            dve.wait_ge(key_step, 2)
            search(0, key_high)
            with dve.Fori(1, half) as i:
                search(i, key_high)
            dve.wait_ge(cand_ready, 4 * half + 1)
            dve.scalar_tensor_tensor(key_tie, key_high, cand[:], key_low, ALU.is_equal, ALU.mult)
            dve.tensor_scalar(key_over, key_high, cand[:], None, ALU.is_gt)
            dve.tensor_copy(cand_high[:], cand[:]).then_inc(key_step, 1)
            dve.wait_ge(key_step, 3)
            dve.tensor_tensor(key, key_tie, key_over, ALU.add).then_inc(key_step, 1)
            dve.memset(cand[:], 0.5).then_inc(key_step, 1)
            dve.wait_ge(key_step, 5)
            with dve.Fori(half, GROUPS) as i:
                search(i, key)
            dve.wait_ge(cand_ready, 4 * GROUPS + 1)
            dve.tensor_scalar(thr_bits[:, 0:1], cand_high[:], 2.0 ** (2 * HALF_BITS), None, ALU.mult)
            dve.tensor_scalar(thr_bits[:, 1:2], cand[:], 2.0 ** HALF_BITS, None, ALU.mult).then_inc(key_step, 1)
            dve.wait_ge(key_step, 6)
            dve.tensor_tensor(thr_wide.bitcast(U32), thr_bits[:, 0:1].broadcast_to([128, TT]), thr_bits[:, 1:2].broadcast_to([128, TT]),
                              ALU.bitwise_or).then_inc(thr_wide_done, 1)
            fin_rows(GROUPS - 1)
            dve.wait_ge(thr_mm, 1)
            dve.tensor_copy(thr, T[2][0:TT, 0:EXPERTS]).then_inc(thr_done, 1)
            dve.wait_ge(thr_done, 1)
            wide = thr.unsqueeze(2).broadcast_to([TT, EXPERTS, TILES])
            by_e = probs[:].rearrange("p k e -> p e k")
            dve.tensor_tensor(over16, by_e, wide, ALU.is_gt)
            dve.tensor_tensor(tie16, by_e, wide, ALU.is_equal).then_inc(masks_done, 1)
            dve.wait_ge(masks_done, 1)
            flat = lambda v: v.rearrange("p e t -> p (e t)")
            fresh = rc[0:TT, RCOLUMNS["not_first"]]
            for src, dst in ((over16, over_c), (tie16, tie_c)):
                dve.tensor_tensor_scan(flat(dst), fresh, flat(src), 0.0, ALU.mult, ALU.add).then_inc(scans_done, 1)
            FAR = 1024.0
            dve.wait_ge(prefix_mm, 1)
            dve.scalar_tensor_tensor(flat(pos1), T[0][0:TT, 0:ET], FAR, flat(over16), ALU.subtract, ALU.mult)
            dve.scalar_tensor_tensor(flat(pos2), T[1][0:TT, 0:ET], FAR, flat(tie16), ALU.subtract, ALU.mult).then_inc(pos_done, 1)
            dve.wait_ge(pos_done, 1)
            dve.scalar_tensor_tensor(flat(pos_i), flat(pos1), FAR, flat(pos2), ALU.add, ALU.add).then_inc(pos_done, 1)
            dve.wait_ge(pos_done, 2)
            dve.tensor_scalar(flat(dig_ai), flat(pos_i), 0xFFF - (DIG_B - 1), None, ALU.bitwise_and)
            dve.tensor_scalar(flat(dig_bi), flat(pos_i), DIG_B - 1, None, ALU.bitwise_and).then_inc(digits_done, 1)
            dve.wait_ge(digits_done, 1)
            dve.tensor_copy(flat(dig_a), flat(dig_ai))
            dve.tensor_copy(flat(dig_b), flat(dig_bi)).then_inc(digits_done, 1)
            dve.wait_ge(digits_done, 2)
            number = token16[:].unsqueeze(1).broadcast_to([TT, EXPERTS, TILES])
            for k in range(DIG_A):
                dve.scalar_tensor_tensor(hotA[:, :, k], dig_a, float(k * DIG_B), number, ALU.is_equal, ALU.mult)
            for h in range(2):
                e = slice(h * HALF_E, (h + 1) * HALF_E)
                for k in range(DIG_B):
                    ins = dve.tensor_scalar(hotB[:, k, e], dig_b[:, e], float(k), None, ALU.is_equal)
                ins.then_inc(hot_done, 1)
            na = DIG_A * HALF_E
            for h in range(2):
                dve.wait_ge(lists_mm, h + 1)
                ins = dve.tensor_tensor(picked[:, h, :], Q[h][0:na, 0:DIG_B * HALF_E], rc[0:na, RCOLUMNS["diagonal"]], ALU.mult)
            ins.then_inc(picked_done, 1)
            dve.wait_ge(picked_done, 1)
            dve.tensor_reduce(lists_f, picked.rearrange("p h (b e) -> p h b e", b=DIG_B), AX_X, ALU.add).then_inc(lists_done, 1)
            dve.wait_ge(idx_mm, 1)
            dve.tensor_scalar(idx[:], T[2][0:HC, 0:2 * EXPERTS], TOKENS // 2, None, ALU.add).then_inc(idx_done, 1)
            dve.wait_ge(idx_done, 1)

            def indices(tile_, e):
                return dve.tensor_copy(tile_[:].rearrange("p (h a) -> p h a", h=2),
                                       idx[:].rearrange("p (h e) -> p h e", h=2)[:, :, bass.ds(e, 1)])

            def copy_gather(e, q):
                indices(gidx[q], e).then_inc(gidx_copied, 1)

            dve.sem_inc(eh_split, 1)
            for e in range(2):
                copy_gather(e, e)

            def step(k, q):
                if not isinstance(k, int) or k + 2 < EXPERTS:
                    copy_gather(k + 2, (q + 2) % RING)
                if not isinstance(k, int) or k < EXPERTS:
                    if past(k, RING):
                        dve.wait_ge(added, k - RING + 2)
                        dve.sem_inc(dve_passed, 1)
                    indices(sidx[q], k).then_inc(sidx_copied, 1)
                    dve.wait_ge(eX_mm, k + 1)
                    src = T[q % 2][:, 0:CAP]
                    dve.tensor_copy(eXh[:, q, :], src).then_inc(eX_hi, 1)
                    dve.tensor_copy(score[:, q, :].unsqueeze(2), gath[q][:, :, bass.ds(C + k, 1)])
                    dve.wait_ge(eX_hi, k + 1)
                    dve.tensor_tensor(eXl[:, q, :], src, eXh[:, q, :], ALU.subtract).then_inc(eX_split, 1)
                if not isinstance(k, int) or 1 <= k <= EXPERTS:
                    e, r2 = k - 1, (q + 1) % 2
                    dve.wait_ge(eh_gelu, e + 1)
                    dve.tensor_copy(ehh[:, r2, :], eh32[:, r2, :]).then_inc(eh_hi, 1)
                    dve.wait_ge(eh_hi, e + 1)
                    dve.tensor_tensor(ehl[:, r2, :], eh32[:, r2, :], ehh[:, r2, :], ALU.subtract).then_inc(eh_split, 1)
                if past(k, 2):
                    e, r2, slot = k - 2, q % 2, (q + 2) % RING
                    dve.wait_ge(ey_mm, e + 1)
                    for h in range(2):
                        ins = dve.tensor_scalar(ey[slot][:, h, :], (T[2], X)[r2][0:HC, h * 128:(h + 1) * 128],
                                                score[:, slot, h:h + 1], None, ALU.mult)
                    ins.then_inc(ey_scaled, 1)

            expert_steps(dve, step)


_IN = ["x", "L0_tok_w1", "L0_tok_w2", "L0_tok_fc_w", "L0_tok_fc_b", "L0_tok_ln_g", "L0_tok_ln_b", "L0_attn_scala",
       "L0_attn_u_w", "L0_attn_u_b", "L0_attn_v_w", "L0_attn_v_b", "L0_attn_base_w", "L0_attn_base_b", "L0_attn_qq_w",
       "L0_attn_qq_b", "L0_attn_qk_w", "L0_attn_qk_b", "L0_attn_lq_w", "L0_attn_lq_b", "L0_attn_lk_w", "L0_attn_lk_b",
       "L0_attn_o_w", "L0_attn_o_b", "L0_attn_w", "L0_ffn_gate_w", "L0_ffn_w1", "L0_ffn_b1", "L0_ffn_w2", "L0_ffn_b2",
       "L0_ffn_sw1", "L0_ffn_sb1", "L0_ffn_sw2", "L0_ffn_sb2"]


def kernel(**inputs):
    import concourse.bacc as bacc
    from concourse.bass_utils import run_bass_kernel_spmd

    nc = bacc.Bacc("TRN2", target_bir_lowering=False, num_devices=1)
    arrays = {n: np.ascontiguousarray(inputs[n]) for n in _IN}
    arrays["constants"] = constant_table()
    arrays["routing"] = routing_table()
    aps = {n: nc.dram_tensor(f"in_{n}", v.shape, mybir.dt.from_np(v.dtype), kind="ExternalInput").ap() for n, v in arrays.items()}
    out = nc.dram_tensor("out_h", (TOKENS, C), F32, kind="ExternalOutput").ap()
    build(nc, aps, out)
    r = run_bass_kernel_spmd(nc, [{f"in_{n}": v for n, v in arrays.items()}], core_ids=[0])
    return r.results[0]["out_h"].reshape(BATCH, TW, C)
```

```python
from contextlib import ExitStack

import numpy as np

import concourse.bass as bass
from concourse import mybir

F32 = mybir.dt.float32
F16 = mybir.dt.float16
U32 = mybir.dt.uint32
I32 = mybir.dt.int32
ALU = mybir.AluOpType
ACT = mybir.ActivationFunctionType
AX_X = mybir.AxisListType.X

BATCH, STEPS, C = 16, 750, 128
MS = 5
TW = STEPS // MS
TOKENS = BATCH * TW
HID = 2 * C * MS
KH = HID // 128
E = 2 * C
CHUNK = 64
PADDED = 3 * CHUNK
A_TOK = 2 * CHUNK
B_TOK = TW - A_TOK
PAD_TOK = PADDED - TW
MAXPOS = 128
GB = 2
GT = GB * TW
GROUPS = BATCH // GB
TT = 100
TPG = GT // TT
TILES = TOKENS // TT
EXPERTS, FF = 16, 512
KF = FF // 128
CAP = TOKENS // EXPERTS
ROW = C + EXPERTS
EPS = 1e-5
OFF_BLOCK = -1e30

SCALE = 16.0

TABLE = GT + PAD_TOK
COLUMNS = {}
_at = 0
for _name, _width in (("ident", 128), ("swap", 128), ("anti", CHUNK), ("mask", A_TOK), ("cos", TABLE), ("sin", TABLE)):
    COLUMNS[_name] = slice(_at, _at + _width)
    _at += _width
N_COLUMNS = _at
DIG_A, DIG_B = 10, 16
LIST = DIG_A * DIG_B
HALF_E = EXPERTS // 2
EARLY = 2
HC = CAP // 2
PHASES, DIGIT = 3, 10
UNITS = (2.0 ** 3, 2.0 ** -7, 2.0 ** -14)
ENOUGH = 2.0 ** 15
RCOLUMNS = {}
_at = 0
for _name, _width in (("same_expert", 128), ("before", TT), ("enough", 128), ("token", TILES),
                      ("not_first", EXPERTS * TILES), ("diagonal", 128), ("bounds", 2 * PHASES * DIGIT), ("pick_b2", EXPERTS)):
    RCOLUMNS[_name] = slice(_at, _at + _width)
    _at += _width
N_RCOLUMNS = _at
LO_ROW = 32
RING = 4
LEAD = RING - 1
REGION = 13044


def routing_table():
    t = np.zeros((128, N_RCOLUMNS), np.float32)
    p = np.arange(128)
    t[:, RCOLUMNS["same_expert"]] = ENOUGH * (p[:, None] % EXPERTS == p[None, :] % EXPERTS)
    t[0, RCOLUMNS["enough"]] = -ENOUGH / 2 ** 10 * (CAP - 0.5)
    t[:, RCOLUMNS["before"]] = p[:, None] < np.arange(TT)[None, :]
    t[:, RCOLUMNS["token"]] = np.arange(TILES) * TT + p[:, None] - TOKENS // 2
    t[:, RCOLUMNS["not_first"]] = np.tile(np.arange(TILES), EXPERTS) > 0
    t[:, RCOLUMNS["diagonal"]] = p[:, None] // DIG_A == p[None, :] % HALF_E
    up = 2.0 ** (DIGIT - 2 - np.arange(DIGIT))
    down = -up
    up[-1], down[-1] = 0, -1
    steps = np.stack([down, up], axis=1).reshape(-1)
    t[:, RCOLUMNS["bounds"]] = np.concatenate([u * steps for u in UNITS])
    e = np.arange(EXPERTS)
    t[:, RCOLUMNS["pick_b2"]] = (p[:, None] == e[None, :]) | (p[:, None] == LO_ROW + e[None, :])
    return t


def constant_table():
    t = np.zeros((128, N_COLUMNS), np.float32)
    p = np.arange(128)
    t[p, COLUMNS["ident"].start + p] = 1
    t[p, COLUMNS["swap"].start + (p + 64) % 128] = 1
    q = np.arange(CHUNK)
    t[q, COLUMNS["anti"].start + CHUNK - 1 - q] = 1
    t[:, COLUMNS["mask"]] = np.where(p[:, None] // CHUNK == p[None, :] // CHUNK, 0, OFF_BLOCK)
    half = C // 2
    inv_freq = (10000.0 ** (-np.arange(half, dtype=np.float32) / half)).astype(np.float32)
    pos = np.concatenate([np.arange(TW)] * GB + [np.arange(TW, PADDED)]).astype(np.float32)
    angle = (pos[None, :] * inv_freq[:, None]).astype(np.float32)
    t[:half, COLUMNS["cos"]] = t[half:, COLUMNS["cos"]] = np.cos(angle)
    t[:half, COLUMNS["sin"]] = -np.sin(angle)
    t[half:, COLUMNS["sin"]] = np.sin(angle)
    return t


V_QQW, V_QQB, V_QKW, V_QKB, V_LQW, V_LQB, V_LKW, V_LKB, V_BASE = range(9)
V_U = 9
V_SB1 = V_U + 2
V_B1 = V_SB1 + KF
N_VEC = V_B1 + EXPERTS * KF
HEADS = (("lk", V_LKW, V_LKB), ("qk", V_QKW, V_QKB), ("qq", V_QQW, V_QQB), ("lq", V_LQW, V_LQB))


def build(nc, a, out):
    x = a["x"]
    with ExitStack() as ctx:
        def sb(name, shape, dt=F32):
            return ctx.enter_context(nc.sbuf_tensor(name, shape, dt))

        def bank(name):
            return ctx.enter_context(nc.psum_tensor(name, [128, 512], F32))

        def sem(name):
            return ctx.enter_context(nc.semaphore(name))

        const = sb("const", [128, N_COLUMNS])
        ident, swap_m, mask = (const[:, COLUMNS[n]] for n in ("ident", "swap", "mask"))
        anti = const[0:CHUNK, COLUMNS["anti"]]
        cos, sin = const[:, COLUMNS["cos"]], const[:, COLUMNS["sin"]]

        arena = sb("arena", [128, 4 * MS * HID + 2 * MS * HID], F16)
        part = MS * HID
        w1h = arena[:, 0:part].rearrange("p (m n) -> p m n", m=MS)
        w1l = arena[:, part:2 * part].rearrange("p (m n) -> p m n", m=MS)
        w2h = arena[:, 2 * part:3 * part].rearrange("p (k m c) -> p k m c", k=KH, m=MS)
        w2l = arena[:, 3 * part:4 * part].rearrange("p (k m c) -> p k m c", k=KH, m=MS)
        stage = arena[:, 4 * part:6 * part].bitcast(F32)
        W1_COLS = HID // MS
        stage1 = stage.rearrange("p (i m n) -> p i m n", i=MS, m=MS)
        stage2 = stage.rearrange("p (k n) -> p k n", k=KH)
        stage2m = stage.rearrange("p (k c m) -> p k m c", k=KH, m=MS)

        wTh, wTl = (sb(n, [128, 6, 128], F16) for n in ("wTh", "wTl"))
        oT_w = sb("oT_w", [128, 2, 128])
        fc_w = sb("fc_w", [128, 128])
        gate_w = sb("gate_w", [128, EXPERTS])
        vec = sb("vec", [128, N_VEC])
        vswap = sb("vswap", [128, V_U])
        whalf = sb("whalf", [128, 2, V_U])
        fcb_bc, lng_bc, lnb_bc, ob_bc = (sb(n, [TT, 128]) for n in ("fcb_bc", "lng_bc", "lnb_bc", "ob_bc"))
        scala = sb("scala", [TT, 1])
        vb16 = sb("vb16", [LO_ROW + 1, E], F16)
        sb2_bc = sb("sb2_bc", [TT, 128])
        mhalf = sb("mhalf", [TT, TPG])
        zw = sb("zw", [CHUNK, A_TOK])
        biasA = sb("biasA", [128, A_TOK])
        halfb = sb("halfb", [128, 4])
        padc = sb("padc", [128, 4, PAD_TOK])
        padv = sb("padv", [128, 4])

        xbuf = sb("xbuf", [128, TPG * MS * C])
        x_tok = xbuf[0:TT, :].rearrange("p (k n) -> p k n", k=TPG)
        xp_xu = sb("xp_xu", [128, 2 * MS * GT])
        xp32, xu32 = (xp_xu[:, k * MS * GT:(k + 1) * MS * GT].rearrange("p (m n) -> p m n", m=MS) for k in (0, 1))
        xh = sb("xh", [128, MS, GT], F16)
        xl = sb("xl", [128, MS, GT], F16)
        hid = sb("hid", [128, 2, KH * GT], F16)
        hidh, hidl = (hid[:, k, :].rearrange("p (k n) -> p k n", k=KH) for k in (0, 1))
        mte = sb("mte", [128, 4, GT])
        mtanh, mexp = mte[:, 0:2, :], mte[:, 2:4, :]
        den, num, prod = (sb(n, [128, GT]) for n in ("den", "num", "prod"))
        pooled = sb("pooled", [128, GT])

        region = sb("region", [128, REGION])

        def carver():
            at = [0]

            def carve(shape, dt=F32):
                n = int(np.prod(shape[1:]))
                words = n if dt != F16 else (n + 1) // 2
                v = region[:, at[0]:at[0] + words]
                at[0] += words
                assert at[0] <= REGION, at[0]
                if dt != F32:
                    v = v.bitcast(dt)
                v = v[0:shape[0], 0:n]
                if len(shape) == 3:
                    v = v.rearrange("p (a n) -> p a n", a=shape[1])
                if len(shape) == 4:
                    v = v.rearrange("p (a b n) -> p a b n", a=shape[1], b=shape[2])
                return v
            return carve

        carve = carver()
        z = carve([TT, TPG, 128])
        h1 = carve([TT, TPG, 128])
        xn = carve([TT, TPG, 128])
        h1ob = carve([TT, TPG, 128])
        st6 = sb("st6", [TT, TPG, 6])
        mv = sb("mv", [TT, 3, TPG, 2])
        pst = sb("pst", [TT, 8, TPG])
        xnh, xnl = (carve([128, GT], F16) for _ in range(2))
        ptanh = carve([128, 2, GT])
        PZ_AT = 4 * TPG * 128 + GT + 2 * GT
        pz = carve([128, 4, GT])
        wst = pz.rearrange("p a n -> p (a n)")[:, 0:1024].rearrange("p (k n) -> p k n", k=8)
        vrows = pz.rearrange("p a n -> p (a n)")[0:N_VEC, 1024:1152]
        base2 = carve([128, 2, GT])
        u2 = carve([128, 2, GT])
        rot = carve([128, 2, GT])
        htmp = carve([128, 2, GT])
        qT = {n: carve([128, GB, PADDED]) for n in ("lk", "qk")}
        for n in ("qq", "lq"):
            qT[n] = carve([128, GB, TW])
        vtA = carve([128, GB, E])
        vtB = carve([CHUNK, GB, E])
        vA = carve([128, GB, E])
        vB = carve([CHUNK, GB, E])
        lkA = carve([128, GB, 128])
        lkB = carve([CHUNK, GB, 128])
        linkv = carve([128, GB, E])
        vb_row, vb_high = linkv[0:LO_ROW + 1, 0, :], linkv[0:LO_ROW + 1, 1, :].bitcast(F16)[:, 0:E]
        sA = carve([128, GB, A_TOK])
        sB = carve([CHUNK, GB, B_TOK])
        kA = carve([128, GB, A_TOK])
        kB = carve([CHUNK, GB, B_TOK])
        gT = carve([128, 2, GT])
        ctab = carve([128, 4, TABLE])
        h2 = sb("h2", [TT, TPG, 128])
        h2s = sb("h2s", [TT, TPG, 128])
        rows = sb("rows", [TT, TPG, ROW])
        n2T = sb("n2T", [128, GT])
        n2hl = sb("n2hl", [128, 2, TOKENS], F16)
        n2h, n2l = n2hl[:, 0, :], n2hl[:, 1, :]
        lmax = sb("lmax", [TT, TPG])
        lg = sb("lg", [TT, TPG, EXPERTS])
        pexp = sb("pexp", [TT, TPG, EXPERTS])
        psum_ = sb("psum_", [TT, TPG])
        prcp = sb("prcp", [TT, TPG])
        probs = sb("probs", [TT, TILES, EXPERTS])

        ew = EXPERTS * FF
        EC = 4

        def chunk(lo, c):
            at_ = (2 * (c // (EXPERTS // EC)) + lo) * ew + c % (EXPERTS // EC) * EC * FF
            return arena[:, at_:at_ + EC * FF]

        e1h, e1l = (arena[:, k * ew:(k + 1) * ew].rearrange("p (e n) -> p e n", e=EXPERTS) for k in (0, 1))
        e2h, e2l = (arena[:, k * ew:(k + 1) * ew].rearrange("p (e j n) -> p e j n", e=EXPERTS, j=KF) for k in (2, 3))
        estage = [arena[:, 4 * ew:4 * ew + 2 * EC * FF].bitcast(F32), xp_xu[:, 0:EC * FF]]
        sw_stage = hid[:, 0, :].bitcast(F32)[:, 0:2 * FF].rearrange("p (a n) -> p a n", a=2)
        sw = mte[:].rearrange("p a n -> p (a n)").bitcast(F16)[:, 0:4 * FF].rearrange("p (a n) -> p a n", a=4)
        sw1h, sw1l = sw[:, 0, :], sw[:, 1, :]
        sw2h, sw2l = (sw[:, k, :].rearrange("p (j n) -> p j n", j=KF) for k in (2, 3))
        shh, shl = (hid[:, 1, k * KF * GT:(k + 1) * KF * GT].rearrange("p (j n) -> p j n", j=KF) for k in (0, 1))
        rc = xbuf[:, 0:N_RCOLUMNS]
        b2st = sb("b2st", [2 * LO_ROW, 128])
        b2hl = sb("b2hl", [128, 128], F16)
        b2t = sb("b2t", [2 * LO_ROW, 128], F16)
        pickb = sb("pickb", [128, EXPERTS], F16)
        same16 = sb("same16", [128, 128], F16)
        enough16 = sb("enough16", [TT, 128], F16)
        before16 = sb("before16", [TT, TT], F16)
        ones16 = sb("ones16", [128, 128], F16)

        carve = carver()
        h2b = carve([TT, TPG, 128])
        fin = carve([TT, TPG, 128])
        pe_major = carve([128, GT])
        pe_bits = carve([128, GT], U32)
        pe_masked = carve([128, PHASES - 1, GT], U32)
        keys = carve([128, PHASES - 1, GT], F16)
        lists = carve([EXPERTS, LIST])
        carve([128, PZ_AT - 2 * TPG * 128 - 5 * GT - LIST])
        sh32 = carve([128, KF, GT])
        digits = carve([128, PHASES, GT], F16)
        shifted = carve([128, GT])
        hits = carve([128, GT], F16)
        cand, found, bounds = (sb(n, [128, k]) for n, k in (("cand", 1), ("found", PHASES), ("bounds", 2)))
        enough_by = sb("enough_by", [TT, 1], F16)
        thr_bits = sb("thr_bits", [128, 2], U32)
        cnt = sb("cnt", [128, 1], F16)
        thr_wide = carve([128, TT])
        thr = carve([TT, EXPERTS])
        over16, tie16, over_c, tie_c = (carve([TT, EXPERTS, TILES], F16) for _ in range(4))
        pos1, pos2 = (carve([TT, EXPERTS, TILES]) for _ in range(2))
        pos_i, dig_ai, dig_bi = (carve([TT, EXPERTS, TILES], I32) for _ in range(3))
        dig_a, dig_b = (carve([TT, EXPERTS, TILES], F16) for _ in range(2))
        ET = EXPERTS * TILES
        hotA = carve([TT, EXPERTS, DIG_A, TILES], F16)
        hotB = carve([TT, DIG_B, EXPERTS, TILES], F16)
        picked = carve([DIG_A * HALF_E, 2, DIG_B * HALF_E])
        lists_f = carve([DIG_A * HALF_E, 2, DIG_B])
        idx = sb("idx", [HC, 2 * EXPERTS], U32)

        carve = carver()
        gath = [carve([HC, 2, ROW]) for _ in range(RING)]
        gidx = [sb(f"gidx{i}", [HC, 2], U32) for i in range(RING)]
        sidx = [sb(f"sidx{i}", [HC, 2], U32) for i in range(RING)]
        score = carve([HC, RING, 2])
        eXh, eXl = (carve([128, RING, CAP], F16) for _ in range(2))
        eh32 = carve([128, 2, KF * CAP])
        ehh, ehl = (carve([128, 2, KF * CAP], F16) for _ in range(2))
        ey = [carve([HC, 2, 128]) for _ in range(RING)]

        h2_dram = nc.dram_tensor("h2_dram", (TILES, TT, C), F32, kind="Internal").ap()
        rows_dram = nc.dram_tensor("rows_dram", (TILES, TT, ROW), F32, kind="Internal").ap()

        T = [bank(f"T{i}") for i in range(3)]
        X = bank("X")
        Q = [bank(f"Q{i}") for i in range(4)]

        x_loaded = sem("x_loaded")
        w1_split = sem("w1_split")
        w2_split = sem("w2_split")
        w1_hi = sem("w1_hi")
        w2_hi = sem("w2_hi")
        small_loaded = sem("small_loaded")
        ident_loaded = sem("ident_loaded")
        const_loaded = sem("const_loaded")
        setup_mm = sem("setup_mm")
        setup_copy = sem("setup_copy")
        setup_vec = sem("setup_vec")
        ones_done = sem("ones_done")
        xT_mm = sem("xT_mm")
        xT_copied = sem("xT_copied")
        xh_done = sem("xh_done")
        xl_done = sem("xl_done")
        xu_done = sem("xu_done")
        hid_mm = sem("hid_mm")
        hid_hi = sem("hid_hi")
        hid_lo = sem("hid_lo")
        mix_mm = sem("mix_mm")
        mix_tanh = sem("mix_tanh")
        mix_exp = sem("mix_exp")
        mix_step = sem("mix_step")
        pooled_done = sem("pooled_done")
        fc_mm = sem("fc_mm")
        ln_step = sem("ln_step")
        ln1_stats = sem("ln1_stats")
        ln1_rstd = sem("ln1_rstd")
        h1_done = sem("h1_done")
        ln2_stats = sem("ln2_stats")
        ln2_r = sem("ln2_r")
        h1ob_done = sem("h1ob_done")
        pool_step = sem("pool_step")
        xn_done = sem("xn_done")
        xnT_mm = sem("xnT_mm")
        xnT_copied = sem("xnT_copied")
        xnT_low = sem("xnT_low")
        proj_mm = sem("proj_mm")
        proj_z = sem("proj_z")
        base_done = sem("base_done")
        u_done = sem("u_done")
        rot_step = sem("rot_step")
        head_done = sem("head_done")
        v_mm = sem("v_mm")
        v_tanh = sem("v_tanh")
        v_done = sem("v_done")
        lkT_mm = sem("lkT_mm")
        lk_copied = sem("lk_copied")
        qk_mm = sem("qk_mm")
        score_done = sem("score_done")
        kern_done = sem("kern_done")
        linkv_mm = sem("linkv_mm")
        linkv_done = sem("linkv_done")
        ot_mm = sem("ot_mm")
        g_done = sem("g_done")
        out_mm = sem("out_mm")
        h2_done = sem("h2_done")
        ln3_stats = sem("ln3_stats")
        ln3_rstd = sem("ln3_rstd")
        n2_done = sem("n2_done")
        n2T_mm = sem("n2T_mm")
        n2T_copied = sem("n2T_copied")
        n2h_done = sem("n2h_done")
        n2_split = sem("n2_split")
        gate_mm = sem("gate_mm")
        lmax_done = sem("lmax_done")
        lg_done = sem("lg_done")
        lexp_done = sem("lexp_done")
        gsum_done = sem("gsum_done")
        grcp_done = sem("grcp_done")
        probs_done = sem("probs_done")
        rows_stored = sem("rows_stored")
        h2_stored = sem("h2_stored")
        h2s_done = sem("h2s_done")
        dve_passed = sem("dve_passed")
        pool_passed = sem("pool_passed")
        rc_loaded = sem("rc_loaded")
        sw_loaded = sem("sw_loaded")
        rc_ready = sem("rc_ready")
        sw_hi = sem("sw_hi")
        sw_split = sem("sw_split")
        ew_hi = sem("ew_hi")
        ew_split = sem("ew_split")
        b2_split = sem("b2_split")
        pm_mm = sem("pm_mm")
        bits_done = sem("bits_done")
        key_step = sem("key_step")
        cand_ready = sem("cand_ready")
        hits_done = sem("hits_done")
        count_mm = sem("count_mm")
        bounds_done = sem("bounds_done")
        sh1_mm = sem("sh1_mm")
        sh_gelu = sem("sh_gelu")
        sh_hi = sem("sh_hi")
        sh_lo_pool = sem("sh_lo_pool")
        sh_lo_dve = sem("sh_lo_dve")
        sh2_mm = sem("sh2_mm")
        h2b_loaded = sem("h2b_loaded")
        fin_done = sem("fin_done")
        out_stored = sem("out_stored")
        thr_wide_done = sem("thr_wide_done")
        thr_mm = sem("thr_mm")
        thr_done = sem("thr_done")
        masks_done = sem("masks_done")
        scans_done = sem("scans_done")
        prefix_mm = sem("prefix_mm")
        pos_done = sem("pos_done")
        digits_done = sem("digits_done")
        dig_b_done = sem("dig_b_done")
        hotA_done = sem("hotA_done")
        numbered = sem("numbered")
        numbered_dve = sem("numbered_dve")
        hotB_done = sem("hotB_done")
        lists_mm = sem("lists_mm")
        picked_done = sem("picked_done")
        lists_done = sem("lists_done")
        lists_loaded = sem("lists_loaded")
        idx_mm = sem("idx_mm")
        idx_done = sem("idx_done")
        gidx_copied = sem("gidx_copied")
        added = sem("added")
        eX_mm = sem("eX_mm")
        eX_hi = sem("eX_hi")
        eX_split = sem("eX_split")
        eh_mm = sem("eh_mm")
        eh_gelu = sem("eh_gelu")
        eh_hi = sem("eh_hi")
        eh_split = sem("eh_split")
        ey_mm = sem("ey_mm")
        ey_scaled = sem("ey_scaled")
        w1_loaded, w2_loaded = ([sem(f"{n}_loaded{i}") for i in range(MS)] for n in ("w1", "w2"))
        estage_loaded = [sem(f"estage_loaded{i}") for i in range(2)]
        gathered = [[sem(f"gathered{i}{h}") for h in range(2)] for i in range(RING)]
        scattered = [sem(f"scattered{h}") for h in range(2)]

        def past(group, n=1):
            return not isinstance(group, int) or group >= n

        def col(c0, n=1):
            return vec[:, c0:c0 + n]

        block = ctx.enter_context(nc.Block())

        PLACES = KH + 2 * MS
        ATTN_STEPS = 14
        AFTER = {2: [0], 3: [1], 5: [2], 6: [3], 7: [4], 8: [5], 9: [6], 11: [7], 12: [8], 13: [9], 14: [10], 16: [11],
                 17: [12], 18: [13]}

        PREP = KH - MS

        def mix_step_of(p):
            return (p - KH) // 2, (p - KH) % 2 == 1

        def schedule(eng, tok, attn):
            for p in range(PLACES):
                tok(0, p)
            with eng.Fori(1, GROUPS - 1) as g:
                for p in range(PLACES):
                    tok(g, p)
                    for s in AFTER.get(p, []):
                        attn(g - 1, s)
            for p in range(PLACES):
                tok(GROUPS - 1, p)
                for s in AFTER.get(p, []):
                    attn(GROUPS - 2, s)
            for s in range(ATTN_STEPS):
                attn(GROUPS - 1, s)

        MIX_STEPS = 1 + 3 * (MS - 1) + 1

        def mix_after(m):
            return 1 + 3 * m if m >= -1 else -1

        SPAN = PHASES * DIGIT // (GROUPS - EARLY)
        expert_turn = [0]

        def expert_steps(eng, step):
            for k in range(3):
                step(k, k % RING)
            with eng.Fori(0, (EXPERTS - 5) // RING) as i:
                expert_turn[0] = i
                for q in range(RING):
                    step(i * RING + q + 3, (q + 3) % RING)
            for k in range(3 + (EXPERTS - 5) // RING * RING, EXPERTS + 2):
                step(k, k % RING)

        def ring_use(k, q):
            if isinstance(k, int):
                return k // RING + 1
            return expert_turn[0] + (2 if q < 3 else 1)

        def bank_of_x(g, m):
            return (Q + [X])[m] if not past(g) else X

        def flat(v):
            return v.rearrange("p e t -> p (e t)")

        numbers = rc[0:TT, RCOLUMNS["token"]]
        ACT_TILES = TILES * 7 // 12

        NSMALL = [0]
        ZEROED = 5

        @block.sync
        def _(sp):
            def load_x(g):
                src = x[bass.ds(g * GB, GB)].rearrange("b (t m) c -> (b t) (m c)", m=MS)
                sp.dma_start(x_tok[:], src.rearrange("(k p) n -> p k n", p=TT)).then_inc(x_loaded, 16)

            sp.dma_start(ident, a["constants"][:, COLUMNS["ident"]]).then_inc(ident_loaded, 16)
            load_x(0)
            w1 = a["L0_tok_w1"].rearrange("(c m) n -> c m n", m=MS)
            for n in range(MS):
                sp.dma_start(stage1[:, n], w1[:, :, n * W1_COLS:(n + 1) * W1_COLS]).then_inc(w1_loaded[n], 16)

            def small(dst, src):
                NSMALL[0] += 1
                sp.dma_start(dst, src).then_inc(small_loaded, 16)

            rest = slice(COLUMNS["ident"].stop, N_COLUMNS)
            sp.dma_start(const[:, rest], a["constants"][:, rest]).then_inc(const_loaded, 16)
            small(fc_w[:], a["L0_tok_fc_w"])
            small(fcb_bc[:], a["L0_tok_fc_b"].partition_broadcast(TT))
            small(lng_bc[:], a["L0_tok_ln_g"].partition_broadcast(TT))
            small(lnb_bc[:], a["L0_tok_ln_b"].partition_broadcast(TT))
            small(ob_bc[:], a["L0_attn_o_b"].partition_broadcast(TT))
            small(scala[:], a["L0_attn_scala"].partition_broadcast(TT))
            for p in (0, LO_ROW):
                small(vb_row[p:p + 1, :], a["L0_attn_v_b"].rearrange("(a n) -> a n", a=1))
            small(vtB[:, 0, :], a["L0_attn_v_b"].partition_broadcast(CHUNK))
            small(wst[:, 0:2, :], a["L0_attn_u_w"].rearrange("(e p) d -> p e d", p=128))
            small(wst[:, 2:4, :], a["L0_attn_v_w"].rearrange("(e p) d -> p e d", p=128))
            small(wst[:, 4, :], a["L0_attn_base_w"])
            small(wst[0:64, 5, :], a["L0_attn_base_w"][64:128, :])
            small(wst[64:128, 5, :], a["L0_attn_base_w"][0:64, :])
            small(wst[:, 6:8, :], a["L0_attn_o_w"].rearrange("d (e p) -> d e p", e=2))

            def load_next(g):
                sp.wait_ge(xT_mm, (g + 1) * MS)
                load_x(g + 1)

            load_next(0)
            w2 = a["L0_tok_w2"].rearrange("(k p) n -> p k n", p=128)
            for n in range(MS):
                sp.wait_ge(w1_split, n + 1)
                sp.dma_start(stage2[:, 2 * n:2 * n + 2, :], w2[:, 2 * n:2 * n + 2, :]).then_inc(w2_loaded[n], 16)
            small(gate_w[:], a["L0_ffn_gate_w"])
            small(sb2_bc[:], a["L0_ffn_sb2"].partition_broadcast(TT))
            small(b2st[0:EXPERTS, :], a["L0_ffn_b2"])
            small(b2st[LO_ROW:LO_ROW + EXPERTS, :], a["L0_ffn_b2"])
            for i, n in enumerate(("qq_w", "qq_b", "qk_w", "qk_b", "lq_w", "lq_b", "lk_w", "lk_b")):
                small(vrows[i:i + 1, :], a["L0_attn_" + n])
            small(vrows[V_BASE:V_BASE + 1, :], a["L0_attn_base_b"].rearrange("(a n) -> a n", a=1))
            small(vrows[V_U:V_U + 2, :], a["L0_attn_u_b"].rearrange("(a n) -> a n", n=128))
            small(vrows[V_SB1:V_SB1 + KF, :], a["L0_ffn_sb1"].rearrange("(a n) -> a n", n=128))
            small(vrows[V_B1:N_VEC, :], a["L0_ffn_b1"].rearrange("e (a n) -> (e a) n", n=128))
            first = MAXPOS - CHUNK
            wv = a["L0_attn_w"]
            window = bass.AP(wv.tensor, first, [[1, CHUNK], [1, CHUNK]])
            small(zw[:, 0:CHUNK], window)
            small(zw[:, CHUNK:A_TOK], window)

            def store(a_):
                sp.wait_ge(h2s_done, a_ + 1)
                sp.dma_start(h2_dram[bass.ds(a_ * TPG, TPG)].rearrange("k p n -> p k n"), h2s[:]).then_inc(h2_stored, 16)
                sp.wait_ge(probs_done, a_ + 1)
                sp.dma_start(rows_dram[bass.ds(a_ * TPG, TPG)].rearrange("k p n -> p k n"), rows[:]).then_inc(rows_stored, 16)

            with sp.Fori(1, GROUPS - 1) as g:
                load_next(g)
                store(g - 1)

            def load_chunk(c):
                if c >= 2:
                    sp.wait_ge(ew_split, c - 1)
                e = slice(c % (EXPERTS // EC) * EC, (c % (EXPERTS // EC) + 1) * EC)
                if c < EXPERTS // EC:
                    src = a["L0_ffn_w1"][e].rearrange("e p n -> p e n")
                    dst = estage[c % 2].rearrange("p (e n) -> p e n", e=EC)
                else:
                    src = a["L0_ffn_w2"][e].rearrange("e (j p) n -> p (e j) n", p=128)
                    dst = estage[c % 2].rearrange("p (k n) -> p k n", k=EC * KF)
                sp.dma_start(dst, src).then_inc(estage_loaded[c % 2], 16)

            sp.wait_ge(xT_mm, GROUPS * MS)
            sp.dma_start(rc, a["routing"]).then_inc(rc_loaded, 16)
            sp.wait_ge(w2_split, MS)
            load_chunk(0)
            store(GROUPS - 2)
            sp.wait_ge(mix_mm, GROUPS * MS)
            sp.dma_start(sw_stage[:, 0, :], a["L0_ffn_sw1"]).then_inc(sw_loaded, 16)
            sp.dma_start(sw_stage[:, 1, :].rearrange("p (j n) -> p j n", j=KF), a["L0_ffn_sw2"].rearrange("(j p) n -> p j n", p=128))\
                .then_inc(sw_loaded, 16)
            sp.wait_ge(pooled_done, GROUPS)
            load_chunk(1)

            def load_h2(i):
                sp.dma_start(h2b, h2_dram[bass.ds(i * TPG, TPG)].rearrange("k p n -> p k n")).then_inc(h2b_loaded, 16)

            def store_out(i):
                sp.wait_ge(fin_done, i + 1)
                sp.dma_start(out[bass.ds(i * TPG * TT, TPG * TT)].rearrange("(k p) n -> p k n", p=TT), fin).then_inc(out_stored, 16)

            sp.wait_ge(h2_stored, 16 * GROUPS)
            sp.wait_ge(xn_done, GROUPS)
            load_h2(0)
            for c in (2, 3, 4):
                load_chunk(c)
            for i in range(EARLY - 1):
                store_out(i)
                load_h2(i + 1)
            load_chunk(5)
            store(GROUPS - 1)
            sp.wait_ge(rows_stored, 16 * (GROUPS + 1))
            sp.wait_ge(h2_stored, 16 * (GROUPS + 1))
            load_chunk(6)
            with sp.Fori(EARLY - 1, GROUPS - 1) as i:
                store_out(i)
                load_h2(i + 1)
            load_chunk(7)
            store_out(GROUPS - 1)
            sp.wait_ge(lists_done, 1)
            for h in range(2):
                sp.dma_start(lists[h * HALF_E:(h + 1) * HALF_E, :].rearrange("e (a b) -> e a b", a=DIG_A),
                             lists_f[:, h, :]).then_inc(lists_loaded, 16)

        @block.gpsimd
        def _(pool):
            pool.memset(mhalf[:], -0.5).then_inc(ones_done, 1)
            pool.memset(ones16[:], 1.0).then_inc(ones_done, 1)
            pool.memset(b2hl[:], 0.0).then_inc(ones_done, 1)
            pool.memset(vb16[:], 0.0).then_inc(ones_done, 1)
            pool.memset(enough_by[:], 2.0 ** 10).then_inc(ones_done, 1)
            pool.wait_ge(ones_done, ZEROED)
            pool.wait_ge(small_loaded, 16 * NSMALL[0])

            def tok(g, p):
                pass

            POOL_STEPS = 4

            def low_part(c, halves=(0, 1)):
                for i in halves:
                    n = slice(i * EC * FF // 2, (i + 1) * EC * FF // 2)
                    pool.wait_ge(ew_hi, c + 1)
                    ins = pool.tensor_tensor(chunk(1, c)[:, n], estage[c % 2][:, n], chunk(0, c)[:, n], ALU.subtract)
                    if i == 1:
                        ins.then_inc(ew_split, 1)

            def shared_low(g):
                for j in range(0, KF, 2):
                    pool.wait_ge(sh_hi, g * KF + j + 1)
                    pool.tensor_tensor(shl[:, j], sh32[:, j], shh[:, j], ALU.subtract).then_inc(sh_lo_pool, 1)

            def last(s):
                if s == 0:
                    low_part(0, (0,))
                if s == 2:
                    low_part(0, (1,))
                    pool.wait_ge(sw_hi, 1)
                    pool.tensor_tensor(sw1l, sw_stage[:, 0, :], sw1h, ALU.subtract)
                    pool.tensor_tensor(sw[:, 3, :], sw_stage[:, 1, :], sw[:, 2, :], ALU.subtract).then_inc(sw_split, 1)
                if s in (3, 4):
                    low_part(s - 2)
                if s == 5:
                    shared_low(0)
                    low_part(3)
                if s == 11:
                    shared_low(1)
                    low_part(4)

            def attn(a_, s):
                if isinstance(a_, int) and a_ == GROUPS - 1:
                    last(s)
                n = [0]

                def step(ins):
                    ins.then_inc(pool_step, 1)
                    n[0] += 1
                    pool.wait_ge(pool_step, a_ * POOL_STEPS + base + n[0])

                if s == 0:
                    base = 0
                    pool.wait_ge(ln1_stats, a_ + 1)
                    pool.sem_inc(pool_passed, 1)
                    step(pool.tensor_scalar(pst[:, 0, :], mv[:, 0, :, 1], EPS, None, ALU.add))
                    pool.tensor_tensor(pst[:, 1, :], pst[:, 0, :], mhalf[:], ALU.pow).then_inc(ln1_rstd, 1)
                if s == 1:
                    base = 1
                    pool.wait_ge(ln2_stats, a_ + 1)
                    pool.sem_inc(pool_passed, 1)
                    step(pool.tensor_scalar(pst[:, 2, :], mv[:, 1, :, 1], 1 + EPS, EPS * EPS, ALU.mult, ALU.add))
                    step(pool.tensor_tensor(pst[:, 5, :], pst[:, 2, :], mhalf[:], ALU.pow))
                    pool.tensor_tensor(pst[:, 6, :], pst[:, 5, :], scala[:, 0:1].broadcast_to([TT, TPG]), ALU.mult).then_inc(ln2_r, 1)
                    pool.wait_ge(h1_done, a_ + 1)
                    pool.tensor_tensor(h1ob[:], h1[:], ob_bc[:].unsqueeze(1).broadcast_to([TT, TPG, 128]), ALU.add)\
                        .then_inc(h1ob_done, 1)
                if s == 10:
                    base = 3
                    pool.wait_ge(ln3_stats, a_ + 1)
                    pool.sem_inc(pool_passed, 1)
                    step(pool.tensor_scalar(pst[:, 7, :], mv[:, 2, :, 1], EPS, None, ALU.add))
                    pool.tensor_tensor(pst[:, 7, :], pst[:, 7, :], mhalf[:], ALU.pow).then_inc(ln3_rstd, 1)
                    pool.wait_ge(h2_done, a_ + 1)
                    pool.wait_ge(h2_stored, 16 * (a_ + 1))
                    pool.tensor_tensor(h2s[:], h2[:], sb2_bc[:].unsqueeze(1).broadcast_to([TT, TPG, 128]), ALU.add)\
                        .then_inc(h2s_done, 1)

            schedule(pool, tok, attn)

            with pool.Fori(EARLY, GROUPS) as i:
                shared_low(i)

            for c in (5, 6, 7):
                low_part(c)

            table = rows_dram.rearrange("k p n -> (k p) n")

            def gather(e, q):
                pool.wait_ge(gidx_copied, e + 1)
                pool.sem_inc(pool_passed, 1)
                for h in range(2):
                    pool.indirect_dma_start(gath[q][:, h, :], None, table,
                                            bass.IndirectOffsetOnAxis(ap=gidx[q][:, h:h + 1], axis=0))\
                        .then_inc(gathered[q][h], 16)

            def scatter(e, q):
                pool.wait_ge(ey_scaled, e + 1)
                if past(e):
                    pool.wait_ge(scattered[0], 16 * e)
                    pool.wait_ge(scattered[1], 16 * e)
                pool.sem_inc(added, 1)
                for h in range(2):
                    pool.indirect_dma_start(out, bass.IndirectOffsetOnAxis(ap=sidx[q][:, h:h + 1], axis=0), ey[q][:, h, :], None,
                                            compute_op=ALU.add).then_inc(scattered[h], 16)

            for e in range(LEAD):
                gather(e, e)

            def step(k, q):
                if not isinstance(k, int) or k + LEAD < EXPERTS:
                    gather(k + LEAD, (q + LEAD) % RING)
                if isinstance(k, int) and k == 1:
                    pool.wait_ge(out_stored, 16 * GROUPS)
                if past(k, 2):
                    scatter(k - 2, (q + 2) % RING)

            expert_steps(pool, step)
            pool.wait_ge(scattered[0], 16 * EXPERTS)
            pool.wait_ge(scattered[1], 16 * EXPERTS)

        @block.scalar
        def _(act):
            def prep(g, m):
                act.wait_ge(xT_mm, g * MS + m + 1)
                if past(g):
                    act.wait_ge(xu_done, g)
                act.activation(xp32[:, m, :], bank_of_x(g, m)[:, 0:GT], ACT.Copy).then_inc(xT_copied, 1)

            for m in range(MS):
                prep(0, m)
            for n in range(MS):
                act.wait_ge(w1_loaded[n], 16)
                act.activation(w1h[:, :, n * W1_COLS:(n + 1) * W1_COLS], stage1[:, n], ACT.Copy, scale=SCALE)\
                    .then_inc(w1_hi, 1)

            def setup():
                act.wait_ge(setup_mm, 1)
                act.activation(wTh[:, 0:4, :], Q[0][:].rearrange("p (k n) -> p k n", k=4), ACT.Copy).then_inc(setup_copy, 1)
                act.wait_ge(setup_mm, 2)
                act.activation(wTh[:, 4:6, :], Q[1][:, 0:256].rearrange("p (k n) -> p k n", k=2), ACT.Copy)
                act.activation(oT_w[:], Q[1][:, 256:512].rearrange("p (k n) -> p k n", k=2), ACT.Copy).then_inc(setup_copy, 1)
                act.wait_ge(setup_mm, 3)
                act.activation(vec[:], Q[2][:, 0:N_VEC], ACT.Copy).then_inc(setup_copy, 1)
                act.wait_ge(setup_mm, 4)
                act.activation(vswap[:], Q[3][:, 0:V_U], ACT.Copy).then_inc(setup_copy, 1)
                act.wait_ge(setup_copy, 4)
                act.activation(padv[:, 0:1], col(V_BASE), ACT.Tanh, scale=0.5).then_inc(setup_copy, 1)
                act.activation(padv[:, 1:2], vswap[:, V_BASE:V_BASE + 1], ACT.Tanh, scale=0.5).then_inc(setup_copy, 1)
                act.wait_ge(small_loaded, 16 * NSMALL[0])
                act.activation(vtB[:, 1, :], vtB[:, 0, :], ACT.Tanh, scale=0.5).then_inc(setup_copy, 1)
                act.activation(halfb[:, 0:1], col(V_BASE), ACT.Copy, scale=0.5)
                act.activation(halfb[:, 1:2], vswap[:, V_BASE:V_BASE + 1], ACT.Copy, scale=0.5)
                act.activation(halfb[:, 2:4], col(V_U, 2), ACT.Copy, scale=0.5).then_inc(setup_copy, 1)

            def shared(g, banks):
                for j in range(KF):
                    if j == 0 and past(g):
                        act.wait_ge(sh_lo_pool, g * KF // 2)
                        act.wait_ge(sh_lo_dve, g * KF // 2)
                    act.wait_ge(sh1_mm, g * KF + j + 1)
                    act.activation(sh32[:, j, :], banks[j][:, 0:GT], ACT.Gelu_apprx_tanh, bias=col(V_SB1 + j)).then_inc(sh_gelu, 1)
                for j in range(KF):
                    if j == 0 and past(g):
                        act.wait_ge(sh2_mm, g)
                    act.wait_ge(sh_gelu, g * KF + j + 1)
                    act.activation(shh[:, j], sh32[:, j], ACT.Copy).then_inc(sh_hi, 1)

            def high_part(c):
                act.wait_ge(estage_loaded[c % 2], 16 * (c // 2 + 1))
                act.activation(chunk(0, c), estage[c % 2], ACT.Copy).then_inc(ew_hi, 1)

            def last(s):
                if s == 0:
                    act.wait_ge(mix_mm, GROUPS * MS)
                    high_part(0)
                    act.wait_ge(rc_loaded, 16)
                    act.wait_ge(ones_done, ZEROED)
                    act.wait_ge(small_loaded, 16 * NSMALL[0])
                    act.activation(same16[:], rc[:, RCOLUMNS["same_expert"]], ACT.Copy)
                    act.activation(enough16[:], rc[0:TT, RCOLUMNS["enough"]], ACT.Copy)
                    act.activation(before16[:], rc[0:TT, RCOLUMNS["before"]], ACT.Copy)
                    act.activation(pickb[:], rc[:, RCOLUMNS["pick_b2"]], ACT.Copy)
                    act.activation(b2hl[0:EXPERTS, :], b2st[0:EXPERTS, :], ACT.Copy)
                    act.activation(b2t[LO_ROW:LO_ROW + EXPERTS, :], b2st[LO_ROW:LO_ROW + EXPERTS, :], ACT.Copy).then_inc(rc_ready, 1)
                    act.wait_ge(sw_loaded, 32)
                    act.wait_ge(pooled_done, GROUPS)
                    act.activation(sw1h, sw_stage[:, 0, :], ACT.Copy)
                    act.activation(sw[:, 2, :], sw_stage[:, 1, :], ACT.Copy).then_inc(sw_hi, 1)
                if s == 3:
                    high_part(1)
                if s == 6:
                    high_part(2)
                if s == 8:
                    act.wait_ge(u_done, GROUPS * 2)
                    shared(0, T + [X])
                if s == 9:
                    high_part(3)
                    shared(1, T + [X])
                if s == 10:
                    high_part(4)

            w2_now = [0]

            def tok(g, p):
                if isinstance(g, int) and p >= KH - MS and w2_now[0] < MS:
                    n = w2_now[0]
                    w2_now[0] += 1
                    act.wait_ge(w2_loaded[n], 16)
                    for k in (2 * n, 2 * n + 1):
                        ins = act.activation(w2h[:, k], stage2m[:, k], ACT.Copy, scale=SCALE)
                    ins.then_inc(w2_hi, 1)
                if isinstance(g, int) and g == 0 and p == KH:
                    setup()
                if p < KH:
                    act.wait_ge(hid_mm, g * KH + p + 1)
                    act.activation(hidh[:, p, :], T[p % 3][:, 0:GT], ACT.Relu).then_inc(hid_hi, 1)
                    if p == PREP - 1:
                        act.wait_ge(xT_copied, (g + 1) * MS)
                        if past(g):
                            act.wait_ge(pooled_done, g)
                        act.activation(xu32, xp32, ACT.Copy).then_inc(xu_done, 1)
                    if p >= PREP and not (isinstance(g, int) and g == GROUPS - 1):
                        prep(g + 1, p - PREP)
                    return
                m, second = mix_step_of(p)
                if second:
                    act.wait_ge(mix_mm, g * MS + m + 1)
                    act.activation(mtanh[:, m % 2, :], T[(KH + m) % 3][:, 0:GT], ACT.Tanh, scale=0.5 / SCALE ** 2)\
                        .then_inc(mix_tanh, 1)
                    act.wait_ge(mix_tanh, g * MS + m + 1)
                    if past(g) or m >= 2:
                        act.wait_ge(mix_step, g * MIX_STEPS + mix_after(m - 2))
                    act.activation(mexp[:, m % 2, :], mtanh[:, m % 2, :], ACT.Exp, scale=0.5).then_inc(mix_exp, 1)

            def attn(a_, s):
                if isinstance(a_, int) and a_ == GROUPS - 1:
                    last(s)
                if s == 3:
                    act.wait_ge(xnT_mm, a_ + 1)
                    act.activation(xnh, Q[0][:, 0:GT], ACT.Copy).then_inc(xnT_copied, 1)
                if s in (4, 5):
                    for i in ((0, 1) if s == 4 else (2, 3)):
                        bank_ = Q[(1, 2, 3, 0)[i]]
                        bias = (col(V_BASE), vswap[:, V_BASE:V_BASE + 1], col(V_U), col(V_U + 1))[i]
                        act.wait_ge(proj_mm, a_ * 4 + i + 1)
                        if i >= 2:
                            act.wait_ge(base_done, a_ * 2 + i - 1)
                        act.activation(ptanh[:, i % 2, :], bank_[:, 0:GT], ACT.Tanh, bias=halfb[:, i:i + 1], scale=0.5)
                        act.activation(pz[:, i, :], bank_[:, 0:GT], ACT.Identity, bias=bias).then_inc(proj_z, 1)
                if s == 6:
                    act.wait_ge(v_mm, a_ * 2 + 1)
                    act.activation(vtA[:], Q[1][:].rearrange("p (b n) -> p b n", b=GB), ACT.Tanh, scale=0.5)\
                        .then_inc(v_tanh, 1)
                    act.wait_ge(v_mm, a_ * 2 + 2)
                    act.activation(vtB[0:B_TOK], Q[2][0:B_TOK, :].rearrange("p (b n) -> p b n", b=GB), ACT.Tanh, scale=0.5)\
                        .then_inc(v_tanh, 1)
                    act.wait_ge(lkT_mm, a_ + 1)
                    q3 = Q[3][:].rearrange("p (k b n) -> p k b n", k=2, b=GB)
                    act.activation(lkA[:], q3[:, 0], ACT.Copy)
                    act.activation(lkB[:], q3[0:CHUNK, 1], ACT.Copy).then_inc(lk_copied, 1)
                if s == 8:
                    act.wait_ge(linkv_mm, a_ + 1)
                    act.activation(linkv[:], Q[1][:].rearrange("p (b n) -> p b n", b=GB), ACT.Copy, scale=1.0 / CHUNK)\
                        .then_inc(linkv_done, 1)
                if s == 12:
                    act.wait_ge(n2T_mm, a_ + 1)
                    act.activation(n2T[:], Q[1][:, 0:GT], ACT.Copy).then_inc(n2T_copied, 1)
                if s == 13:
                    act.wait_ge(lg_done, a_ + 1)
                    act.activation(pexp[:], lg[:], ACT.Exp).then_inc(lexp_done, 1)

            schedule(act, tok, attn)

            act.wait_ge(probs_done, GROUPS)
            shared(EARLY, Q[:3] + [X])
            with act.Fori(EARLY + 1, GROUPS) as i:
                shared(i, Q)
            for c in (5, 6):
                high_part(c)

            act.wait_ge(digits_done, 1)
            act.activation(flat(dig_b), flat(dig_bi), ACT.Copy).then_inc(dig_b_done, 1)
            act.wait_ge(hotA_done, 1)
            for t in range(ACT_TILES):
                act.activation(hotA[:, :, :, t], hotA[:, :, :, t], ACT.Copy, scale=numbers[:, t:t + 1]).then_inc(numbered, 1)
            high_part(7)

            def step(k, q):
                if not isinstance(k, int) or 1 <= k <= EXPERTS:
                    e, r2 = k - 1, (q + 1) % 2
                    if past(e):
                        act.wait_ge(eh_split, e)
                    for j in range(KF):
                        act.wait_ge(eh_mm, 2 * e + j // 2 + 1)
                        bias = vec[:, bass.ds(V_B1 + e * KF + j, 1)]
                        ins = act.activation(eh32[:, r2, j * CAP:(j + 1) * CAP], Q[2 * r2 + j // 2][:, j % 2 * CAP:(j % 2 + 1) * CAP],
                                             ACT.Gelu_apprx_tanh, bias=bias)
                    ins.then_inc(eh_gelu, 1)

            expert_steps(act, step)

        @block.tensor
        def _(pe):
            def transposes(dst, src, n=TPG):
                for k in range(n):
                    ins = pe.transpose(dst[:, k * TT:(k + 1) * TT], src(k), ident[0:TT, 0:TT])
                return ins

            def prep(g, m):
                pe.wait_ge(x_loaded, 16 * (g + 1))
                if past(g):
                    pe.wait_ge(xT_copied, g * MS + m)
                if m == 0 and past(g, 2):
                    pe.wait_ge(ln1_stats, g - 1)
                transposes(bank_of_x(g, m), lambda k: x_tok[:, k, m * C:(m + 1) * C]).then_inc(xT_mm, 1)

            def setup():
                pe.wait_ge(const_loaded, 16)
                pe.wait_ge(small_loaded, 16 * NSMALL[0])
                for k in range(8):
                    ins = pe.transpose(Q[k // 4][:, (k % 4) * 128:(k % 4 + 1) * 128], wst[:, k, :], ident)
                    if k % 4 == 3:
                        ins.then_inc(setup_mm, 1)
                pe.transpose(Q[2][:, 0:N_VEC], vrows, ident[0:N_VEC, 0:N_VEC]).then_inc(setup_mm, 1)
                pe.wait_ge(setup_copy, 3)
                pe.matmul(Q[3][:, 0:V_U], swap_m, vec[:, 0:V_U], start=True, stop=True).then_inc(setup_mm, 1)
                pe.wait_ge(xT_copied, 2 * MS)
                pe.matmul(X[:, 0:CHUNK], zw[:], anti, start=True, stop=True).then_inc(setup_mm, 1)

            pe.wait_ge(ident_loaded, 16)
            for m in range(MS):
                prep(0, m)

            def tok(g, p):
                if isinstance(g, int) and g == 0 and p == KH:
                    setup()
                if p < KH:
                    dst = T[p % 3][:, 0:GT]
                    if p < 3 and past(g):
                        pe.wait_ge(mix_tanh, g * MS + p - 2)
                    if p >= 3:
                        pe.wait_ge(hid_lo, g * KH + p - 2)
                    if isinstance(g, int) and g == 0:
                        pe.wait_ge(w1_split, p // 2 + 1)
                    n = slice(p * 128, (p + 1) * 128)
                    for m in range(MS):
                        if p == 0:
                            pe.wait_ge(xl_done, g * MS + m + 1)
                        pe.matmul(dst, w1h[:, m, n], xh[:, m, :], start=(m == 0), stop=False)
                        pe.matmul(dst, w1h[:, m, n], xl[:, m, :], start=False, stop=False)
                        ins = pe.matmul(dst, w1l[:, m, n], xh[:, m, :], start=False, stop=(m == MS - 1))
                    ins.then_inc(hid_mm, 1)
                    if p >= PREP and not (isinstance(g, int) and g == GROUPS - 1):
                        prep(g + 1, p - PREP)
                    return
                m, second = mix_step_of(p)
                dst = T[(KH + m) % 3][:, 0:GT]
                if not second and m >= 3:
                    pe.wait_ge(mix_tanh, g * MS + m - 2)
                for k in range(KH // 2, KH) if second else range(KH // 2):
                    if isinstance(g, int) and g == 0 and m == 0:
                        pe.wait_ge(w2_split, k // 2 + 1)
                    if m == 0:
                        pe.wait_ge(hid_lo, g * KH + max(k + 1, KH - 2))
                    pe.matmul(dst, w2h[:, k, m, :], hidh[:, k, :], start=(k == 0), stop=False)
                    pe.matmul(dst, w2h[:, k, m, :], hidl[:, k, :], start=False, stop=False)
                    ins = pe.matmul(dst, w2l[:, k, m, :], hidh[:, k, :], start=False, stop=(k == KH - 1))
                if second:
                    ins.then_inc(mix_mm, 1)

            def first_layer(g, js, banks):
                toks = bass.ds(g * GT, GT)
                for j in js:
                    if past(g):
                        pe.wait_ge(sh_gelu, (g - 1) * KF + j + 1)
                    n = slice(j * 128, (j + 1) * 128)
                    pe.matmul(banks[j][:, 0:GT], sw1h[:, n], n2h[:, toks], start=True, stop=False)
                    pe.matmul(banks[j][:, 0:GT], sw1h[:, n], n2l[:, toks], start=False, stop=False)
                    pe.matmul(banks[j][:, 0:GT], sw1l[:, n], n2h[:, toks], start=False, stop=True).then_inc(sh1_mm, 1)

            def second_layer(g, ks, bank_):
                if 0 in ks:
                    pe.wait_ge(sh_lo_pool, (g + 1) * KF // 2)
                    pe.wait_ge(sh_lo_dve, (g + 1) * KF // 2)
                    if past(g):
                        pe.wait_ge(fin_done, g)
                for k in ks:
                    o = bank_[0:TT, k * 128:(k + 1) * 128]
                    t = slice(k * TT, (k + 1) * TT)
                    for j in range(KF):
                        pe.matmul(o, shh[:, j, t], sw2h[:, j, :], start=(j == 0), stop=False)
                        pe.matmul(o, shl[:, j, t], sw2h[:, j, :], start=False, stop=False)
                        ins = pe.matmul(o, shh[:, j, t], sw2l[:, j, :], start=False, stop=(j == KF - 1))
                if TPG - 1 in ks:
                    ins.then_inc(sh2_mm, 1)

            def last(s):
                if s == 7:
                    pe.wait_ge(sw_split, 1)
                    first_layer(0, range(KF), T + [X])
                if s == 9:
                    first_layer(1, range(KF), T + [X])
                if s == 11:
                    second_layer(0, range(TPG), Q[3])

            def attn(a_, s):
                if isinstance(a_, int) and a_ == GROUPS - 1:
                    last(s)
                if s == 0:
                    pe.wait_ge(pooled_done, a_ + 1)
                    pe.wait_ge(xT_copied, (a_ + 2) * MS if not (isinstance(a_, int) and a_ == GROUPS - 1) else GROUPS * MS)
                    for k in range(TPG):
                        ins = pe.matmul(X[0:TT, k * 128:(k + 1) * 128], pooled[:, k * TT:(k + 1) * TT], fc_w[:], start=True, stop=True)
                    ins.then_inc(fc_mm, 1)
                if s == 3:
                    pe.wait_ge(xn_done, a_ + 1)
                    transposes(Q[0], lambda k: xn[:, k, :]).then_inc(xnT_mm, 1)
                if s in (4, 5):
                    pe.wait_ge(xnT_low, a_ + 1)
                    for i in ((0, 1) if s == 4 else (2, 3)):
                        k = (4, 5, 0, 1)[i]
                        o = Q[(1, 2, 3, 0)[i]][:, 0:GT]
                        pe.matmul(o, wTh[:, k, :], xnh, start=True, stop=False)
                        pe.matmul(o, wTh[:, k, :], xnl, start=False, stop=False)
                        pe.matmul(o, wTl[:, k, :], xnh, start=False, stop=True).then_inc(proj_mm, 1)
                if s == 6:
                    pe.wait_ge(proj_z, a_ * 4 + 4)
                    vh, vl = (v[:, 2:4, :].rearrange("p k n -> p (k n)") for v in (wTh, wTl))
                    for bank_, first, rows_ in ((Q[1], 0, A_TOK), (Q[2], A_TOK, B_TOK)):
                        for b in range(GB):
                            t = slice(b * TW + first, b * TW + first + rows_)
                            o = bank_[0:rows_, b * E:(b + 1) * E]
                            pe.matmul(o, xnh[:, t], vh, start=True, stop=False)
                            pe.matmul(o, xnl[:, t], vh, start=False, stop=False)
                            pe.matmul(o, xnh[:, t], vl, start=False, stop=False)
                            ins = pe.matmul(o, ones16[0:LO_ROW + 1, 0:rows_], vb16[:], start=False, stop=True)
                        ins.then_inc(v_mm, 1)
                    pe.wait_ge(head_done, a_ * 4 + 1)
                    for b in range(GB):
                        pe.transpose(Q[3][:, b * 128:(b + 1) * 128], qT["lk"][:, b, 0:A_TOK], ident)
                        ins = pe.transpose(Q[3][0:CHUNK, (GB + b) * 128:(GB + b + 1) * 128], qT["lk"][:, b, A_TOK:PADDED], ident)
                    ins.then_inc(lkT_mm, 1)
                if s == 7:
                    pe.wait_ge(head_done, a_ * 4 + 4)
                    for b in range(GB):
                        pe.matmul(Q[0][:, b * A_TOK:(b + 1) * A_TOK], qT["qk"][:, b, 0:A_TOK], qT["qq"][:, b, 0:A_TOK],
                                  start=True, stop=True)
                        c0 = GB * A_TOK + b * B_TOK
                        ins = pe.matmul(Q[0][0:CHUNK, c0:c0 + B_TOK], qT["qk"][:, b, A_TOK:PADDED], qT["qq"][:, b, A_TOK:TW],
                                        start=True, stop=True)
                    ins.then_inc(qk_mm, 1)
                if s == 8:
                    pe.wait_ge(lk_copied, a_ + 1)
                    pe.wait_ge(v_done, a_ * 2 + 2)
                    for b in range(GB):
                        o = Q[1][:, b * E:(b + 1) * E]
                        pe.matmul(o, lkA[:, b, :], vA[:, b, :], start=True, stop=False)
                        ins = pe.matmul(o, lkB[:, b, :], vB[:, b, :], start=False, stop=True)
                    ins.then_inc(linkv_mm, 1)
                if s == 9:
                    pe.wait_ge(linkv_done, a_ + 1)
                    pe.wait_ge(kern_done, a_ + 1)
                    for i in range(2):
                        e = slice(i * 128, (i + 1) * 128)
                        for b in range(GB):
                            t0 = b * TW
                            o = Q[2 + i]
                            pe.matmul(o[:, t0:t0 + TW], linkv[:, b, e], qT["lq"][:, b, :], start=True, stop=False)
                            pe.matmul(o[:, t0:t0 + A_TOK], vA[:, b, e], kA[:, b, :], start=False, stop=False)
                            ins = pe.matmul(o[:, t0 + A_TOK:t0 + TW], vB[:, b, e], kB[:, b, :], start=False, stop=True)
                    ins.then_inc(ot_mm, 1)
                if s == 10:
                    pe.wait_ge(g_done, a_ + 1)
                    for k in range(TPG):
                        o = Q[0][0:TT, k * 128:(k + 1) * 128]
                        for i in range(2):
                            ins = pe.matmul(o, gT[:, i, k * TT:(k + 1) * TT], oT_w[:, i, :], start=(i == 0), stop=(i == 1))
                    ins.then_inc(out_mm, 1)
                if s == 12:
                    pe.wait_ge(n2_done, a_ + 1)
                    transposes(Q[1], lambda k: rows[:, k, 0:C]).then_inc(n2T_mm, 1)
                if s == 13:
                    pe.wait_ge(n2T_copied, a_ + 1)
                    for k in range(TPG):
                        ins = pe.matmul(Q[2][0:TT, k * EXPERTS:(k + 1) * EXPERTS], n2T[:, k * TT:(k + 1) * TT], gate_w[:],
                                        start=True, stop=True)
                    ins.then_inc(gate_mm, 1)

            schedule(pe, tok, attn)

            second_layer(1, range(TPG), Q[3])
            per_row = TILES // TPG
            pe.wait_ge(probs_done, GROUPS)
            for n in range(TPG):
                ins = pe.transpose(T[0][:, n * TT:(n + 1) * TT], probs[:, n * per_row:(n + 1) * per_row, :].rearrange("p k e -> p (k e)"),
                                   ident[0:TT, 0:TT])
            ins.then_inc(pm_mm, 1)

            def count(n):
                pe.wait_ge(cand_ready, n + 1)
                pe.matmul(T[1][:, 0:1], enough16[:], enough_by[:], start=True, stop=False)
                pe.wait_ge(hits_done, n + 1)
                pe.matmul(T[1][:, 0:1], same16[:], cnt[:], start=False, stop=True).then_inc(count_mm, 1)

            pe.wait_ge(rc_ready, 1)
            pe.wait_ge(n2_split, GROUPS)
            first_layer(EARLY, range(KF), Q[:3] + [X])
            pe.wait_ge(fin_done, EARLY)

            def search(i):
                g = i + EARLY
                more = not isinstance(i, int)
                count(i * SPAN)
                if more:
                    first_layer(g + 1, (0, 1), Q)
                count(i * SPAN + 1)
                if more:
                    first_layer(g + 1, (2, 3), Q)
                for k in range(TPG):
                    count(i * SPAN + 2 + k)
                    second_layer(g, (k,), X)

            with pe.Fori(0, GROUPS - EARLY - 1) as i:
                search(i)
            search(GROUPS - EARLY - 1)

            pe.wait_ge(thr_wide_done, 1)
            pe.transpose(T[2][0:TT, 0:128], thr_wide, ident).then_inc(thr_mm, 1)
            pe.wait_ge(masks_done, 1)
            pe.matmul(T[0][0:TT, 0:ET], before16[:], flat(over16), start=True, stop=False)
            pe.matmul(T[1][0:TT, 0:ET], before16[:], flat(tie16), start=True, stop=False)
            later = [T[n][0:TT, 0:ET].rearrange("p (e t) -> p e t", e=EXPERTS)[:, :, 1:TILES] for n in (0, 1)]
            pe.wait_ge(scans_done, 1)
            pe.matmul(later[0], ones16[0:TT, 0:TT], over_c[:, :, 0:TILES - 1], start=False, stop=True)
            pe.matmul(T[1][0:TT, 0:ET].rearrange("p (e t) -> p e t", e=EXPERTS), ones16[0:TT, 0:TT],
                      over_c[:, :, TILES - 1:TILES].broadcast_to([TT, EXPERTS, TILES]), start=False, stop=False)
            pe.wait_ge(scans_done, 2)
            pe.matmul(later[1], ones16[0:TT, 0:TT], tie_c[:, :, 0:TILES - 1], start=False, stop=True).then_inc(prefix_mm, 1)
            split = TILES // 2 - 1
            for tiles in (range(split), range(split, TILES)):
                for h in range(2):
                    pe.wait_ge(hotB_done, h + 1)
                    e = slice(h * HALF_E, (h + 1) * HALF_E)
                    o = Q[h][0:DIG_A * HALF_E, 0:DIG_B * HALF_E]
                    for t in tiles:
                        if h == 0 and t < ACT_TILES:
                            pe.wait_ge(numbered, t + 1)
                        if h == 0 and t >= ACT_TILES:
                            pe.wait_ge(numbered_dve, t - ACT_TILES + 1)
                        ins = pe.matmul(o, hotA[:, e, :, t].rearrange("p e a -> p (e a)"), hotB[:, :, e, t],
                                        start=(t == 0), stop=(t == TILES - 1))
                    if TILES - 1 in tiles:
                        ins.then_inc(lists_mm, 1)
            pe.wait_ge(lists_loaded, 32)
            for h in range(2):
                ins = pe.transpose(T[2][0:HC, h * EXPERTS:(h + 1) * EXPERTS], lists[:, h * HC:(h + 1) * HC], ident[0:EXPERTS, 0:EXPERTS])
            ins.then_inc(idx_mm, 1)

            def step(k, q):
                if not isinstance(k, int) or 1 <= k <= EXPERTS:
                    e, r2, slot = k - 1, (q + 1) % 2, (q + 3) % RING
                    pe.wait_ge(eX_split, e + 1)
                    for j in range(KF):
                        o = Q[2 * r2 + j // 2][:, j % 2 * CAP:(j % 2 + 1) * CAP]
                        wh, wl = (v[:, bass.ds(e, 1), j * 128:(j + 1) * 128].rearrange("p a n -> p (a n)") for v in (e1h, e1l))
                        pe.matmul(o, wh, eXh[:, slot, :], start=True, stop=False)
                        pe.matmul(o, wh, eXl[:, slot, :], start=False, stop=False)
                        ins = pe.matmul(o, wl, eXh[:, slot, :], start=False, stop=True)
                        if j % 2:
                            ins.then_inc(eh_mm, 1)
                if not isinstance(k, int) or k < EXPERTS:
                    for h in range(2):
                        pe.wait_ge(gathered[q][h], 16 * ring_use(k, q))
                        ins = pe.transpose(T[q % 2][:, h * HC:(h + 1) * HC], gath[q][:, h, 0:C], ident[0:HC, 0:HC])
                    ins.then_inc(eX_mm, 1)
                if past(k, 2):
                    e, r2 = k - 2, q % 2
                    pe.wait_ge(eh_split, e + 2)
                    for h in range(2):
                        o = (T[2], X)[r2][0:HC, h * 128:(h + 1) * 128]
                        for j in range(KF):
                            sl = slice(j * CAP + h * HC, j * CAP + (h + 1) * HC)
                            wh, wl = (v[:, bass.ds(e, 1), j, :].rearrange("p a n -> p (a n)") for v in (e2h, e2l))
                            pe.matmul(o, ehh[:, r2, sl], wh, start=(j == 0), stop=False)
                            pe.matmul(o, ehl[:, r2, sl], wh, start=False, stop=False)
                            pe.matmul(o, ehh[:, r2, sl], wl, start=False, stop=False)
                        ins = pe.matmul(o, pickb[:, bass.ds(e, 1)].broadcast_to([128, HC]), b2hl[:], start=False, stop=True)
                    ins.then_inc(ey_mm, 1)

            pe.wait_ge(b2_split, 1)
            pe.wait_ge(ew_split, 2 * EXPERTS // EC)
            expert_steps(pe, step)

        @block.vector
        def _(dve):
            def split_x(g, m):
                dve.wait_ge(xT_copied, g * MS + m + 1)
                if past(g):
                    dve.wait_ge(hid_mm, g * KH)
                dve.tensor_copy(xh[:, m, :], xp32[:, m, :]).then_inc(xh_done, 1)
                dve.wait_ge(xh_done, g * MS + m + 1)
                dve.tensor_tensor(xl[:, m, :], xp32[:, m, :], xh[:, m, :], ALU.subtract).then_inc(xl_done, 1)

            for m in range(MS):
                split_x(0, m)
            for n in range(MS):
                cols = slice(n * W1_COLS, (n + 1) * W1_COLS)
                dve.wait_ge(w1_hi, n + 1)
                dve.scalar_tensor_tensor(w1l[:, :, cols], stage1[:, n], SCALE, w1h[:, :, cols], ALU.mult, ALU.subtract)\
                    .then_inc(w1_split, 1)

            def setup():
                n = [0]

                def step(ins):
                    n[0] += 1
                    ins.then_inc(setup_vec, 1)
                    dve.wait_ge(setup_vec, n[0])

                dve.wait_ge(setup_copy, 8)
                dve.wait_ge(setup_mm, 5)
                dve.wait_ge(small_loaded, 16 * NSMALL[0])
                dve.wait_ge(ones_done, ZEROED)
                low = slice(LO_ROW, LO_ROW + 1)
                step(dve.tensor_copy(vb16[0:1, :], vb_row[0:1, :]))
                step(dve.tensor_copy(vb_high[low, :], vb_row[low, :]))
                step(dve.tensor_tensor(vb16[low, :], vb_row[low, :], vb_high[low, :], ALU.subtract))
                for h in range(GB):
                    c = slice(h * CHUNK, (h + 1) * CHUNK)
                    step(dve.tensor_tensor(biasA[:, c], X[:, 0:CHUNK], mask[:, c], ALU.add))
                step(dve.tensor_tensor(wTl[:, 0:4, :], Q[0][:].rearrange("p (k n) -> p k n", k=4), wTh[:, 0:4, :], ALU.subtract))
                step(dve.tensor_tensor(wTl[:, 4:6, :], Q[1][:, 0:256].rearrange("p (k n) -> p k n", k=2), wTh[:, 4:6, :], ALU.subtract))
                step(dve.tensor_scalar(whalf[:, 0, :], vec[:, 0:V_U], 0.5, None, ALU.mult))
                step(dve.tensor_scalar(whalf[:, 1, :], vswap[:], 0.5, None, ALU.mult))
                step(dve.scalar_tensor_tensor(padv[:, 2:3], padv[:, 0:1], 1.0, col(V_BASE), ALU.add, ALU.mult))
                step(dve.scalar_tensor_tensor(padv[:, 3:4], padv[:, 1:2], 1.0, vswap[:, V_BASE:V_BASE + 1], ALU.add, ALU.mult))
                step(dve.scalar_tensor_tensor(vB[:, 0, :], vtB[:, 1, :], 1.0, vtB[:, 0, :], ALU.add, ALU.mult))
                step(dve.tensor_copy(vB[:, 1, :], vB[:, 0, :]))
                pad = slice(GT, TABLE)
                step(dve.tensor_scalar(padc[:, 0, :], cos[:, pad], padv[:, 2:3], None, ALU.mult))
                step(dve.tensor_scalar(padc[:, 1, :], sin[:, pad], padv[:, 3:4], None, ALU.mult))
                for i, (name, wc, bc) in enumerate(HEADS):
                    step(dve.tensor_scalar(ctab[:, i, :], cos, col(bc), None, ALU.mult))
                    step(dve.scalar_tensor_tensor(ctab[:, i, :], sin, vswap[:, bc:bc + 1], ctab[:, i, :], ALU.mult, ALU.add))
                    if name in ("lk", "qk"):
                        step(dve.scalar_tensor_tensor(padc[:, 2, :], padc[:, 0, :], whalf[:, 0, wc:wc + 1], ctab[:, i, pad],
                                                      ALU.mult, ALU.add))
                        step(dve.scalar_tensor_tensor(padc[:, 3, :], padc[:, 1, :], whalf[:, 1, wc:wc + 1], padc[:, 2, :],
                                                      ALU.mult, ALU.add))
                        for b in range(GB):
                            step(dve.tensor_copy(qT[name][:, b, TW:PADDED], padc[:, 3, :]))

            w2_now = [0]

            def tok(g, p):
                first = isinstance(g, int) and g == 0
                if first and p >= KH - MS and w2_now[0] < MS:
                    n = w2_now[0]
                    w2_now[0] += 1
                    dve.wait_ge(w2_hi, n + 1)
                    for k in (2 * n, 2 * n + 1):
                        ins = dve.scalar_tensor_tensor(w2l[:, k], stage2m[:, k], SCALE, w2h[:, k], ALU.mult, ALU.subtract)
                    ins.then_inc(w2_split, 1)
                if first and p == KH + 2:
                    setup()
                if p < KH:
                    dve.wait_ge(hid_hi, g * KH + p + 1)
                    dve.scalar_tensor_tensor(hidl[:, p, :], T[p % 3][:, 0:GT], 0.0, hidh[:, p, :], ALU.max, ALU.subtract)\
                        .then_inc(hid_lo, 1)
                    return
                if p - KH < MS and not (isinstance(g, int) and g == GROUPS - 1):
                    split_x(g + 1, p - KH)
                m, second = mix_step_of(p)
                if not second:
                    return
                base = g * MIX_STEPS + mix_after(m - 1)

                def done(ins):
                    return ins.then_inc(mix_step, 1)

                dve.wait_ge(mix_exp, g * MS + m + 1)
                if m == 0:
                    dve.wait_ge(xu_done, g + 1)
                    dve.tensor_copy(den[:], mexp[:, 0, :])
                    done(dve.tensor_tensor(num[:], mexp[:, 0, :], xu32[:, 0, :], ALU.mult))
                else:
                    dve.wait_ge(mix_step, base)
                    done(dve.tensor_tensor(prod[:], mexp[:, m % 2, :], xu32[:, m, :], ALU.mult))
                    done(dve.tensor_tensor(den[:], den[:], mexp[:, m % 2, :], ALU.add))
                    dve.wait_ge(mix_step, base + 1)
                    done(dve.tensor_tensor(num[:], num[:], prod[:], ALU.add))
                if m == MS - 1:
                    dve.wait_ge(mix_step, base + 3)
                    done(dve.reciprocal(den[:], den[:]))
                    dve.wait_ge(mix_step, base + 4)
                    dve.tensor_tensor(pooled[:], num[:], den[:], ALU.mult).then_inc(pooled_done, 1)

            LN_STEPS = 5
            ROT_STEPS = 5

            def stats(a_, src, n, signal):
                for k in range(TPG):
                    ins = dve.bn_stats(st6[:, k, :], src(k))
                ins.then_inc(ln_step, 1)
                dve.wait_ge(ln_step, a_ * LN_STEPS + (2, 4, 5)[n])
                dve.sem_inc(dve_passed, 1)
                for k in range(TPG):
                    ins = dve.bn_aggr(mv[:, n, k, :], st6[:, k, :])
                ins.then_inc(signal, 1)

            def bc(t):
                return t[:].unsqueeze(1).broadcast_to([TT, TPG, 128])

            def fin_rows(g, bank_):
                dve.wait_ge(sh2_mm, g + 1)
                dve.wait_ge(h2b_loaded, 16 * (g + 1))
                if past(g):
                    dve.wait_ge(out_stored, 16 * g)
                dve.tensor_tensor(fin, bank_[0:TT, 0:TPG * 128].rearrange("p (k n) -> p k n", k=TPG), h2b, ALU.add)\
                    .then_inc(fin_done, 1)

            def split_low(g, j):
                dve.wait_ge(sh_hi, g * KF + j + 1)
                dve.tensor_tensor(shl[:, j], sh32[:, j], shh[:, j], ALU.subtract).then_inc(sh_lo_dve, 1)

            def last(s):
                if s == 9:
                    split_low(0, 1)
                    split_low(0, 3)
                if s == 12:
                    fin_rows(0, Q[3])
                    split_low(1, 1)
                    split_low(1, 3)

            def attn(a_, s):
                if isinstance(a_, int) and a_ == GROUPS - 1:
                    last(s)
                if s == 0:
                    dve.wait_ge(fc_mm, a_ + 1)
                    dve.tensor_tensor(z[:], X[0:TT, 0:TPG * 128].rearrange("p (k n) -> p k n", k=TPG), bc(fcb_bc), ALU.add)\
                        .then_inc(ln_step, 1)
                    dve.wait_ge(ln_step, a_ * LN_STEPS + 1)
                    stats(a_, lambda k: z[:, k, :], 0, ln1_stats)
                    dve.wait_ge(ln1_stats, a_ + 1)
                    for k in range(TPG):
                        ins = dve.scalar_tensor_tensor(xn[:, k, :], z[:, k, :], mv[:, 0, k, 0:1], lng_bc[:], ALU.subtract, ALU.mult)
                    ins.then_inc(ln_step, 1)
                if s == 1:
                    dve.wait_ge(ln_step, a_ * LN_STEPS + 3)
                    dve.wait_ge(ln1_rstd, a_ + 1)
                    for k in range(TPG):
                        ins = dve.scalar_tensor_tensor(h1[:, k, :], xn[:, k, :], pst[:, 1, k:k + 1], lnb_bc[:], ALU.mult, ALU.add)
                    ins.then_inc(h1_done, 1)
                    dve.wait_ge(h1_done, a_ + 1)
                    stats(a_, lambda k: h1[:, k, :], 1, ln2_stats)
                if s == 2:
                    dve.wait_ge(ln2_stats, a_ + 1)
                    dve.wait_ge(ln2_r, a_ + 1)
                    for k in range(TPG):
                        ins = dve.tensor_scalar(xn[:, k, :], h1[:, k, :], mv[:, 1, k, 0:1], pst[:, 6, k:k + 1], ALU.subtract, ALU.mult)
                    ins.then_inc(xn_done, 1)
                if s == 3:
                    dve.wait_ge(xnT_copied, a_ + 1)
                    dve.tensor_tensor(xnl, Q[0][:, 0:GT], xnh, ALU.subtract).then_inc(xnT_low, 1)
                if s == 4:
                    for i in range(2):
                        dve.wait_ge(proj_z, a_ * 4 + i + 1)
                        ins = dve.scalar_tensor_tensor(base2[:, i, :], ptanh[:, i, :], 1.0, pz[:, i, :], ALU.add, ALU.mult)
                        ins.then_inc(base_done, 1)
                    dve.wait_ge(base_done, a_ * 2 + 2)
                    dve.tensor_tensor(rot[:, 0, :], base2[:, 0, :], cos[:, 0:GT], ALU.mult)
                    dve.tensor_tensor(rot[:, 1, :], base2[:, 1, :], sin[:, 0:GT], ALU.mult).then_inc(rot_step, 1)
                    dve.wait_ge(rot_step, a_ * ROT_STEPS + 1)
                    for i, (name, wc, _) in enumerate(HEADS):
                        dve.scalar_tensor_tensor(htmp[:, i % 2, :], rot[:, 0, :], whalf[:, 0, wc:wc + 1], ctab[:, i, 0:GT],
                                                 ALU.mult, ALU.add).then_inc(rot_step, 1)
                        dve.wait_ge(rot_step, a_ * ROT_STEPS + 2 + i)
                        dve.scalar_tensor_tensor(qT[name][:, :, 0:TW], rot[:, 1, :].rearrange("p (b n) -> p b n", b=GB),
                                                 whalf[:, 1, wc:wc + 1], htmp[:, i % 2, :].rearrange("p (b n) -> p b n", b=GB),
                                                 ALU.mult, ALU.add).then_inc(head_done, 1)
                if s == 5:
                    for i in range(2):
                        dve.wait_ge(proj_z, a_ * 4 + i + 3)
                        dve.scalar_tensor_tensor(u2[:, i, :], ptanh[:, i, :], 1.0, pz[:, 2 + i, :], ALU.add, ALU.mult)\
                            .then_inc(u_done, 1)
                if s == 6:
                    dve.wait_ge(v_tanh, a_ * 2 + 1)
                    dve.scalar_tensor_tensor(vA[:], vtA[:], 1.0, Q[1][:].rearrange("p (b n) -> p b n", b=GB), ALU.add, ALU.mult)\
                        .then_inc(v_done, 1)
                    dve.wait_ge(v_tanh, a_ * 2 + 2)
                    dve.scalar_tensor_tensor(vB[0:B_TOK], vtB[0:B_TOK], 1.0, Q[2][0:B_TOK, :].rearrange("p (b n) -> p b n", b=GB),
                                             ALU.add, ALU.mult).then_inc(v_done, 1)
                if s == 7:
                    dve.wait_ge(qk_mm, a_ + 1)
                    n = GB * A_TOK
                    dve.scalar_tensor_tensor(sA[:], Q[0][:, 0:n].rearrange("p (b n) -> p b n", b=GB), 1.0 / CHUNK,
                                             biasA[:].unsqueeze(1).broadcast_to([128, GB, A_TOK]), ALU.mult, ALU.add)
                    dve.scalar_tensor_tensor(sB[:], Q[0][0:CHUNK, n:n + GB * B_TOK].rearrange("p (b n) -> p b n", b=GB), 1.0 / CHUNK,
                                             biasA[0:CHUNK, 0:B_TOK].unsqueeze(1).broadcast_to([CHUNK, GB, B_TOK]),
                                             ALU.mult, ALU.add).then_inc(score_done, 1)
                    dve.wait_ge(score_done, a_ + 1)
                    dve.scalar_tensor_tensor(kA[:], sA[:], 0.0, sA[:], ALU.max, ALU.mult)
                    dve.scalar_tensor_tensor(kB[:], sB[:], 0.0, sB[:], ALU.max, ALU.mult).then_inc(kern_done, 1)
                if s == 9:
                    dve.wait_ge(ot_mm, a_ + 1)
                    dve.wait_ge(u_done, a_ * 2 + 2)
                    for i in range(2):
                        ins = dve.scalar_tensor_tensor(gT[:, i, :], Q[2 + i][:, 0:GT], 0.25, u2[:, i, :], ALU.mult, ALU.mult)
                    ins.then_inc(g_done, 1)
                if s == 10:
                    dve.wait_ge(out_mm, a_ + 1)
                    dve.wait_ge(h1ob_done, a_ + 1)
                    dve.tensor_tensor(h2[:], Q[0][0:TT, 0:TPG * 128].rearrange("p (k n) -> p k n", k=TPG), h1ob[:], ALU.add)\
                        .then_inc(h2_done, 1)
                    dve.wait_ge(h2_done, a_ + 1)
                    stats(a_, lambda k: h2[:, k, :], 2, ln3_stats)
                if s == 11:
                    dve.wait_ge(ln3_stats, a_ + 1)
                    dve.wait_ge(ln3_rstd, a_ + 1)
                    dve.wait_ge(rows_stored, 16 * (a_ + 1))
                    for k in range(TPG):
                        ins = dve.tensor_scalar(rows[:, k, 0:C], h2[:, k, :],
                                                mv[:, 2, k, 0:1], pst[:, 7, k:k + 1], ALU.subtract, ALU.mult)
                    ins.then_inc(n2_done, 1)
                if s == 12:
                    dve.wait_ge(n2T_copied, a_ + 1)
                    dve.tensor_copy(n2h[:, bass.ds(a_ * GT, GT)], n2T[:]).then_inc(n2h_done, 1)
                    dve.wait_ge(n2h_done, a_ + 1)
                    dve.tensor_tensor(n2l[:, bass.ds(a_ * GT, GT)], n2T[:], n2h[:, bass.ds(a_ * GT, GT)], ALU.subtract)\
                        .then_inc(n2_split, 1)
                if s == 13:
                    dve.wait_ge(gate_mm, a_ + 1)
                    q2 = Q[2][0:TT, 0:TPG * EXPERTS].rearrange("p (k n) -> p k n", k=TPG)

                    def over(t):
                        return t[:].unsqueeze(2).broadcast_to([TT, TPG, EXPERTS])

                    dve.tensor_reduce(lmax[:], q2, AX_X, ALU.max).then_inc(lmax_done, 1)
                    dve.wait_ge(lmax_done, a_ + 1)
                    dve.tensor_tensor(lg[:], q2, over(lmax), ALU.subtract).then_inc(lg_done, 1)
                    dve.wait_ge(lexp_done, a_ + 1)
                    dve.tensor_reduce(psum_[:], pexp[:], AX_X, ALU.add).then_inc(gsum_done, 1)
                    dve.wait_ge(gsum_done, a_ + 1)
                    dve.reciprocal(prcp[:], psum_[:]).then_inc(grcp_done, 1)
                    dve.wait_ge(grcp_done, a_ + 1)
                    dve.tensor_tensor(rows[:, :, C:ROW], pexp[:], over(prcp), ALU.mult)
                    dve.tensor_tensor(probs[:, bass.ds(a_ * TPG, TPG), :], pexp[:], over(prcp), ALU.mult)\
                        .then_inc(probs_done, 1)

            dve.sem_inc(rows_stored, 16)
            dve.sem_inc(h2_stored, 16)
            schedule(dve, tok, attn)

            dve.wait_ge(pm_mm, 1)
            dve.tensor_copy(pe_major, T[0][:, 0:GT]).then_inc(bits_done, 1)
            dve.memset(cand[:], UNITS[0] * 2 ** (DIGIT - 1)).then_inc(cand_ready, 1)
            dve.wait_ge(bits_done, 1)
            masked = [pe_bits] + [pe_masked[:, k] for k in range(PHASES - 1)]
            for k in range(PHASES):
                bits = (2 ** DIGIT - 1) << (DIGIT * (PHASES - 1 - k))
                dve.tensor_scalar(masked[k], pe_major.bitcast(U32), bits, None, ALU.bitwise_and).then_inc(bits_done, 1)
            for k in range(PHASES):
                dve.wait_ge(bits_done, 2 + k)
                dve.tensor_scalar(digits[:, k], masked[k], UNITS[k] / 2 ** (DIGIT * (PHASES - 1 - k)), None, ALU.mult)\
                    .then_inc(key_step, 1)
            deltas = rc[:, RCOLUMNS["bounds"]]
            dve.wait_ge(rc_ready, 1)
            rl = slice(LO_ROW, LO_ROW + EXPERTS)
            dve.tensor_tensor(b2hl[rl, :], b2st[rl, :], b2t[rl, :], ALU.subtract).then_inc(b2_split, 1)

            def search(i, key):
                g = i + EARLY
                for q in range(SPAN):
                    n = i * SPAN + q
                    dve.wait_ge(cand_ready, n + 1)
                    dve.tensor_scalar(hits, key, cand[:], None, ALU.is_ge, ALU.add, accum_out=cnt[:]).then_inc(hits_done, 1)
                    dve.tensor_tensor(bounds[:], cand[:].broadcast_to([128, 2]), deltas[:, bass.ds(2 * n, 2)], ALU.add)\
                        .then_inc(bounds_done, 1)
                    if q == 0 and past(i):
                        fin_rows(g - 1, X)
                    if q in (1, 2):
                        split_low(g, 2 * q - 1)
                    dve.wait_ge(bounds_done, n + 1)
                    dve.wait_ge(count_mm, n + 1)
                    dve.tensor_scalar(cand[:], T[1][:, 0:1], bounds[:, 0:1], bounds[:, 1:2], ALU.max, ALU.min)\
                        .then_inc(cand_ready, 1)

            def found_digit(k):
                dve.wait_ge(cand_ready, (k + 1) * DIGIT + 1)
                dve.tensor_copy(found[:, k:k + 1], cand[:]).then_inc(key_step, 1)

            fin_rows(EARLY - 1, Q[3])
            dve.wait_ge(key_step, PHASES)
            search(0, digits[:, 0])
            search(1, digits[:, 0])
            found_digit(0)
            dve.scalar_tensor_tensor(keys[:, 0], digits[:, 0], cand[:], digits[:, 1], ALU.subtract, ALU.add).then_inc(key_step, 1)
            dve.wait_ge(key_step, PHASES + 2)
            dve.memset(cand[:], UNITS[1] * 2 ** (DIGIT - 1)).then_inc(key_step, 1)
            dve.wait_ge(key_step, PHASES + 3)
            with dve.Fori(2, 4) as i:
                search(i, keys[:, 0])
            found_digit(1)
            rescaled = UNITS[2] * 2 ** DIGIT / UNITS[1]
            dve.tensor_scalar(shifted, keys[:, 0], cand[:], rescaled, ALU.subtract, ALU.mult).then_inc(key_step, 1)
            dve.wait_ge(key_step, PHASES + 5)
            dve.tensor_tensor(keys[:, 1], shifted, digits[:, 2], ALU.add).then_inc(key_step, 1)
            dve.memset(cand[:], UNITS[2] * 2 ** (DIGIT - 1)).then_inc(key_step, 1)
            dve.wait_ge(key_step, PHASES + 7)
            with dve.Fori(4, 6) as i:
                search(i, keys[:, 1])
            dve.wait_ge(cand_ready, PHASES * DIGIT + 1)
            scale = 2.0 ** (DIGIT * 2) / UNITS[0]
            dve.tensor_scalar(thr_bits[:, 0:1], found[:, 0:1], found[:, 1:2], scale, ALU.add, ALU.mult)
            dve.tensor_scalar(thr_bits[:, 1:2], cand[:], 1 / UNITS[2], None, ALU.mult).then_inc(key_step, 1)
            dve.wait_ge(key_step, PHASES + 8)
            dve.tensor_tensor(thr_wide.bitcast(U32), thr_bits[:, 0:1].broadcast_to([128, TT]), thr_bits[:, 1:2].broadcast_to([128, TT]),
                              ALU.bitwise_or).then_inc(thr_wide_done, 1)
            dve.wait_ge(thr_mm, 1)
            dve.tensor_copy(thr, T[2][0:TT, 0:EXPERTS]).then_inc(thr_done, 1)
            dve.wait_ge(thr_done, 1)
            wide = thr.unsqueeze(2).broadcast_to([TT, EXPERTS, TILES])
            by_e = probs[:].rearrange("p k e -> p e k")
            dve.tensor_tensor(over16, by_e, wide, ALU.is_gt)
            dve.tensor_tensor(tie16, by_e, wide, ALU.is_equal).then_inc(masks_done, 1)
            dve.wait_ge(masks_done, 1)
            fresh = rc[0:TT, RCOLUMNS["not_first"]]
            for src, dst in ((over16, over_c), (tie16, tie_c)):
                dve.tensor_tensor_scan(flat(dst), fresh, flat(src), 0.0, ALU.mult, ALU.add).then_inc(scans_done, 1)
            FAR = 1024.0
            dve.wait_ge(prefix_mm, 1)
            dve.scalar_tensor_tensor(flat(pos1), T[0][0:TT, 0:ET], FAR, flat(over16), ALU.subtract, ALU.mult)
            dve.scalar_tensor_tensor(flat(pos2), T[1][0:TT, 0:ET], FAR, flat(tie16), ALU.subtract, ALU.mult).then_inc(pos_done, 1)
            dve.wait_ge(pos_done, 1)
            dve.scalar_tensor_tensor(flat(pos_i), flat(pos1), FAR, flat(pos2), ALU.add, ALU.add).then_inc(pos_done, 1)
            dve.wait_ge(pos_done, 2)
            dve.tensor_scalar(flat(dig_ai), flat(pos_i), 0xFFF - (DIG_B - 1), None, ALU.bitwise_and)
            dve.tensor_scalar(flat(dig_bi), flat(pos_i), DIG_B - 1, None, ALU.bitwise_and).then_inc(digits_done, 1)
            dve.wait_ge(digits_done, 1)
            dve.tensor_copy(flat(dig_a), flat(dig_ai)).then_inc(digits_done, 1)
            dve.wait_ge(digits_done, 2)
            for k in range(DIG_A):
                ins = dve.tensor_scalar(hotA[:, :, k], dig_a, float(k * DIG_B), None, ALU.is_equal)
            ins.then_inc(hotA_done, 1)
            dve.wait_ge(dig_b_done, 1)
            for h in range(2):
                e = slice(h * HALF_E, (h + 1) * HALF_E)
                for k in range(DIG_B):
                    ins = dve.tensor_scalar(hotB[:, k, e], dig_b[:, e], float(k), None, ALU.is_equal)
                ins.then_inc(hotB_done, 1)
            dve.wait_ge(hotA_done, 1)
            for t in range(ACT_TILES, TILES):
                dve.tensor_scalar(hotA[:, :, :, t], hotA[:, :, :, t], numbers[:, t:t + 1], None, ALU.mult).then_inc(numbered_dve, 1)
            fin_rows(GROUPS - 1, X)
            na = DIG_A * HALF_E
            for h in range(2):
                dve.wait_ge(lists_mm, h + 1)
                ins = dve.tensor_tensor(picked[:, h, :], Q[h][0:na, 0:DIG_B * HALF_E], rc[0:na, RCOLUMNS["diagonal"]], ALU.mult)
            ins.then_inc(picked_done, 1)
            dve.wait_ge(picked_done, 1)
            dve.tensor_reduce(lists_f, picked.rearrange("p h (b e) -> p h b e", b=DIG_B), AX_X, ALU.add).then_inc(lists_done, 1)
            dve.wait_ge(idx_mm, 1)
            dve.tensor_scalar(idx[:], T[2][0:HC, 0:2 * EXPERTS], TOKENS // 2, None, ALU.add).then_inc(idx_done, 1)
            dve.wait_ge(idx_done, 1)

            def indices(tile_, e):
                return dve.tensor_copy(tile_[:].rearrange("p (h a) -> p h a", h=2),
                                       idx[:].rearrange("p (h e) -> p h e", h=2)[:, :, bass.ds(e, 1)])

            def copy_gather(e, q):
                indices(gidx[q], e).then_inc(gidx_copied, 1)

            dve.sem_inc(eh_split, 1)
            for e in range(LEAD):
                copy_gather(e, e)

            def step(k, q):
                if not isinstance(k, int) or k + LEAD < EXPERTS:
                    copy_gather(k + LEAD, (q + LEAD) % RING)
                if not isinstance(k, int) or k < EXPERTS:
                    if past(k, RING):
                        dve.wait_ge(added, k - RING + 2)
                        dve.sem_inc(dve_passed, 1)
                    indices(sidx[q], k)
                    dve.wait_ge(eX_mm, k + 1)
                    src = T[q % 2][:, 0:CAP]
                    dve.tensor_copy(eXh[:, q, :], src).then_inc(eX_hi, 1)
                    dve.tensor_copy(score[:, q, :].unsqueeze(2), gath[q][:, :, bass.ds(C + k, 1)])
                    dve.wait_ge(eX_hi, k + 1)
                    dve.tensor_tensor(eXl[:, q, :], src, eXh[:, q, :], ALU.subtract).then_inc(eX_split, 1)
                if not isinstance(k, int) or 1 <= k <= EXPERTS:
                    e, r2 = k - 1, (q + 1) % 2
                    dve.wait_ge(eh_gelu, e + 1)
                    dve.tensor_copy(ehh[:, r2, :], eh32[:, r2, :]).then_inc(eh_hi, 1)
                    dve.wait_ge(eh_hi, e + 1)
                    dve.tensor_tensor(ehl[:, r2, :], eh32[:, r2, :], ehh[:, r2, :], ALU.subtract).then_inc(eh_split, 1)
                if past(k, 2):
                    e, r2, slot = k - 2, q % 2, (q + 2) % RING
                    dve.wait_ge(ey_mm, e + 1)
                    for h in range(2):
                        ins = dve.tensor_scalar(ey[slot][:, h, :], (T[2], X)[r2][0:HC, h * 128:(h + 1) * 128],
                                                score[:, slot, h:h + 1], None, ALU.mult)
                    ins.then_inc(ey_scaled, 1)

            expert_steps(dve, step)


_IN = ["x", "L0_tok_w1", "L0_tok_w2", "L0_tok_fc_w", "L0_tok_fc_b", "L0_tok_ln_g", "L0_tok_ln_b", "L0_attn_scala",
       "L0_attn_u_w", "L0_attn_u_b", "L0_attn_v_w", "L0_attn_v_b", "L0_attn_base_w", "L0_attn_base_b", "L0_attn_qq_w",
       "L0_attn_qq_b", "L0_attn_qk_w", "L0_attn_qk_b", "L0_attn_lq_w", "L0_attn_lq_b", "L0_attn_lk_w", "L0_attn_lk_b",
       "L0_attn_o_w", "L0_attn_o_b", "L0_attn_w", "L0_ffn_gate_w", "L0_ffn_w1", "L0_ffn_b1", "L0_ffn_w2", "L0_ffn_b2",
       "L0_ffn_sw1", "L0_ffn_sb1", "L0_ffn_sw2", "L0_ffn_sb2"]


def kernel(**inputs):
    import concourse.bacc as bacc
    from concourse.bass_utils import run_bass_kernel_spmd

    nc = bacc.Bacc("TRN2", target_bir_lowering=False, num_devices=1)
    arrays = {n: np.ascontiguousarray(inputs[n]) for n in _IN}
    arrays["constants"] = constant_table()
    arrays["routing"] = routing_table()
    aps = {n: nc.dram_tensor(f"in_{n}", v.shape, mybir.dt.from_np(v.dtype), kind="ExternalInput").ap() for n, v in arrays.items()}
    out = nc.dram_tensor("out_h", (TOKENS, C), F32, kind="ExternalOutput").ap()
    build(nc, aps, out)
    r = run_bass_kernel_spmd(nc, [{f"in_{n}": v for n, v in arrays.items()}], core_ids=[0])
    return r.results[0]["out_h"].reshape(BATCH, TW, C)
```
